# Optimizing a Trainium2 kernel written in Bass

```python
import numpy as np
import jax
import jax.numpy as jnp

def _softmax(x, axis=-1):
    return jax.nn.softmax(x, axis=axis)

def _gelu(x):
    return jax.nn.gelu(x, approximate=True)

def _silu(x):
    return jax.nn.silu(x)

def _sigmoid(x):
    return jax.nn.sigmoid(x)

def _layernorm(x, axis=-1, eps=1e-05):
    m = jnp.mean(x, axis=axis, keepdims=True)
    v = jnp.var(x, axis=axis, keepdims=True)
    return (x - m) / jnp.sqrt(v + eps)

def _scatter_add(tgt, idx, src, axis=0):
    return tgt.at[idx].add(src)

def _segment_sum(src, seg, n):
    return jax.ops.segment_sum(src, seg, n)
kernel_name = 'mk_xattn_ffn_d4_seqx_r8_4e3e4b'

def setup_inputs(seed: int=0):
    np.random.seed(seed)
    _w = jnp.asarray

    def _rec_inputs():
        import jax
        import jax.numpy as jnp
        _rk = jax.random.key(seed)
        x = 0.0002417 + 0.9998 * jax.random.normal(jax.random.fold_in(_rk, 1), (8, 128, 128), jnp.float32)
        _lenS = 128 - jax.random.randint(jax.random.fold_in(_rk, 7), (8,), 0, max(1, 128 // 4) + 1, jnp.int32)
        _lenS2 = 120 - jax.random.randint(jax.random.fold_in(_rk, 8), (8,), 0, max(1, 120 // 4) + 1, jnp.int32)
        _ctx_1024P = jax.random.normal(jax.random.fold_in(_rk, 11), (8, 16, 128), jnp.float32)
        _ctx_1024c = jax.random.dirichlet(jax.random.fold_in(_rk, 511), 0.3 * jnp.ones((16,), jnp.float32), (8, 120))
        _ctx_1024t = jnp.einsum('bsk,bkd->bsd', _ctx_1024c, _ctx_1024P)
        _ctx_1024t = _ctx_1024t * jax.lax.rsqrt(jnp.mean(jnp.square(_ctx_1024t)) + 1e-12) * 0.953939
        ctx_1024 = 7.22013e-05 + 1.00017 * (_ctx_1024t + 0.3 * jax.random.normal(jax.random.fold_in(_rk, 611), (8, 120, 128), jnp.float32))
        fside_1x1xSxS2_0 = 0.000675642 + 1.00031 * jax.random.normal(jax.random.fold_in(_rk, 15), (1, 1, 128, 120), jnp.float32)
        _validS = jnp.arange(128)[None, :] < _lenS[:, None]
        _validS2 = jnp.arange(120)[None, :] < _lenS2[:, None]
        _causal = jnp.tril(jnp.ones((128, 128), dtype=bool))
        mask_BxS2_if1 = jnp.where(jnp.ones((8, 120), dtype=bool), 1, 0).astype(jnp.int32)
        mask_BxS2_ik0 = jnp.where(jnp.broadcast_to(_validS2[:, :], (8, 120)), 0, 1).astype(jnp.int32)
        mask_BxSxS2_bk0 = jnp.logical_not(jnp.broadcast_to(_validS2[:, None, :], (8, 128, 120)))
        return (x, ctx_1024, fside_1x1xSxS2_0, mask_BxS2_if1, mask_BxS2_ik0, mask_BxSxS2_bk0)
    x, ctx_1024, fside_1x1xSxS2_0, mask_BxS2_if1, mask_BxS2_ik0, mask_BxSxS2_bk0 = _rec_inputs()

    def _L0_xattn_setup():
        import jax, jax.numpy as jnp
        import numpy as np
        D_MODEL = 128
        B, S = (4, 256)
        key = jax.random.key(seed)
        ks = jax.random.split(key, 10)
        s = 1.0 / np.sqrt(D_MODEL)
        return {'k': jax.random.normal(ks[0], (B, S, D_MODEL), jnp.float32), 'v': jax.random.normal(ks[1], (B, S, D_MODEL), jnp.float32), 'q': jax.random.normal(ks[2], (B, S, D_MODEL), jnp.float32), 'Wk': jax.random.normal(ks[3], (D_MODEL, D_MODEL), jnp.float32) * s, 'Wv': jax.random.normal(ks[4], (D_MODEL, D_MODEL), jnp.float32) * s, 'bv': jnp.zeros((D_MODEL,), jnp.float32), 'Wq': jax.random.normal(ks[5], (D_MODEL, D_MODEL), jnp.float32) * s, 'bq': jnp.zeros((D_MODEL,), jnp.float32), 'Wo': jax.random.normal(ks[6], (D_MODEL, D_MODEL), jnp.float32) * s, 'bo': jnp.zeros((D_MODEL,), jnp.float32)}
    _L0_xattn_all = _L0_xattn_setup()
    _L0_xattn_in = {k: v for k, v in _L0_xattn_all.items() if k in ('Wk', 'Wv', 'bv', 'Wq', 'bq', 'Wo', 'bo')}
    del _L0_xattn_all

    def _L0_ffn_setup():
        import jax, jax.numpy as jnp
        import numpy as np
        B, S, D = (2, 256, 128)
        H, E, P, K = (8, 8, 128, 2)
        SCALE = 1.0 / np.sqrt(P)

        def _get_sel_gate(x, w, route_scale):
            logits = jnp.einsum('bsd,ed->bse', x, w).astype(jnp.float32)
            raw = logits.reshape(x.shape[0], x.shape[1], H, E)
            probs = jax.nn.sigmoid(raw)
            vals, idx = jax.lax.top_k(probs, K)
            vals = vals / jnp.clip(vals.sum(-1, keepdims=True), 1e-09)
            vals = vals * route_scale
            gate = (jax.nn.one_hot(idx, E, dtype=vals.dtype) * vals[..., None]).sum(-2)
            return gate
        key = jax.random.key(seed)
        ks = jax.random.split(key, 8)
        std = 1.0 / np.sqrt(D)
        return {'x': jax.random.normal(ks[0], (B, S, D), jnp.float32), 'q_w': jax.random.normal(ks[1], (H * P, D), jnp.float32) * std, 'k_w': jax.random.normal(ks[2], (H * P, D), jnp.float32) * std, 'v_w': jax.random.normal(ks[3], (H * E, D, P), jnp.float32) * std, 'o_w': jax.random.normal(ks[4], (H * E, P, D), jnp.float32) * (1.0 / np.sqrt(H * P)), 'sel_v_w': jax.random.normal(ks[5], (H * E, D), jnp.float32) * std, 'sel_o_w': jax.random.normal(ks[6], (H * E, D), jnp.float32) * std, 'route_scale': jnp.ones((1,), jnp.float32)}
    _L0_ffn_all = _L0_ffn_setup()
    _L0_ffn_in = {k: v for k, v in _L0_ffn_all.items() if k in ('q_w', 'k_w', 'v_w', 'o_w', 'sel_v_w', 'sel_o_w', 'route_scale')}
    del _L0_ffn_all

    def _L1_xattn_setup():
        import jax, jax.numpy as jnp
        import numpy as np
        import math
        D_MODEL = 128
        N_HEADS = 16
        D_K = D_MODEL // N_HEADS
        B, S = (2, 256)
        key = jax.random.key(seed)
        ks = jax.random.split(key, 12)
        inp = {'in_Q': jax.random.normal(ks[0], (B, S, D_MODEL), dtype=jnp.float32), 'in_K': jax.random.normal(ks[1], (B, S, D_MODEL), dtype=jnp.float32), 'in_V': jax.random.normal(ks[2], (B, S, D_MODEL), dtype=jnp.float32), 'Q_pad_mask': jnp.ones((B, S), dtype=jnp.int32), 'K_pad_mask': jax.random.randint(ks[3], (B, S), 0, 2, dtype=jnp.int32)}
        scale = 1.0 / math.sqrt(D_MODEL)
        for i, name in enumerate(['Q', 'K', 'V', 'O']):
            inp[f'W_{name}'] = jax.random.normal(ks[4 + i], (D_MODEL, D_MODEL), dtype=jnp.float32) * scale
            inp[f'b_{name}'] = jnp.zeros((D_MODEL,), dtype=jnp.float32)
        return inp
    _L1_xattn_all = _L1_xattn_setup()
    _L1_xattn_in = {k: v for k, v in _L1_xattn_all.items() if k in ('W_Q', 'b_Q', 'W_K', 'b_K', 'W_V', 'b_V', 'W_O', 'b_O')}
    del _L1_xattn_all

    def _L1_ffn_setup():
        import jax, jax.numpy as jnp
        import numpy as np
        EPS = 1e-06
        LN_EPS = 1e-05

        def _absmean_core(W):
            gamma = jnp.mean(jnp.abs(W)) + EPS
            Ws = W / gamma
            Wq = jnp.sign(Ws) * jnp.minimum(jnp.round(jnp.abs(Ws)), 1.0)
            return (Wq, gamma)

        @jax.custom_vjp
        def absmean(W):
            return _absmean_core(W)[0]

        def _absmean_fwd(W):
            Wq, gamma = _absmean_core(W)
            return (Wq, gamma)

        def _absmean_bwd(gamma, g):
            return (g / gamma,)
        absmean.defvjp(_absmean_fwd, _absmean_bwd)

        def layernorm(x, w, b, eps=LN_EPS):
            mu = jnp.mean(x, axis=-1, keepdims=True)
            var = jnp.mean((x - mu) ** 2, axis=-1, keepdims=True)
            return (x - mu) * jax.lax.rsqrt(var + eps) * w + b
        key = jax.random.key(seed)
        k1, k2, k3 = jax.random.split(key, 3)
        d, h = (128, 512)
        B, T = (8, 256)
        return {'x': jax.random.normal(k1, (B, T, d), jnp.float32), 'W_fc': jax.random.normal(k2, (h, d), jnp.float32), 'ln_w': jnp.ones((h,), jnp.float32), 'ln_b': jnp.zeros((h,), jnp.float32), 'W_proj': jax.random.normal(k3, (d, h), jnp.float32)}
    _L1_ffn_all = _L1_ffn_setup()
    _L1_ffn_in = {k: v for k, v in _L1_ffn_all.items() if k in ('W_fc', 'ln_w', 'ln_b', 'W_proj')}
    del _L1_ffn_all

    def _L2_xattn_setup():
        import jax, jax.numpy as jnp
        import numpy as np
        DIM = 128
        HEAD_DIM = 64
        NUM_HEADS = DIM // HEAD_DIM
        EPS = 1e-06
        SCALE = HEAD_DIM ** (-0.5)

        def _per_head_ln(t, w):
            mu = jnp.mean(t, axis=-1, keepdims=True)
            var = jnp.mean(jnp.square(t - mu), axis=-1, keepdims=True)
            t = (t - mu) * jax.lax.rsqrt(var + EPS)
            return t * w[None, :, None, :]
        key = jax.random.key(seed)
        ks = jax.random.split(key, 8)
        B, N, M = (2, 128, 256)
        x = jax.random.normal(ks[0], (B, N, DIM), dtype=jnp.float32)
        context = jax.random.normal(ks[1], (B, M, DIM), dtype=jnp.float32)
        mask = jax.random.randint(ks[2], (B, N, M), 0, 2).astype(jnp.bool_)
        Wq = jax.random.normal(ks[3], (DIM, DIM), dtype=jnp.float32) * 0.02
        Wkv = jax.random.normal(ks[4], (DIM, 2 * DIM), dtype=jnp.float32) * 0.02
        Wo = jax.random.normal(ks[5], (DIM, DIM), dtype=jnp.float32) * 0.02
        qn_w = jnp.ones((NUM_HEADS, HEAD_DIM), dtype=jnp.float32)
        kn_w = jnp.ones((NUM_HEADS, HEAD_DIM), dtype=jnp.float32)
        return {'x': x, 'context': context, 'mask': mask, 'Wq': Wq, 'Wkv': Wkv, 'Wo': Wo, 'qn_w': qn_w, 'kn_w': kn_w}
    _L2_xattn_all = _L2_xattn_setup()
    _L2_xattn_in = {k: v for k, v in _L2_xattn_all.items() if k in ('Wq', 'Wkv', 'Wo', 'qn_w', 'kn_w')}
    del _L2_xattn_all

    def _L2_ffn_setup():
        import jax, jax.numpy as jnp
        import numpy as np
        B, S, H = (4, 256, 128)
        E, I, K = (8, 256, 2)
        key = jax.random.key(seed)
        ks = jax.random.split(key, 6)
        return {'hidden_states': jax.random.normal(ks[0], (B, S, H), dtype=jnp.float32), 'Wg': jax.random.normal(ks[1], (H, E), dtype=jnp.float32) * 0.02, 'W1': jax.random.normal(ks[2], (E, H, I), dtype=jnp.float32) * 0.02, 'b1': jnp.zeros((E, I), dtype=jnp.float32), 'W2': jax.random.normal(ks[3], (E, I, H), dtype=jnp.float32) * 0.02, 'b2': jnp.zeros((E, H), dtype=jnp.float32)}
    _L2_ffn_all = _L2_ffn_setup()
    _L2_ffn_in = {k: v for k, v in _L2_ffn_all.items() if k in ('Wg', 'W1', 'b1', 'W2', 'b2')}
    del _L2_ffn_all

    def _L3_xattn_setup():
        import jax, jax.numpy as jnp
        import numpy as np
        D_MODEL = 128
        N_HEAD = 16
        D_KEY = 64
        D_VALUE = 64

        def _split_heads(x, n_head, d_head):
            B, S, _ = x.shape
            return x.reshape(B, S, n_head, d_head).transpose(0, 2, 1, 3)
        key = jax.random.key(seed)
        ks = jax.random.split(key, 8)
        B, S = (2, 256)
        queries = jax.random.normal(ks[0], (B, S, D_MODEL), dtype=jnp.float32)
        keys = jax.random.normal(ks[1], (B, S, D_MODEL), dtype=jnp.float32)
        values = jax.random.normal(ks[2], (B, S, D_MODEL), dtype=jnp.float32)
        attn_bias = jax.random.normal(ks[3], (1, 1, S, S), dtype=jnp.float32)
        s = 1.0 / np.sqrt(D_MODEL)
        Wq = jax.random.normal(ks[4], (N_HEAD * D_KEY, D_MODEL), dtype=jnp.float32) * s
        Wk = jax.random.normal(ks[5], (N_HEAD * D_KEY, D_MODEL), dtype=jnp.float32) * s
        Wv = jax.random.normal(ks[6], (N_HEAD * D_VALUE, D_MODEL), dtype=jnp.float32) * s
        Wp = jax.random.normal(ks[7], (D_MODEL, N_HEAD * D_VALUE), dtype=jnp.float32) * s
        return {'queries': queries, 'keys': keys, 'values': values, 'attn_bias': attn_bias, 'Wq': Wq, 'Wk': Wk, 'Wv': Wv, 'Wp': Wp}
    _L3_xattn_all = _L3_xattn_setup()
    _L3_xattn_in = {k: v for k, v in _L3_xattn_all.items() if k in ('Wq', 'Wk', 'Wv', 'Wp')}
    del _L3_xattn_all

    def _L3_ffn_setup():
        import jax, jax.numpy as jnp
        import numpy as np
        DIM = 128
        LATENT = 64
        INTER = 64
        SHARED = 512
        E = 8
        TOPK = 2
        NGROUP = 2
        TOPKG = 1
        NORM_TOPK = True
        SCALE = 1.0
        B, S = (2, 128)

        def relu2(x):
            r = jnp.maximum(x, 0.0)
            return r * r
        key = jax.random.key(seed)
        ks = jax.random.split(key, 8)

        def w(k, shape, std=0.02):
            return jax.random.normal(k, shape, dtype=jnp.float32) * std
        return {'x': jax.random.normal(ks[0], (B, S, DIM), dtype=jnp.float32), 'gate': w(ks[1], (E, DIM)), 'corr_bias': jnp.zeros((E,), jnp.float32), 'w1': w(ks[2], (E, INTER, LATENT)), 'w2': w(ks[3], (E, LATENT, INTER)), 'fc1_w': w(ks[4], (LATENT, DIM)), 'fc2_w': w(ks[5], (DIM, LATENT)), 'up_w': w(ks[6], (SHARED, DIM)), 'down_w': w(ks[7], (DIM, SHARED))}
    _L3_ffn_all = _L3_ffn_setup()
    _L3_ffn_in = {k: v for k, v in _L3_ffn_all.items() if k in ('gate', 'corr_bias', 'w1', 'w2', 'fc1_w', 'fc2_w', 'up_w', 'down_w')}
    del _L3_ffn_all
    return {'x': x, 'ctx_1024': ctx_1024, 'fside_1x1xSxS2_0': fside_1x1xSxS2_0, 'mask_BxS2_if1': mask_BxS2_if1, 'mask_BxS2_ik0': mask_BxS2_ik0, 'mask_BxSxS2_bk0': mask_BxSxS2_bk0, 'L0_xattn_Wk': _L0_xattn_in['Wk'], 'L0_xattn_Wv': _L0_xattn_in['Wv'], 'L0_xattn_bv': _L0_xattn_in['bv'], 'L0_xattn_Wq': _L0_xattn_in['Wq'], 'L0_xattn_bq': _L0_xattn_in['bq'], 'L0_xattn_Wo': _L0_xattn_in['Wo'], 'L0_xattn_bo': _L0_xattn_in['bo'], 'L0_ffn_q_w': _L0_ffn_in['q_w'], 'L0_ffn_k_w': _L0_ffn_in['k_w'], 'L0_ffn_v_w': _L0_ffn_in['v_w'], 'L0_ffn_o_w': _L0_ffn_in['o_w'], 'L0_ffn_sel_v_w': _L0_ffn_in['sel_v_w'], 'L0_ffn_sel_o_w': _L0_ffn_in['sel_o_w'], 'L0_ffn_route_scale': _L0_ffn_in['route_scale'], 'L1_xattn_W_Q': _L1_xattn_in['W_Q'], 'L1_xattn_b_Q': _L1_xattn_in['b_Q'], 'L1_xattn_W_K': _L1_xattn_in['W_K'], 'L1_xattn_b_K': _L1_xattn_in['b_K'], 'L1_xattn_W_V': _L1_xattn_in['W_V'], 'L1_xattn_b_V': _L1_xattn_in['b_V'], 'L1_xattn_W_O': _L1_xattn_in['W_O'], 'L1_xattn_b_O': _L1_xattn_in['b_O'], 'L1_ffn_W_fc': _L1_ffn_in['W_fc'], 'L1_ffn_ln_w': _L1_ffn_in['ln_w'], 'L1_ffn_ln_b': _L1_ffn_in['ln_b'], 'L1_ffn_W_proj': _L1_ffn_in['W_proj'], 'L2_xattn_Wq': _L2_xattn_in['Wq'], 'L2_xattn_Wkv': _L2_xattn_in['Wkv'], 'L2_xattn_Wo': _L2_xattn_in['Wo'], 'L2_xattn_qn_w': _L2_xattn_in['qn_w'], 'L2_xattn_kn_w': _L2_xattn_in['kn_w'], 'L2_ffn_Wg': _L2_ffn_in['Wg'], 'L2_ffn_W1': _L2_ffn_in['W1'], 'L2_ffn_b1': _L2_ffn_in['b1'], 'L2_ffn_W2': _L2_ffn_in['W2'], 'L2_ffn_b2': _L2_ffn_in['b2'], 'L3_xattn_Wq': _L3_xattn_in['Wq'], 'L3_xattn_Wk': _L3_xattn_in['Wk'], 'L3_xattn_Wv': _L3_xattn_in['Wv'], 'L3_xattn_Wp': _L3_xattn_in['Wp'], 'L3_ffn_gate': _L3_ffn_in['gate'], 'L3_ffn_corr_bias': _L3_ffn_in['corr_bias'], 'L3_ffn_w1': _L3_ffn_in['w1'], 'L3_ffn_w2': _L3_ffn_in['w2'], 'L3_ffn_fc1_w': _L3_ffn_in['fc1_w'], 'L3_ffn_fc2_w': _L3_ffn_in['fc2_w'], 'L3_ffn_up_w': _L3_ffn_in['up_w'], 'L3_ffn_down_w': _L3_ffn_in['down_w']}

def reference(x, ctx_1024, fside_1x1xSxS2_0, mask_BxS2_if1, mask_BxS2_ik0, mask_BxSxS2_bk0, L0_xattn_Wk, L0_xattn_Wv, L0_xattn_bv, L0_xattn_Wq, L0_xattn_bq, L0_xattn_Wo, L0_xattn_bo, L0_ffn_q_w, L0_ffn_k_w, L0_ffn_v_w, L0_ffn_o_w, L0_ffn_sel_v_w, L0_ffn_sel_o_w, L0_ffn_route_scale, L1_xattn_W_Q, L1_xattn_b_Q, L1_xattn_W_K, L1_xattn_b_K, L1_xattn_W_V, L1_xattn_b_V, L1_xattn_W_O, L1_xattn_b_O, L1_ffn_W_fc, L1_ffn_ln_w, L1_ffn_ln_b, L1_ffn_W_proj, L2_xattn_Wq, L2_xattn_Wkv, L2_xattn_Wo, L2_xattn_qn_w, L2_xattn_kn_w, L2_ffn_Wg, L2_ffn_W1, L2_ffn_b1, L2_ffn_W2, L2_ffn_b2, L3_xattn_Wq, L3_xattn_Wk, L3_xattn_Wv, L3_xattn_Wp, L3_ffn_gate, L3_ffn_corr_bias, L3_ffn_w1, L3_ffn_w2, L3_ffn_fc1_w, L3_ffn_fc2_w, L3_ffn_up_w, L3_ffn_down_w):
    import jax
    import jax.numpy as jnp

    def _L0_xattn_ref(k, v, q, Wk, Wv, bv, Wq, bq, Wo, bo):
        import jax, jax.numpy as jnp
        import numpy as np
        D_MODEL = 128
        B, S = (4, 256)
        kp = jnp.einsum('bsd,ed->bse', k, Wk)
        vp = jnp.einsum('bsd,ed->bse', v, Wv) + bv
        qp = jnp.einsum('bsd,ed->bse', q, Wq) + bq
        scale = 1.0 / jnp.sqrt(jnp.float32(kp.shape[-1]))
        scores = jnp.einsum('bqd,bkd->bqk', qp, kp) * scale
        probs = jax.nn.softmax(scores, axis=-1)
        ctx = jnp.einsum('bqk,bkd->bqd', probs, vp)
        return jnp.einsum('bqd,ed->bqe', ctx, Wo) + bo

    def _L0_ffn_ref(x, q_w, k_w, v_w, o_w, sel_v_w, sel_o_w, route_scale):
        import jax, jax.numpy as jnp
        import numpy as np
        B, S, D = (2, 256, 128)
        H, E, P, K = (8, 8, 128, 2)
        SCALE = 1.0 / np.sqrt(P)

        def _get_sel_gate(x, w, route_scale):
            logits = jnp.einsum('bsd,ed->bse', x, w).astype(jnp.float32)
            raw = logits.reshape(x.shape[0], x.shape[1], H, E)
            probs = jax.nn.sigmoid(raw)
            vals, idx = jax.lax.top_k(probs, K)
            vals = vals / jnp.clip(vals.sum(-1, keepdims=True), 1e-09)
            vals = vals * route_scale
            gate = (jax.nn.one_hot(idx, E, dtype=vals.dtype) * vals[..., None]).sum(-2)
            return gate
        rs = route_scale[0]
        gate_v = _get_sel_gate(x, sel_v_w, rs)
        gate_o = _get_sel_gate(x, sel_o_w, rs)
        q = jnp.einsum('bsd,hpd->bhsp', x, q_w.reshape(H, P, D))
        k = jnp.einsum('bsd,hpd->bhsp', x, k_w.reshape(H, P, D))
        xv = jnp.einsum('bsd,hedp->bshep', x, v_w.reshape(H, E, D, P))
        v = jnp.einsum('bshep,bshe->bhsp', xv, gate_v)
        att = jax.nn.softmax(jnp.einsum('bhqp,bhkp->bhqk', q, k) * SCALE, axis=-1)
        ctx = jnp.einsum('bhqk,bhkp->bqhp', att, v)
        weighted = ctx[:, :, :, None, :] * gate_o[..., None]
        out = jnp.einsum('bshep,hepd->bsd', weighted, o_w.reshape(H, E, P, D))
        return out

    def _L1_xattn_ref(in_Q, in_K, in_V, Q_pad_mask, K_pad_mask, W_Q, b_Q, W_K, b_K, W_V, b_V, W_O, b_O):
        import jax, jax.numpy as jnp
        import numpy as np
        import math
        D_MODEL = 128
        N_HEADS = 16
        D_K = D_MODEL // N_HEADS
        B, S = (2, 256)
        b, sq, _ = in_Q.shape
        sk = in_K.shape[1]
        neg_inf = jnp.float32(-jnp.inf)
        Q = in_Q @ W_Q + b_Q
        K = in_K @ W_K + b_K
        V = in_V @ W_V + b_V
        Qh = Q.reshape(b, sq, N_HEADS, D_K).transpose(0, 2, 1, 3)
        Kh = K.reshape(b, sk, N_HEADS, D_K).transpose(0, 2, 1, 3)
        Vh = V.reshape(b, sk, N_HEADS, D_K).transpose(0, 2, 1, 3)
        scores = jnp.einsum('bhqd,bhkd->bhqk', Qh, Kh) / math.sqrt(D_K)
        causal = jnp.triu(jnp.full((sq, sk), neg_inf, dtype=scores.dtype), k=1)
        scores = scores + causal
        q_len = Q_pad_mask.sum(axis=1)
        k_len = K_pad_mask.sum(axis=1)
        q_valid = jnp.arange(sq)[None, :] < q_len[:, None]
        k_valid = jnp.arange(sk)[None, :] < k_len[:, None]
        non_padding = q_valid[:, :, None] & k_valid[:, None, :]
        scores = jnp.where(non_padding[:, None, :, :], scores, neg_inf)
        importances = jax.nn.softmax(scores, axis=-1)
        importances = jnp.nan_to_num(importances)
        attn = jnp.einsum('bhqk,bhkd->bhqd', importances, Vh)
        H = attn.transpose(0, 2, 1, 3).reshape(b, sq, D_MODEL)
        return H @ W_O + b_O

    def _L1_ffn_ref(x, W_fc, ln_w, ln_b, W_proj):
        import jax, jax.numpy as jnp
        import numpy as np
        EPS = 1e-06
        LN_EPS = 1e-05

        def _absmean_core(W):
            gamma = jnp.mean(jnp.abs(W)) + EPS
            Ws = W / gamma
            Wq = jnp.sign(Ws) * jnp.minimum(jnp.round(jnp.abs(Ws)), 1.0)
            return (Wq, gamma)

        @jax.custom_vjp
        def absmean(W):
            return _absmean_core(W)[0]

        def _absmean_fwd(W):
            Wq, gamma = _absmean_core(W)
            return (Wq, gamma)

        def _absmean_bwd(gamma, g):
            return (g / gamma,)
        absmean.defvjp(_absmean_fwd, _absmean_bwd)

        def layernorm(x, w, b, eps=LN_EPS):
            mu = jnp.mean(x, axis=-1, keepdims=True)
            var = jnp.mean((x - mu) ** 2, axis=-1, keepdims=True)
            return (x - mu) * jax.lax.rsqrt(var + eps) * w + b
        h = jnp.einsum('btd,hd->bth', x, absmean(W_fc))
        h = jax.nn.gelu(h, approximate=False)
        h = layernorm(h, ln_w, ln_b)
        return jnp.einsum('bth,dh->btd', h, absmean(W_proj))

    def _L2_xattn_ref(x, context, mask, Wq, Wkv, Wo, qn_w, kn_w):
        import jax, jax.numpy as jnp
        import numpy as np
        DIM = 128
        HEAD_DIM = 64
        NUM_HEADS = DIM // HEAD_DIM
        EPS = 1e-06
        SCALE = HEAD_DIM ** (-0.5)

        def _per_head_ln(t, w):
            mu = jnp.mean(t, axis=-1, keepdims=True)
            var = jnp.mean(jnp.square(t - mu), axis=-1, keepdims=True)
            t = (t - mu) * jax.lax.rsqrt(var + EPS)
            return t * w[None, :, None, :]
        B, N, C = x.shape
        M = context.shape[1]
        H, D = (NUM_HEADS, HEAD_DIM)
        q = (x @ Wq).reshape(B, N, H, D).transpose(0, 2, 1, 3)
        kv = (context @ Wkv).reshape(B, M, 2, H, D)
        k = kv[:, :, 0].transpose(0, 2, 1, 3)
        v = kv[:, :, 1].transpose(0, 2, 1, 3)
        q = _per_head_ln(q, qn_w)
        k = _per_head_ln(k, kn_w)
        attn = jnp.einsum('bhnd,bhmd->bhnm', q, k) * SCALE
        attn = jnp.where(mask[:, None, :, :], attn, -jnp.inf)
        attn = jax.nn.softmax(attn, axis=-1)
        out = jnp.einsum('bhnm,bhmd->bhnd', attn, v)
        out = out.transpose(0, 2, 1, 3).reshape(B, N, C)
        return out @ Wo

    def _L2_ffn_ref(hidden_states, Wg, W1, b1, W2, b2):
        import jax, jax.numpy as jnp
        import numpy as np
        B, S, H = (4, 256, 128)
        E, I, K = (8, 256, 2)
        b, s, h = hidden_states.shape
        x = hidden_states.reshape(-1, h)
        gate_logits = x @ Wg
        gate_probs = jax.nn.softmax(gate_logits, axis=-1)
        topk_probs, topk_idx = jax.lax.top_k(gate_probs, K)
        topk_probs = topk_probs / jnp.sum(topk_probs, axis=-1, keepdims=True)
        T = x.shape[0]
        w = jnp.zeros((T, E), dtype=x.dtype)
        w = w.at[jnp.arange(T)[:, None], topk_idx].set(topk_probs)
        h1 = jax.nn.gelu(jnp.einsum('th,ehi->eti', x, W1) + b1[:, None, :], approximate=False)
        y = jnp.einsum('eti,eih->eth', h1, W2) + b2[:, None, :]
        out = jnp.einsum('te,eth->th', w, y)
        return out.reshape(b, s, h)

    def _L3_xattn_ref(queries, keys, values, attn_bias, Wq, Wk, Wv, Wp):
        import jax, jax.numpy as jnp
        import numpy as np
        D_MODEL = 128
        N_HEAD = 16
        D_KEY = 64
        D_VALUE = 64

        def _split_heads(x, n_head, d_head):
            B, S, _ = x.shape
            return x.reshape(B, S, n_head, d_head).transpose(0, 2, 1, 3)
        q = _split_heads(queries @ Wq.T, N_HEAD, D_KEY)
        k = _split_heads(keys @ Wk.T, N_HEAD, D_KEY)
        v = _split_heads(values @ Wv.T, N_HEAD, D_VALUE)
        scores = jnp.einsum('bhqd,bhkd->bhqk', q, k) * D_MODEL ** (-0.5) + attn_bias
        weights = jax.nn.softmax(scores, axis=-1)
        out = jnp.einsum('bhqk,bhkd->bhqd', weights, v)
        B, H, Sq, Dv = out.shape
        out = out.transpose(0, 2, 1, 3).reshape(B, Sq, H * Dv)
        return out @ Wp.T

    def _L3_ffn_ref(x, gate, corr_bias, w1, w2, fc1_w, fc2_w, up_w, down_w):
        import jax, jax.numpy as jnp
        import numpy as np
        DIM = 128
        LATENT = 64
        INTER = 64
        SHARED = 512
        E = 8
        TOPK = 2
        NGROUP = 2
        TOPKG = 1
        NORM_TOPK = True
        SCALE = 1.0
        B, S = (2, 128)

        def relu2(x):
            r = jnp.maximum(x, 0.0)
            return r * r
        Bv, Sv, D = x.shape
        xf = x.reshape(-1, D)
        N = xf.shape[0]
        scores = jax.nn.sigmoid(xf.astype(jnp.float32) @ gate.T)
        sfc = scores + corr_bias
        gs = E // NGROUP
        if NGROUP > 1:
            group_scores = jax.lax.top_k(sfc.reshape(N, NGROUP, gs), 2)[0].sum(-1)
            gidx = jax.lax.top_k(group_scores, TOPKG)[1]
            gmask = jnp.zeros((N, NGROUP), sfc.dtype).at[jnp.arange(N)[:, None], gidx].set(1.0)
            smask = jnp.repeat(gmask, gs, axis=1)
            sfc = jnp.where(smask > 0, sfc, 0.0)
        sel = jax.lax.top_k(sfc, TOPK)[1]
        top_scores = jnp.take_along_axis(scores, sel, axis=1)
        if NORM_TOPK:
            top_scores = top_scores / (top_scores.sum(-1, keepdims=True) + 1e-20)
        flat = sel.reshape(-1)
        perm = jnp.argsort(flat, stable=True)
        sorted_eid = flat[perm]
        scores_sorted = top_scores.reshape(-1)[perm]
        tok = perm // TOPK
        lat = xf @ fc1_w.T
        xs = lat[tok]
        out = jnp.zeros_like(xs)
        for e in range(E):
            he = relu2(xs @ w1[e].T) @ w2[e].T
            out = jnp.where((sorted_eid == e)[:, None], he, out)
        out = out * scores_sorted[:, None]
        comb = jnp.zeros((N, LATENT), out.dtype).at[tok].add(out)
        routed = comb @ fc2_w.T * SCALE
        shared = relu2(xf @ up_w.T) @ down_w.T
        return (routed + shared).reshape(Bv, Sv, D)
    x = x + _L0_xattn_ref(ctx_1024, ctx_1024, _layernorm(x, axis=-1), L0_xattn_Wk, L0_xattn_Wv, L0_xattn_bv, L0_xattn_Wq, L0_xattn_bq, L0_xattn_Wo, L0_xattn_bo)
    x = x + _L0_ffn_ref(_layernorm(x, axis=-1), L0_ffn_q_w, L0_ffn_k_w, L0_ffn_v_w, L0_ffn_o_w, L0_ffn_sel_v_w, L0_ffn_sel_o_w, L0_ffn_route_scale)
    x = x + _L1_xattn_ref(_layernorm(x, axis=-1), ctx_1024, ctx_1024, mask_BxS2_if1, mask_BxS2_ik0, L1_xattn_W_Q, L1_xattn_b_Q, L1_xattn_W_K, L1_xattn_b_K, L1_xattn_W_V, L1_xattn_b_V, L1_xattn_W_O, L1_xattn_b_O)
    x = x + _L1_ffn_ref(_layernorm(x, axis=-1), L1_ffn_W_fc, L1_ffn_ln_w, L1_ffn_ln_b, L1_ffn_W_proj)
    x = x + _L2_xattn_ref(_layernorm(x, axis=-1), ctx_1024, mask_BxSxS2_bk0, L2_xattn_Wq, L2_xattn_Wkv, L2_xattn_Wo, L2_xattn_qn_w, L2_xattn_kn_w)
    x = x + _L2_ffn_ref(_layernorm(x, axis=-1), L2_ffn_Wg, L2_ffn_W1, L2_ffn_b1, L2_ffn_W2, L2_ffn_b2)
    x = x + _L3_xattn_ref(_layernorm(x, axis=-1), ctx_1024, ctx_1024, fside_1x1xSxS2_0, L3_xattn_Wq, L3_xattn_Wk, L3_xattn_Wv, L3_xattn_Wp)
    x = x + _L3_ffn_ref(_layernorm(x, axis=-1), L3_ffn_gate, L3_ffn_corr_bias, L3_ffn_w1, L3_ffn_w2, L3_ffn_fc1_w, L3_ffn_fc2_w, L3_ffn_up_w, L3_ffn_down_w)
    return x

_drawn_inputs = setup_inputs


def setup_inputs(seed=0):
    import zlib

    import numpy as np

    out = dict(_drawn_inputs(seed))
    spreads = {'L0_xattn_bv': (0.0, 0.1),
     'L0_xattn_bq': (0.0, 0.1),
     'L0_xattn_bo': (0.0, 0.1),
     'L1_xattn_b_Q': (0.0, 0.348),
     'L1_xattn_b_K': (0.0, 0.8),
     'L1_xattn_b_V': (0.0, 0.1),
     'L1_xattn_b_O': (0.0, 0.1),
     'L1_ffn_ln_w': (1.0, 0.2),
     'L1_ffn_ln_b': (0.0, 0.1),
     'L2_xattn_qn_w': (1.0, 0.6),
     'L2_xattn_kn_w': (1.0, 0.6),
     'L2_ffn_b1': (0.0, 0.8),
     'L2_ffn_b2': (0.0, 0.8),
     'L3_ffn_corr_bias': (0.0, 0.8)}
    factors = {'fside_1x1xSxS2_0': 3.377,
     'L2_xattn_Wq': 8.0,
     'L2_xattn_Wkv': 8.0,
     'L2_xattn_Wo': 8.0,
     'L2_ffn_Wg': 8.0,
     'L2_ffn_W1': 8.0,
     'L2_ffn_W2': 8.0,
     'L3_ffn_gate': 8.0,
     'L3_ffn_w1': 8.0,
     'L3_ffn_w2': 8.0,
     'L3_ffn_fc1_w': 8.0,
     'L3_ffn_fc2_w': 8.0,
     'L3_ffn_up_w': 8.0,
     'L3_ffn_down_w': 8.0}
    for name, (base, spread) in spreads.items():
        noise = np.random.default_rng([zlib.crc32(name.encode()), seed]).standard_normal(out[name].shape)
        drawn = base * np.exp(spread * noise) if base else spread * noise
        out[name] = jnp.asarray(drawn.astype(out[name].dtype))
    for name, factor in factors.items():
        out[name] = (out[name] * factor).astype(out[name].dtype)
    return out
```

```python
from contextlib import ExitStack

import concourse.bass as bass
from concourse import mybir

F32 = mybir.dt.float32
ALU = mybir.AluOpType
ACT = mybir.ActivationFunctionType
AX = mybir.AxisListType

B, S, K, D = 8, 128, 120, 128
E = 8
LANES = (0, 1)
L0X, L0F, L1X, L1F, L2X, L2F, L3X, L3F = range(8)
H0F, H1X, H2X, H3X = 8, 16, 2, 16
MASKED = -1e30
GONE = -1e30

PACKS = {
    "const": [("ident", 128), ("causal", K), ("iota_k", K), ("iota_q", 1), ("first", E), ("head_rows", H1X),
              ("ones", 128), ("minus_half", 4)],
    "L0x": [("wk", D), ("wv", D), ("wq", D), ("wo", D), ("bq", 1), ("bv", D), ("bo", D)],
    "L0f": [("sel", 2 * H0F * E), ("qk", 2 * H0F * D), ("route", 1)],
    "L0v": [("v", H0F * E * D)],
    "L0o": [("o", H0F * E * D)],
    "L1x": [("wk", D), ("wv", D), ("wq", D), ("wo", D), ("bq", 1), ("bk", 1), ("bv", D), ("bo", D)],
    "L1f": [("fc", 512), ("proj", 512), ("lnw", 4), ("lnb", 4)],
    "L2x": [("wkv", 2 * D), ("wq", D), ("wo", D), ("qn", 1), ("kn", 1)],
    "L2f": [("wg", E), ("w1", 2048), ("b1", 16), ("w2", 2048), ("b2", D)],
    "L3x": [("wk", 1024), ("wv", 1024), ("wq", 1024), ("wp", 1024), ("bias", K)],
    "L3f": [("gate", E), ("cb", E), ("fc1", 64), ("w1", 512), ("w2", 256), ("fc2", D), ("up", 512), ("down", 512)],
}


def width(pack):
    return sum(n for _, n in PACKS[pack])


def build(nc, x_in, ctx_in, q_mask, k_mask, pair_mask, packs, out):
    with ExitStack() as stack:
        def sb(name, shape, dt=F32):
            return stack.enter_context(nc.sbuf_tensor(name, shape, dt))

        def sem(name):
            return stack.enter_context(nc.semaphore(name))

        class Step:

            def __init__(self, name, per_layer):
                self.sems = [sem(f"{name}_{lane}") for lane in LANES]
                self.per_layer = per_layer

            def __getitem__(self, lane):
                return self.sems[lane]

            def upto(self, layer, n):
                assert 1 <= n <= self.per_layer[layer]
                return sum(self.per_layer[:layer]) + n

        part, loaded = {}, {}
        for pack, members in PACKS.items():
            t = sb(f"w_{pack}", [128, width(pack)])
            at = 0
            for name, n in members:
                part[pack, name] = t[:, at:at + n]
                at += n
            part[pack] = t
            loaded[pack] = sem(f"loaded_{pack}")
        inputs_loaded = sem("inputs_loaded")
        out_stored = sem("out_stored")
        setup_chain = sem("setup_chain")
        abs_summed = sem("abs_summed")
        abs_total = sem("abs_total")
        ident = part["const", "ident"]
        x_all = sb("x_all", [128, B * D])
        ctx_all = sb("ctx_all", [128, B * K])
        qm = sb("qm", [128, B * K], mybir.dt.int32)
        km = sb("km", [128, B * K], mybir.dt.int32)
        pm = sb("pm", [128, B * K], mybir.dt.uint8)
        q_len = sb("q_len", [128, B])
        k_len = sb("k_len", [128, B])
        abs_sum = sb("abs_sum", [128, 2])
        threshold = sb("threshold", [128, 4])

        def lanes(name, shape):
            return [sb(f"{name}_{lane}", shape) for lane in LANES]

        x = lanes("x", [128, D])
        x_bias = lanes("x_bias", [128, D])
        xn = lanes("xn", [128, D])
        xnT = lanes("xnT", [128, D])
        ctxT = lanes("ctxT", [128, K])
        wide_a = lanes("wide_a", [128, 2048])
        wide_b = lanes("wide_b", [128, 2048])
        v = lanes("v", [128, 1024])
        small = lanes("small", [128, 384])
        stats = lanes("stats", [128, 4, 6])
        mean_var = lanes("mean_var", [128, 4, 2])
        var_eps = lanes("var_eps", [128, 4])
        rstd = lanes("rstd", [128, 4])
        max_neg = lanes("max_neg", [128, 16])
        row_sum = lanes("row_sum", [128, 16])
        row_inv = lanes("row_inv", [128, 16])
        route = lanes("route", [128, 8, 128])
        per_head = lanes("per_head", [128, 4, 16])
        gate = lanes("gate", [128, 128])
        mask1 = lanes("mask1", [128, K])
        mask2 = lanes("mask2", [128, K])
        lens = lanes("lens", [128, 2])
        row_ok = lanes("row_ok", [128, 4])
        gateT = lanes("gateT", [128, S])
        bank = [[stack.enter_context(nc.psum_tensor(f"bank{lane}{i}", [128, 512], F32)) for i in range(4)]
                for lane in LANES]

        once = [1] * 8
        var_ready = Step("var_ready", [1, 1, 1, 2, 2, 1, 1, 1])
        rstd_ready = Step("rstd_ready", [1, 1, 1, 2, 3, 1, 1, 1])
        xn_ready = Step("xn_ready", once)
        xnT_psum = Step("xnT_psum", once)
        xnT_ready = Step("xnT_ready", once)
        lane_ready = Step("lane_ready", [1] + [0] * 7)
        masks_ready = Step("masks_ready", [0, 0, 1, 0, 0, 0, 0, 0])
        x_bias_ready = Step("x_bias_ready", [1, 0, 1, 0, 0, 0, 0, 0])
        x_ready = Step("x_ready", [1, 0, 1, 1, 1, 1, 1, 1])
        kv_psum = Step("kv_psum", [2, 0, 2, 0, 1, 0, 4, 0])
        kv_ready = Step("kv_ready", [1, 0, 1, 0, 1, 0, 4, 0])
        v_ready = Step("v_ready", [1, 0, 1, 0, 0, 0, 0, 0])
        v_mixed = Step("v_mixed", [0, 2 * H0F, 0, 0, 0, 0, 0, 0])
        k_blocks = Step("k_blocks", [0, 0, 1, 0, 0, 0, 0, 0])
        q_psum = Step("q_psum", [1, 4, 1, 0, 1, 0, 2, 0])
        q_ready = Step("q_ready", [1, 4, 1, 0, 1, 0, 2, 0])
        qk_normed = Step("qk_normed", [0, 0, 0, 0, 1, 0, 0, 0])
        qkT_psum = Step("qkT_psum", [0, 0, 0, 0, 1, 0, 0, 0])
        qkT_ready = Step("qkT_ready", [0, 0, 0, 0, 1, 0, 0, 0])
        scores_psum = Step("scores_psum", [1, 2, 4, 0, 1, 0, 4, 0])
        max_ready = Step("max_ready", [1, 1, 1, 0, 1, 0, 1, 0])
        probs_ready = Step("probs_ready", [1, 1, 1, 0, 1, 0, 1, 0])
        probs_normed = Step("probs_normed", [0, 0, 0, 0, 1, 0, 1, 0])
        inv_ready = Step("inv_ready", [0, 0, 0, 0, 0, 0, 1, 0])
        pT_psum = Step("pT_psum", [1, 2, 4, 0, 1, 0, 4, 0])
        pT_ready = Step("pT_ready", [1, 2, 4, 0, 1, 0, 4, 0])
        mix_psum = Step("mix_psum", [1, 2, 1, 0, 1, 0, 2, 0])
        mix_scaled = Step("mix_scaled", [0, 0, 1, 0, 0, 0, 0, 0])
        mixT_psum = Step("mixT_psum", [0, 0, 1, 0, 0, 0, 0, 0])
        mixT_ready = Step("mixT_ready", [1, 2, 1, 0, 1, 0, 2, 0])
        out_psum = Step("out_psum", [1, 2 * H0F, 1, 1, 1, 3, 1, 1])
        out_mixed = Step("out_mixed", [0, 2 * H0F, 0, 0, 0, 0, 0, 0])
        gate_psum = Step("gate_psum", [0, 1, 0, 0, 0, 1, 0, 1])
        logits_ready = Step("logits_ready", [0, 1, 0, 0, 0, 1, 0, 1])
        gate_exp = Step("gate_exp", [0, 0, 0, 0, 0, 1, 0, 0])
        gate_ready = Step("gate_ready", [0, 0, 0, 0, 0, 1, 0, 0])
        gateT_psum = Step("gateT_psum", [0, 0, 0, 0, 0, 1, 0, 0])
        gateT_ready = Step("gateT_ready", [0, 0, 0, 0, 0, 1, 0, 0])
        v_psum = Step("v_psum", [0, 2 * H0F, 0, 0, 0, 0, 0, 0])
        hidden_psum = Step("hidden_psum", [0, 0, 0, 1, 0, 4, 0, 3])
        hidden_ready = Step("hidden_ready", [0, 0, 0, 1, 0, 4, 0, 3])
        hidden_normed = Step("hidden_normed", [0, 0, 0, 1, 0, 0, 0, 0])
        hiddenT_psum = Step("hiddenT_psum", [0, 0, 0, 1, 0, 0, 0, 0])
        hiddenT_ready = Step("hiddenT_ready", [0, 0, 0, 1, 0, 0, 0, 0])
        squared = Step("squared", [0, 0, 0, 0, 0, 0, 0, 2])
        expert_psum = Step("expert_psum", [0, 0, 0, 0, 0, 0, 0, 1])
        expert_mixed = Step("expert_mixed", [0, 0, 0, 0, 0, 0, 0, 1])
        expertT_psum = Step("expertT_psum", [0, 0, 0, 0, 0, 0, 0, 1])
        expertT_ready = Step("expertT_ready", [0, 0, 0, 0, 0, 0, 0, 1])
        dve_chain = sem("dve_chain")
        pool_chain = sem("pool_chain")
        turn_sems = [s for st in (
            var_ready, rstd_ready, xn_ready, xnT_psum, xnT_ready, lane_ready, masks_ready, x_bias_ready, x_ready,
            kv_psum, kv_ready, v_ready, v_mixed, k_blocks, q_psum, q_ready, qk_normed, qkT_psum, qkT_ready,
            scores_psum, max_ready, probs_ready, probs_normed, inv_ready, pT_psum, pT_ready, mix_psum, mix_scaled,
            mixT_psum, mixT_ready, out_psum, out_mixed, gate_psum, logits_ready, gate_exp, gate_ready, gateT_psum,
            gateT_ready, v_psum, hidden_psum, hidden_ready, hidden_normed, hiddenT_psum, hiddenT_ready, squared,
            expert_psum, expert_mixed, expertT_psum, expertT_ready) for s in st.sems] + [dve_chain, pool_chain]
        numbers = sorted(s.num for s in turn_sems)
        assert numbers[-1] - numbers[0] + 1 == len(numbers)

        with nc.Block() as block:
            @block.sync
            def _(sp):
                sp.dma_start(part["const"][:, :], packs["const"]).then_inc(loaded["const"], 16)
                sp.dma_start(x_all[:, :], x_in).then_inc(inputs_loaded, 16)
                sp.dma_start(ctx_all[:, :], ctx_in).then_inc(inputs_loaded, 16)
                for pack in ("L0x", "L1f", "L0f", "L0v", "L1x", "L2x", "L3x"):
                    sp.dma_start(part[pack][:, :], packs[pack]).then_inc(loaded[pack], 16)

            @block.scalar
            def _(act):
                act.dma_start(qm[:, :], q_mask).then_inc(inputs_loaded, 16)
                act.dma_start(km[:, :], k_mask).then_inc(inputs_loaded, 16)
                act.dma_start(pm[:, :], pair_mask).then_inc(inputs_loaded, 16)
                for pack in ("L0o", "L2f", "L3f"):
                    act.dma_start(part[pack][:, :], packs[pack]).then_inc(loaded[pack], 16)

            @block.vector
            def _(dve):
                chain = [0]

                def link(ins):
                    chain[0] += 1
                    ins.then_inc(setup_chain, 1)
                    dve.wait_ge(setup_chain, chain[0])

                dve.wait_ge(inputs_loaded, 5 * 16)
                nc.vector.tensor_reduce(q_len[:, :], qm[:, :].rearrange("p (b k) -> p b k", k=K), AX.X, ALU.add)
                nc.vector.tensor_reduce(k_len[:, :], km[:, :].rearrange("p (b k) -> p b k", k=K), AX.X, ALU.add)
                dve.wait_ge(loaded["L1f"], 16)
                for i, name in enumerate(("fc", "proj")):
                    last = nc.vector.tensor_reduce(abs_sum[:, i:i + 1], part["L1f", name], AX.X, ALU.add,
                                                   apply_absolute_value=True)
                last.then_inc(abs_summed, 1)
                dve.wait_ge(abs_total, 1)
                link(nc.vector.tensor_scalar(threshold[:, 0:2], bank[0][0][:, 0:2], 1.0 / (512 * D), 1e-6, ALU.mult, ALU.add))
                link(nc.vector.tensor_scalar(threshold[:, 2:4], threshold[:, 0:2], -0.5, None, ALU.mult))
                link(nc.vector.tensor_scalar(threshold[:, 0:2], threshold[:, 0:2], 0.5, None, ALU.mult))
                for i, name in enumerate(("fc", "proj")):
                    w = part["L1f", name]
                    below = wide_b[0][:, 512 * i:512 * (i + 1)]
                    link(nc.vector.tensor_scalar(below, w, threshold[:, 2 + i:3 + i], None, ALU.is_lt))
                    link(nc.vector.tensor_scalar(w, w, threshold[:, i:i + 1], None, ALU.is_gt))
                    link(nc.vector.tensor_tensor(w, w, below, ALU.subtract))

            @block.tensor
            def _(pe):
                pe.wait_ge(loaded["const"], 16)
                pe.wait_ge(abs_summed, 1)
                nc.tensor.matmul(bank[0][0][:, 0:2], part["const", "ones"], abs_sum[:, :],
                                 start=True, stop=True).then_inc(abs_total, 1)

        with nc.Fori(0, B // len(LANES)) as turn:
            b = turn * len(LANES)
            with nc.Block() as block:
                @block.sync
                def _(sp):
                    for lane in LANES:
                        sp.wait_ge(x_ready[lane], x_ready.upto(L3F, 1))
                        sp.dma_start(out[:, bass.ds((b + lane) * D, D)], x[lane][:, :]).then_inc(out_stored, 16)
                    sp.wait_ge(out_stored, 16 * len(LANES))

                @block.tensor
                def _(pe):
                    def mm(o, lhsT, rhs, first=True, last=True):
                        return nc.tensor.matmul(o, lhsT, rhs, start=first, stop=last)

                    def turn_x(lane, layer):
                        pe.wait_ge(xn_ready[lane], xn_ready.upto(layer, 1))
                        nc.tensor.transpose(bank[lane][0][:, 0:S], xn[lane][:, :], ident)\
                            .then_inc(xnT_psum[lane], 1)

                    def keys_values(lane, layer, pack):
                        b1, b2 = bank[lane][1], bank[lane][2]
                        mm(b1[:, 0:K], part[pack, "wk"], ctxT[lane][:, :]).then_inc(kv_psum[lane], 1)
                        mm(b2[0:K, 0:D], ctxT[lane][:, :], part[pack, "wv"]).then_inc(kv_psum[lane], 1)

                    pe.wait_ge(loaded["L0x"], 16)
                    for lane in LANES:
                        pe.wait_ge(lane_ready[lane], 1)
                        keys_values(lane, L0X, "L0x")
                        turn_x(lane, L0X)
                    for lane in LANES:
                        pe.wait_ge(xnT_ready[lane], xnT_ready.upto(L0X, 1))
                        mm(bank[lane][3][:, 0:S], part["L0x", "wq"], xnT[lane][:, :]).then_inc(q_psum[lane], 1)
                    for lane in LANES:
                        pe.wait_ge(kv_ready[lane], kv_ready.upto(L0X, 1))
                        pe.wait_ge(q_ready[lane], q_ready.upto(L0X, 1))
                        mm(bank[lane][0][:, 0:K], wide_a[lane][:, 0:S], wide_a[lane][:, 1024:1024 + K])\
                            .then_inc(scores_psum[lane], 1)
                    for lane in LANES:
                        pe.wait_ge(probs_ready[lane], probs_ready.upto(L0X, 1))
                        nc.tensor.transpose(bank[lane][1][0:K, 0:S], wide_b[lane][:, 0:K], ident)\
                            .then_inc(pT_psum[lane], 1)
                    for lane in LANES:
                        pe.wait_ge(v_ready[lane], v_ready.upto(L0X, 1))
                        pe.wait_ge(pT_ready[lane], pT_ready.upto(L0X, 1))
                        mm(bank[lane][2][:, 0:S], v[lane][0:K, 0:D], wide_a[lane][0:K, 0:S]).then_inc(mix_psum[lane], 1)
                    for lane in LANES:
                        pe.wait_ge(mixT_ready[lane], mixT_ready.upto(L0X, 1))
                        mm(bank[lane][3][:, 0:D], wide_b[lane][:, 0:S], part["L0x", "wo"]).then_inc(out_psum[lane], 1)

                    pe.wait_ge(loaded["L0f"], 16)
                    for lane in LANES:
                        turn_x(lane, L0F)
                    for lane in LANES:
                        pe.wait_ge(xnT_ready[lane], xnT_ready.upto(L0F, 1))
                        mm(bank[lane][1][:, 0:128], xnT[lane][:, :], part["L0f", "sel"]).then_inc(gate_psum[lane], 1)
                        for i, b_to in enumerate((2, 3, 0, 1)):
                            if b_to == 1:
                                pe.wait_ge(logits_ready[lane], logits_ready.upto(L0F, 1))
                            for c in range(4):
                                at = 512 * i + 128 * c
                                last = mm(bank[lane][b_to][:, 128 * c:128 * c + 128],
                                          part["L0f", "qk"][:, at:at + 128], xnT[lane][:, :])
                            last.then_inc(q_psum[lane], 1)
                    for lane in LANES:
                        pe.wait_ge(q_ready[lane], q_ready.upto(L0F, 4))
                        for h in range(H0F):
                            last = mm(bank[lane][2 + h // 4][:, 128 * (h % 4):128 * (h % 4) + 128],
                                      wide_a[lane][:, 128 * h:128 * h + 128],
                                      wide_a[lane][:, 1024 + 128 * h:1024 + 128 * h + 128])
                            if h % 4 == 3:
                                last.then_inc(scores_psum[lane], 1)
                    pe.wait_ge(loaded["L0v"], 16)
                    for h in range(H0F):
                        for lane in LANES:
                            if h == 1:
                                pe.wait_ge(probs_ready[lane], probs_ready.upto(L0F, 1))
                            for half in range(2):
                                if h >= 2:
                                    pe.wait_ge(v_mixed[lane], v_mixed.upto(L0F, 2 * (h - 2) + half + 1))
                                at = (2 * h + half) * 512
                                mm(bank[lane][2 * (h % 2) + half][:, :], xnT[lane][:, :],
                                   part["L0v", "v"][:, at:at + 512]).then_inc(v_psum[lane], 1)
                    for lane in LANES:
                        for half in range(2):
                            pe.wait_ge(v_mixed[lane], v_mixed.upto(L0F, 2 * (H0F - 2) + half + 1))
                            for c in range(4):
                                h = 4 * half + c
                                last = nc.tensor.transpose(bank[lane][half][:, 128 * c:128 * c + 128],
                                                           wide_b[lane][:, 128 * h:128 * h + 128], ident)
                            last.then_inc(pT_psum[lane], 1)
                    for lane in LANES:
                        for half in range(2):
                            pe.wait_ge(pT_ready[lane], pT_ready.upto(L0F, half + 1))
                            pe.wait_ge(v_mixed[lane], v_mixed.upto(L0F, 2 * H0F))
                            for c in range(4):
                                h = 4 * half + c
                                last = mm(bank[lane][2 + half][:, 128 * c:128 * c + 128],
                                          v[lane][:, 128 * h:128 * h + 128], wide_a[lane][:, 128 * h:128 * h + 128])
                            last.then_inc(mix_psum[lane], 1)
                    pe.wait_ge(loaded["L0o"], 16)
                    for h in range(H0F):
                        for lane in LANES:
                            if h in (0, 1):
                                pe.wait_ge(mixT_ready[lane], mixT_ready.upto(L0F, h + 1))
                            for half in range(2):
                                if h >= 2:
                                    pe.wait_ge(out_mixed[lane], out_mixed.upto(L0F, 2 * (h - 2) + half + 1))
                                at = (2 * h + half) * 512
                                mm(bank[lane][2 * (h % 2) + half][:, :], wide_b[lane][:, 128 * h:128 * h + 128],
                                   part["L0o", "o"][:, at:at + 512]).then_inc(out_psum[lane], 1)

                    pe.wait_ge(loaded["L1x"], 16)
                    for lane in LANES:
                        pe.wait_ge(out_mixed[lane], out_mixed.upto(L0F, 2 * H0F))
                        keys_values(lane, L1X, "L1x")
                        turn_x(lane, L1X)
                    for lane in LANES:
                        pe.wait_ge(xnT_ready[lane], xnT_ready.upto(L1X, 1))
                        mm(bank[lane][3][:, 0:S], part["L1x", "wq"], xnT[lane][:, :]).then_inc(q_psum[lane], 1)
                    for lane in LANES:
                        pe.wait_ge(q_ready[lane], q_ready.upto(L1X, 1))
                        pe.wait_ge(v_ready[lane], v_ready.upto(L1X, 1))
                        pe.wait_ge(k_blocks[lane], k_blocks.upto(L1X, 1))
                        for i in range(4):
                            mm(bank[lane][i][:, 0:4 * K], small[lane][:, 0:S],
                               wide_a[lane][:, 4 * K * i:4 * K * (i + 1)]).then_inc(scores_psum[lane], 1)
                    for lane in LANES:
                        pe.wait_ge(probs_ready[lane], probs_ready.upto(L1X, 1))
                        for i in range(4):
                            for c in range(4):
                                h = 4 * i + c
                                last = nc.tensor.transpose(bank[lane][i][0:K, 128 * c:128 * c + 128],
                                                           wide_b[lane][:, K * h:K * h + K], ident)
                            last.then_inc(pT_psum[lane], 1)
                    for lane in LANES:
                        for h in range(H1X):
                            if h % 4 == 0:
                                pe.wait_ge(pT_ready[lane], pT_ready.upto(L1X, h // 4 + 1))
                            last = mm(bank[lane][0][:, 8 * h:8 * h + 8], wide_a[lane][0:K, 128 * h:128 * h + 128],
                                      v[lane][0:K, 8 * h:8 * h + 8])
                        last.then_inc(mix_psum[lane], 1)
                    for lane in LANES:
                        pe.wait_ge(mix_scaled[lane], mix_scaled.upto(L1X, 1))
                        nc.tensor.transpose(bank[lane][1][:, 0:S], small[lane][:, 256:384], ident)\
                            .then_inc(mixT_psum[lane], 1)
                    for lane in LANES:
                        pe.wait_ge(mixT_ready[lane], mixT_ready.upto(L1X, 1))
                        mm(bank[lane][2][:, 0:D], wide_b[lane][:, 0:S], part["L1x", "wo"]).then_inc(out_psum[lane], 1)

                    for lane in LANES:
                        turn_x(lane, L1F)
                    for lane in LANES:
                        pe.wait_ge(xnT_ready[lane], xnT_ready.upto(L1F, 1))
                        mm(bank[lane][1][:, :], xnT[lane][:, :], part["L1f", "fc"]).then_inc(hidden_psum[lane], 1)
                    for lane in LANES:
                        pe.wait_ge(hidden_normed[lane], hidden_normed.upto(L1F, 1))
                        for c in range(4):
                            last = nc.tensor.transpose(bank[lane][2][:, 128 * c:128 * c + 128],
                                                       wide_b[lane][:, 512 + 128 * c:512 + 128 * c + 128], ident)
                        last.then_inc(hiddenT_psum[lane], 1)
                    for lane in LANES:
                        pe.wait_ge(hiddenT_ready[lane], hiddenT_ready.upto(L1F, 1))
                        for c in range(4):
                            last = mm(bank[lane][3][:, 0:D], wide_a[lane][:, 128 * c:128 * c + 128],
                                      part["L1f", "proj"][:, 128 * c:128 * c + 128], c == 0, c == 3)
                        last.then_inc(out_psum[lane], 1)

                    pe.wait_ge(loaded["L2x"], 16)
                    for lane in LANES:
                        mm(bank[lane][1][0:K, 0:2 * D], ctxT[lane][:, :], part["L2x", "wkv"]).then_inc(kv_psum[lane], 1)
                    for lane in LANES:
                        turn_x(lane, L2X)
                    for lane in LANES:
                        pe.wait_ge(xnT_ready[lane], xnT_ready.upto(L2X, 1))
                        mm(bank[lane][2][:, 0:D], xnT[lane][:, :], part["L2x", "wq"]).then_inc(q_psum[lane], 1)
                    for lane in LANES:
                        pe.wait_ge(qk_normed[lane], qk_normed.upto(L2X, 1))
                        nc.tensor.transpose(bank[lane][3][:, 0:S], small[lane][:, 0:D], ident)
                        nc.tensor.transpose(bank[lane][3][:, S:S + K], small[lane][0:K, D:2 * D], ident[0:K, 0:K])\
                            .then_inc(qkT_psum[lane], 1)
                    for lane in LANES:
                        pe.wait_ge(qkT_ready[lane], qkT_ready.upto(L2X, 1))
                        for h in range(H2X):
                            r = slice(64 * h, 64 * h + 64)
                            last = mm(bank[lane][h][:, 0:K], wide_a[lane][r, 0:S], wide_a[lane][r, S:S + K])
                        last.then_inc(scores_psum[lane], 1)
                    for lane in LANES:
                        pe.wait_ge(probs_normed[lane], probs_normed.upto(L2X, 1))
                        for h in range(H2X):
                            last = nc.tensor.transpose(bank[lane][2][0:K, 128 * h:128 * h + 128],
                                                       wide_b[lane][:, K * h:K * h + K], ident)
                        last.then_inc(pT_psum[lane], 1)
                    for lane in LANES:
                        pe.wait_ge(pT_ready[lane], pT_ready.upto(L2X, 1))
                        for h in range(H2X):
                            r = slice(64 * h, 64 * h + 64)
                            last = mm(bank[lane][3][r, 0:S], v[lane][0:K, D + 64 * h:D + 64 * h + 64],
                                      wide_a[lane][0:K, 256 + 128 * h:256 + 128 * h + 128])
                        last.then_inc(mix_psum[lane], 1)
                    for lane in LANES:
                        pe.wait_ge(mixT_ready[lane], mixT_ready.upto(L2X, 1))
                        mm(bank[lane][0][:, 0:D], wide_b[lane][:, 0:S], part["L2x", "wo"]).then_inc(out_psum[lane], 1)

                    pe.wait_ge(loaded["L2f"], 16)
                    for lane in LANES:
                        turn_x(lane, L2F)
                    for lane in LANES:
                        pe.wait_ge(xnT_ready[lane], xnT_ready.upto(L2F, 1))
                        mm(bank[lane][1][:, 0:E], xnT[lane][:, :], part["L2f", "wg"]).then_inc(gate_psum[lane], 1)
                        for i, b_to in enumerate((2, 3, 0, 1)):
                            if b_to == 1:
                                pe.wait_ge(logits_ready[lane], logits_ready.upto(L2F, 1))
                            for c in range(4):
                                at = 512 * i + 128 * c
                                last = mm(bank[lane][b_to][:, 128 * c:128 * c + 128],
                                          part["L2f", "w1"][:, at:at + 128], xnT[lane][:, :])
                            last.then_inc(hidden_psum[lane], 1)
                    for lane in LANES:
                        for e in range(E):
                            if e % 2 == 0:
                                pe.wait_ge(hidden_ready[lane], hidden_ready.upto(L2F, e // 2 + 1))
                            for c in range(2):
                                at = 256 * e + 128 * c
                                last = mm(bank[lane][2 + e // 4][:, 128 * (e % 4):128 * (e % 4) + 128],
                                          wide_a[lane][:, at:at + 128], part["L2f", "w2"][:, at:at + 128],
                                          c == 0, c == 1)
                            if e % 4 == 3:
                                last.then_inc(out_psum[lane], 1)
                    for lane in LANES:
                        pe.wait_ge(gate_ready[lane], gate_ready.upto(L2F, 1))
                        nc.tensor.transpose(bank[lane][0][0:E, 0:S], gate[lane][:, 0:E], ident)\
                            .then_inc(gateT_psum[lane], 1)
                    for lane in LANES:
                        pe.wait_ge(gateT_ready[lane], gateT_ready.upto(L2F, 1))
                        mm(bank[lane][1][:, 0:D], gateT[lane][0:E, :], part["L2f", "b2"][0:E, :])\
                            .then_inc(out_psum[lane], 1)

                    pe.wait_ge(loaded["L3x"], 16)
                    for lane in LANES:
                        pe.wait_ge(x_ready[lane], x_ready.upto(L2F, 1))
                        for half in range(2):
                            for c in range(4):
                                at = 512 * half + 128 * c
                                last = mm(bank[lane][1 + half][:, 128 * c:128 * c + K],
                                          part["L3x", "wk"][:, at:at + 128], ctxT[lane][:, :])
                            last.then_inc(kv_psum[lane], 1)
                        mm(bank[lane][3][0:K, :], ctxT[lane][:, :], part["L3x", "wv"][:, 0:512])\
                            .then_inc(kv_psum[lane], 1)
                    for lane in LANES:
                        turn_x(lane, L3X)
                        pe.wait_ge(kv_ready[lane], kv_ready.upto(L3X, 1))
                        mm(bank[lane][1][0:K, :], ctxT[lane][:, :], part["L3x", "wv"][:, 512:1024])\
                            .then_inc(kv_psum[lane], 1)
                    for lane in LANES:
                        pe.wait_ge(xnT_ready[lane], xnT_ready.upto(L3X, 1))
                        for half in range(2):
                            pe.wait_ge(kv_ready[lane], kv_ready.upto(L3X, half + 2))
                            for c in range(4):
                                at = 512 * half + 128 * c
                                last = mm(bank[lane][2 + half][:, 128 * c:128 * c + 128],
                                          part["L3x", "wq"][:, at:at + 128], xnT[lane][:, :])
                            last.then_inc(q_psum[lane], 1)
                    for lane in LANES:
                        pe.wait_ge(kv_ready[lane], kv_ready.upto(L3X, 4))
                        pe.wait_ge(q_ready[lane], q_ready.upto(L3X, 2))
                        for i in range(4):
                            for c in range(4):
                                odd, chunk = i // 2, 4 * (i % 2) + c
                                r = slice(64 * odd, 64 * odd + 64)
                                last = mm(bank[lane][i][:, K * c:K * c + K],
                                          wide_a[lane][r, 128 * chunk:128 * chunk + 128],
                                          wide_a[lane][r, 1024 + 128 * chunk:1024 + 128 * chunk + K])
                            last.then_inc(scores_psum[lane], 1)
                    for lane in LANES:
                        pe.wait_ge(probs_normed[lane], probs_normed.upto(L3X, 1))
                        for i in range(4):
                            for c in range(4):
                                h = 4 * i + c
                                last = nc.tensor.transpose(bank[lane][i][0:K, 128 * c:128 * c + 128],
                                                           wide_b[lane][:, K * h:K * h + K], ident)
                            last.then_inc(pT_psum[lane], 1)
                    for lane in LANES:
                        pe.wait_ge(pT_ready[lane], pT_ready.upto(L3X, 4))
                        for half in range(2):
                            for c in range(4):
                                for odd in range(2):
                                    chunk = 4 * half + c
                                    at, h = 128 * (8 * odd + chunk), 2 * chunk + odd
                                    last = mm(bank[lane][half][64 * odd:64 * odd + 64, 128 * c:128 * c + 128],
                                              v[lane][0:K, 64 * h:64 * h + 64], wide_a[lane][0:K, at:at + 128])
                            last.then_inc(mix_psum[lane], 1)
                    for lane in LANES:
                        for c in range(8):
                            if c % 4 == 0:
                                pe.wait_ge(mixT_ready[lane], mixT_ready.upto(L3X, c // 4 + 1))
                            last = mm(bank[lane][2][:, 0:D], wide_b[lane][:, 128 * c:128 * c + 128],
                                      part["L3x", "wp"][:, 128 * c:128 * c + 128], c == 0, c == 7)
                        last.then_inc(out_psum[lane], 1)

                    pe.wait_ge(loaded["L3f"], 16)
                    for lane in LANES:
                        turn_x(lane, L3F)
                    for lane in LANES:
                        pe.wait_ge(xnT_ready[lane], xnT_ready.upto(L3F, 1))
                        mm(bank[lane][1][:, 0:E], xnT[lane][:, :], part["L3f", "gate"]).then_inc(gate_psum[lane], 1)
                        mm(bank[lane][2][0:64, 0:S], part["L3f", "fc1"], xnT[lane][:, :]).then_inc(hidden_psum[lane], 1)
                        for c in range(4):
                            last = mm(bank[lane][3][:, 128 * c:128 * c + 128],
                                      part["L3f", "up"][:, 128 * c:128 * c + 128], xnT[lane][:, :])
                        last.then_inc(hidden_psum[lane], 1)
                    for lane in LANES:
                        pe.wait_ge(hidden_ready[lane], hidden_ready.upto(L3F, 1))
                        pe.wait_ge(logits_ready[lane], logits_ready.upto(L3F, 1))
                        for p in range(4):
                            last = mm(bank[lane][1][:, 128 * p:128 * p + 128],
                                      part["L3f", "w1"][0:64, 128 * p:128 * p + 128], small[lane][0:64, 0:S])
                        last.then_inc(hidden_psum[lane], 1)
                    for lane in LANES:
                        pe.wait_ge(squared[lane], squared.upto(L3F, 2))
                        for odd in range(2):
                            r = slice(64 * odd, 64 * odd + 64)
                            for p in range(4):
                                last = mm(bank[lane][2 * odd][:, 64 * p:64 * p + 64],
                                          wide_a[lane][r, 512 + 128 * p:512 + 128 * p + 128],
                                          part["L3f", "w2"][r, 64 * p:64 * p + 64])
                        last.then_inc(expert_psum[lane], 1)
                    for lane in LANES:
                        pe.wait_ge(squared[lane], squared.upto(L3F, 1))
                        for c in range(4):
                            mm(bank[lane][3][:, 0:D], wide_a[lane][:, 128 * c:128 * c + 128],
                               part["L3f", "down"][:, 128 * c:128 * c + 128], c == 0, False)
                        pe.wait_ge(expert_mixed[lane], expert_mixed.upto(L3F, 1))
                        nc.tensor.transpose(bank[lane][1][0:64, 0:S], gate[lane][:, 64:128], ident)\
                            .then_inc(expertT_psum[lane], 1)
                        pe.wait_ge(expertT_ready[lane], expertT_ready.upto(L3F, 1))
                        mm(bank[lane][3][:, 0:D], gateT[lane][0:64, :], part["L3f", "fc2"][0:64, :], False, True)\
                            .then_inc(out_psum[lane], 1)

                @block.scalar
                def _(act):
                    def copy(o, i, bias=0.0, scale=1.0):
                        return nc.scalar.activation(o, i, ACT.Identity, bias=bias, scale=scale)

                    def take_xT(lane, layer):
                        act.wait_ge(xnT_psum[lane], xnT_psum.upto(layer, 1))
                        copy(xnT[lane][:, :], bank[lane][0][:, 0:S]).then_inc(xnT_ready[lane], 1)

                    def exponentials(lane, layer, heads, scores, cols, scale):
                        act.wait_ge(max_ready[lane], max_ready.upto(layer, 1))
                        for h in range(heads):
                            last = nc.scalar.activation(wide_b[lane][:, cols * h:cols * h + cols], scores(lane, h), ACT.Exp,
                                                        bias=max_neg[lane][:, h:h + 1], scale=scale,
                                                        accum_out=row_sum[lane][:, h:h + 1])
                        last.then_inc(probs_ready[lane], 1)

                    for lane in LANES:
                        act.wait_ge(kv_psum[lane], kv_psum.upto(L0X, 1))
                        copy(wide_a[lane][:, 1024:1024 + K], bank[lane][1][:, 0:K]).then_inc(kv_ready[lane], 1)
                        take_xT(lane, L0X)
                    for lane in LANES:
                        act.wait_ge(q_psum[lane], q_psum.upto(L0X, 1))
                        copy(wide_a[lane][:, 0:S], bank[lane][3][:, 0:S], bias=part["L0x", "bq"]).then_inc(q_ready[lane], 1)
                    for lane in LANES:
                        exponentials(lane, L0X, 1, lambda n, h: bank[n][0][:, 0:K], K, D ** -0.5)
                    for lane in LANES:
                        act.wait_ge(pT_psum[lane], pT_psum.upto(L0X, 1))
                        copy(wide_a[lane][0:K, 0:S], bank[lane][1][0:K, 0:S]).then_inc(pT_ready[lane], 1)
                    for lane in LANES:
                        act.wait_ge(mix_psum[lane], mix_psum.upto(L0X, 1))
                        copy(wide_b[lane][:, 0:S], bank[lane][2][:, 0:S]).then_inc(mixT_ready[lane], 1)

                    for lane in LANES:
                        take_xT(lane, L0F)
                    for lane in LANES:
                        act.wait_ge(gate_psum[lane], gate_psum.upto(L0F, 1))
                        nc.scalar.activation(route[lane][:, 1, :], bank[lane][1][:, 0:128], ACT.Exp, scale=-1.0)
                        copy(route[lane][:, 0, :], bank[lane][1][:, 0:128]).then_inc(logits_ready[lane], 1)
                        for i, b_to in enumerate((2, 3, 0, 1)):
                            act.wait_ge(q_psum[lane], q_psum.upto(L0F, i + 1))
                            copy(wide_a[lane][:, 512 * i:512 * i + 512], bank[lane][b_to][:, :]).then_inc(q_ready[lane], 1)
                    for lane in LANES:
                        exponentials(lane, L0F, H0F,
                                     lambda n, h: bank[n][2 + h // 4][:, 128 * (h % 4):128 * (h % 4) + 128], S, D ** -0.5)
                    for lane in LANES:
                        for half in range(2):
                            act.wait_ge(pT_psum[lane], pT_psum.upto(L0F, half + 1))
                            copy(wide_a[lane][:, 512 * half:512 * half + 512], bank[lane][half][:, :])\
                                .then_inc(pT_ready[lane], 1)
                    for lane in LANES:
                        for half in range(2):
                            act.wait_ge(mix_psum[lane], mix_psum.upto(L0F, half + 1))
                            copy(wide_b[lane][:, 512 * half:512 * half + 512], bank[lane][2 + half][:, :])\
                                .then_inc(mixT_ready[lane], 1)

                    for lane in LANES:
                        act.wait_ge(kv_psum[lane], kv_psum.upto(L1X, 1))
                        copy(small[lane][:, 128:128 + K], bank[lane][1][:, 0:K], bias=part["L1x", "bk"])\
                            .then_inc(kv_ready[lane], 1)
                        take_xT(lane, L1X)
                    for lane in LANES:
                        act.wait_ge(q_psum[lane], q_psum.upto(L1X, 1))
                        copy(small[lane][:, 0:S], bank[lane][3][:, 0:S], bias=part["L1x", "bq"]).then_inc(q_ready[lane], 1)
                    for lane in LANES:
                        exponentials(lane, L1X, H1X, lambda n, h: wide_b[n][:, K * h:K * h + K], K, 8 ** -0.5)
                    for lane in LANES:
                        for i in range(4):
                            act.wait_ge(pT_psum[lane], pT_psum.upto(L1X, i + 1))
                            copy(wide_a[lane][0:K, 512 * i:512 * i + 512], bank[lane][i][0:K, :]).then_inc(pT_ready[lane], 1)
                    for lane in LANES:
                        act.wait_ge(mixT_psum[lane], mixT_psum.upto(L1X, 1))
                        copy(wide_b[lane][:, 0:S], bank[lane][1][:, 0:S]).then_inc(mixT_ready[lane], 1)

                    for lane in LANES:
                        take_xT(lane, L1F)
                    for lane in LANES:
                        act.wait_ge(hidden_psum[lane], hidden_psum.upto(L1F, 1))
                        nc.scalar.activation(wide_b[lane][:, 0:512], bank[lane][1][:, :], ACT.Gelu)\
                            .then_inc(hidden_ready[lane], 1)

                    for lane in LANES:
                        act.wait_ge(kv_psum[lane], kv_psum.upto(L2X, 1))
                        copy(v[lane][0:K, 0:2 * D], bank[lane][1][0:K, 0:2 * D]).then_inc(kv_ready[lane], 1)
                    for lane in LANES:
                        take_xT(lane, L2X)
                    for lane in LANES:
                        act.wait_ge(q_psum[lane], q_psum.upto(L2X, 1))
                        copy(small[lane][:, 256:256 + D], bank[lane][2][:, 0:D]).then_inc(q_ready[lane], 1)
                    for lane in LANES:
                        act.wait_ge(qkT_psum[lane], qkT_psum.upto(L2X, 1))
                        copy(wide_a[lane][:, 0:S], bank[lane][3][:, 0:S], scale=part["L2x", "qn"])
                        copy(wide_a[lane][:, S:S + K], bank[lane][3][:, S:S + K], scale=part["L2x", "kn"])\
                            .then_inc(qkT_ready[lane], 1)
                    for lane in LANES:
                        exponentials(lane, L2X, H2X, lambda n, h: wide_b[n][:, K * h:K * h + K], K, 64 ** -0.5)
                    for lane in LANES:
                        act.wait_ge(pT_psum[lane], pT_psum.upto(L2X, 1))
                        copy(wide_a[lane][0:K, 256:512], bank[lane][2][0:K, 0:256]).then_inc(pT_ready[lane], 1)
                    for lane in LANES:
                        act.wait_ge(mix_psum[lane], mix_psum.upto(L2X, 1))
                        copy(wide_b[lane][:, 0:S], bank[lane][3][:, 0:S]).then_inc(mixT_ready[lane], 1)

                    for lane in LANES:
                        take_xT(lane, L2F)
                    for lane in LANES:
                        act.wait_ge(logits_ready[lane], logits_ready.upto(L2F, 1))
                        nc.scalar.activation(route[lane][:, 1, 0:E], route[lane][:, 0, 0:E], ACT.Exp,
                                             bias=max_neg[lane][:, 0:1]).then_inc(gate_exp[lane], 1)
                    for lane in LANES:
                        for i, b_to in enumerate((2, 3, 0, 1)):
                            act.wait_ge(hidden_psum[lane], hidden_psum.upto(L2F, i + 1))
                            for c in range(4):
                                j = 4 * i + c
                                last = nc.scalar.activation(wide_a[lane][:, 128 * j:128 * j + 128],
                                                            bank[lane][b_to][:, 128 * c:128 * c + 128], ACT.Gelu,
                                                            bias=part["L2f", "b1"][:, j:j + 1])
                            last.then_inc(hidden_ready[lane], 1)
                    for lane in LANES:
                        act.wait_ge(gateT_psum[lane], gateT_psum.upto(L2F, 1))
                        copy(gateT[lane][0:E, :], bank[lane][0][0:E, 0:S]).then_inc(gateT_ready[lane], 1)

                    for lane in LANES:
                        for half in range(2):
                            act.wait_ge(kv_psum[lane], kv_psum.upto(L3X, half + 1))
                            copy(wide_a[lane][:, 1024 + 512 * half:1536 + 512 * half].rearrange("p (c k) -> p c k", c=4)[:, :, 0:K],
                                 bank[lane][1 + half][:, :].rearrange("p (c k) -> p c k", c=4)[:, :, 0:K])\
                                .then_inc(kv_ready[lane], 1)
                        act.wait_ge(kv_psum[lane], kv_psum.upto(L3X, 3))
                        copy(v[lane][0:K, 0:512], bank[lane][3][0:K, :]).then_inc(kv_ready[lane], 1)
                    for lane in LANES:
                        take_xT(lane, L3X)
                        act.wait_ge(kv_psum[lane], kv_psum.upto(L3X, 4))
                        copy(v[lane][0:K, 512:1024], bank[lane][1][0:K, :]).then_inc(kv_ready[lane], 1)
                    for lane in LANES:
                        for half in range(2):
                            act.wait_ge(q_psum[lane], q_psum.upto(L3X, half + 1))
                            copy(wide_a[lane][:, 512 * half:512 * half + 512], bank[lane][2 + half][:, :])\
                                .then_inc(q_ready[lane], 1)
                    for lane in LANES:
                        exponentials(lane, L3X, H3X, lambda n, h: wide_b[n][:, K * h:K * h + K], K, 1.0)
                    for lane in LANES:
                        for i in range(4):
                            act.wait_ge(pT_psum[lane], pT_psum.upto(L3X, i + 1))
                            copy(wide_a[lane][0:K, 512 * i:512 * i + 512], bank[lane][i][0:K, :]).then_inc(pT_ready[lane], 1)
                    for lane in LANES:
                        for half in range(2):
                            act.wait_ge(mix_psum[lane], mix_psum.upto(L3X, half + 1))
                            copy(wide_b[lane][:, 512 * half:512 * half + 512], bank[lane][half][:, :])\
                                .then_inc(mixT_ready[lane], 1)

                    for lane in LANES:
                        take_xT(lane, L3F)
                    for lane in LANES:
                        act.wait_ge(gate_psum[lane], gate_psum.upto(L3F, 1))
                        nc.scalar.activation(route[lane][:, 1, 0:E], bank[lane][1][:, 0:E], ACT.Exp, scale=-1.0)\
                            .then_inc(logits_ready[lane], 1)
                        act.wait_ge(hidden_psum[lane], hidden_psum.upto(L3F, 1))
                        copy(small[lane][0:64, 0:S], bank[lane][2][0:64, 0:S]).then_inc(hidden_ready[lane], 1)
                        act.wait_ge(hidden_psum[lane], hidden_psum.upto(L3F, 2))
                        nc.scalar.activation(wide_b[lane][:, 0:512], bank[lane][3][:, :], ACT.Relu)\
                            .then_inc(hidden_ready[lane], 1)
                    for lane in LANES:
                        act.wait_ge(hidden_psum[lane], hidden_psum.upto(L3F, 3))
                        nc.scalar.activation(wide_b[lane][:, 512:1024], bank[lane][1][:, :], ACT.Relu)\
                            .then_inc(hidden_ready[lane], 1)
                    for lane in LANES:
                        act.wait_ge(expertT_psum[lane], expertT_psum.upto(L3F, 1))
                        copy(gateT[lane][0:64, :], bank[lane][1][0:64, 0:S]).then_inc(expertT_ready[lane], 1)

                @block.gpsimd
                def _(pool):
                    chain = [0]

                    def link(ins):
                        chain[0] += 1
                        ins.then_inc(pool_chain, 1)
                        pool.wait_ge(pool_chain, chain[0])

                    def inverse_root(lane, layer, n, cols, rows=128):
                        pool.wait_ge(var_ready[lane], var_ready.upto(layer, n))
                        nc.gpsimd.tensor_tensor(rstd[lane][0:rows, cols], var_eps[lane][0:rows, cols],
                                                part["const", "minus_half"][0:rows, 0:cols.stop - cols.start], ALU.pow)\
                            .then_inc(rstd_ready[lane], 1)

                    one = slice(0, 1)
                    for lane in LANES:
                        nc.gpsimd.tensor_copy(ctxT[lane][:, :], ctx_all[:, bass.ds((b + lane) * K, K)])\
                            .then_inc(lane_ready[lane], 1)
                    for lane in LANES:
                        inverse_root(lane, L0X, 1, one)
                    for lane in LANES:
                        nc.gpsimd.tensor_tensor(x_bias[lane][:, :], x[lane][:, :], part["L0x", "bo"], ALU.add)\
                            .then_inc(x_bias_ready[lane], 1)
                    for lane in LANES:
                        link(nc.gpsimd.tensor_copy(lens[lane][:, 0:1], q_len[:, bass.ds(b + lane, 1)]))
                        link(nc.gpsimd.tensor_copy(lens[lane][:, 1:2], k_len[:, bass.ds(b + lane, 1)]))
                        link(nc.gpsimd.tensor_scalar(mask1[lane][:, :], part["const", "iota_k"], lens[lane][:, 1:2], MASKED,
                                                     ALU.is_ge, ALU.mult))
                        link(nc.gpsimd.tensor_tensor(mask1[lane][:, :], mask1[lane][:, :], part["const", "causal"], ALU.add))
                        link(nc.gpsimd.tensor_scalar(row_ok[lane][:, 0:1], lens[lane][:, 1:2], 1.0, None, ALU.is_ge))
                        link(nc.gpsimd.tensor_scalar(row_ok[lane][:, 1:2], part["const", "iota_q"], lens[lane][:, 0:1],
                                                     row_ok[lane][:, 0:1], ALU.is_lt, ALU.mult))
                        link(nc.gpsimd.tensor_copy(mask2[lane][:, :], pm[:, bass.ds((b + lane) * K, K)]))
                        link(nc.gpsimd.tensor_scalar(mask2[lane][:, :], mask2[lane][:, :], 0.5, None, ALU.is_lt))
                        nc.gpsimd.tensor_scalar(mask2[lane][:, :], mask2[lane][:, :], MASKED, None, ALU.mult)\
                            .then_inc(masks_ready[lane], 1)
                    for lane in LANES:
                        inverse_root(lane, L0F, 1, one)
                    for lane in LANES:
                        inverse_root(lane, L1X, 1, one)
                    for lane in LANES:
                        pool.wait_ge(kv_ready[lane], kv_ready.upto(L1X, 1))
                        nc.gpsimd.tensor_tensor(
                            wide_a[lane][:, 0:H1X * K].rearrange("p (h k) -> p h k", k=K),
                            small[lane][:, 128:128 + K].unsqueeze(1).broadcast_to([128, H1X, K]),
                            part["const", "head_rows"].unsqueeze(2).broadcast_to([128, H1X, K]), ALU.mult)\
                            .then_inc(k_blocks[lane], 1)
                        nc.gpsimd.tensor_tensor(x_bias[lane][:, :], x[lane][:, :], part["L1x", "bo"], ALU.add)\
                            .then_inc(x_bias_ready[lane], 1)
                    for lane in LANES:
                        inverse_root(lane, L1F, 1, one)
                    for lane in LANES:
                        inverse_root(lane, L1F, 2, one)
                    for lane in LANES:
                        inverse_root(lane, L2X, 1, one)
                    for lane in LANES:
                        inverse_root(lane, L2X, 2, slice(0, 2))
                        inverse_root(lane, L2X, 2, slice(2, 4), K)
                    for lane in LANES:
                        inverse_root(lane, L2F, 1, one)
                    for lane in LANES:
                        inverse_root(lane, L3X, 1, one)
                    for lane in LANES:
                        pool.wait_ge(inv_ready[lane], inv_ready.upto(L3X, 1))
                        p3 = wide_b[lane][:, 0:H3X * K].rearrange("p (h k) -> p h k", k=K)
                        nc.gpsimd.tensor_tensor(p3, p3, row_inv[lane][:, 0:H3X].unsqueeze(2).broadcast_to([128, H3X, K]),
                                                ALU.mult).then_inc(probs_normed[lane], 1)
                    for lane in LANES:
                        inverse_root(lane, L3F, 1, one)
                    for n in range(2):
                        for lane in LANES:
                            pool.wait_ge(hidden_ready[lane], hidden_ready.upto(L3F, n + 2))
                            r = wide_b[lane][:, 512 * n:512 * n + 512]
                            nc.gpsimd.tensor_tensor(wide_a[lane][:, 512 * n:512 * n + 512], r, r, ALU.mult)\
                                .then_inc(squared[lane], 1)

                @block.vector
                def _(dve):
                    chain = [0]

                    def link(ins):
                        chain[0] += 1
                        ins.then_inc(dve_chain, 1)
                        dve.wait_ge(dve_chain, chain[0])

                    def ts(o, i, s1, s2, op0, op1=None):
                        if op1 is None:
                            return nc.vector.tensor_scalar(o, i, s1, None, op0)
                        return nc.vector.tensor_scalar(o, i, s1, s2, op0, op1)

                    def tt(o, a, c, op):
                        return nc.vector.tensor_tensor(o, a, c, op)

                    def norm_stats(lane, layer):
                        link(nc.vector.bn_stats(stats[lane][:, 0, :], x[lane][:, :]))
                        link(nc.vector.bn_aggr(mean_var[lane][:, 0, :], stats[lane][:, 0, :]))
                        ts(var_eps[lane][:, 0:1], mean_var[lane][:, 0, 1:2], 1e-5, None, ALU.add)\
                            .then_inc(var_ready[lane], 1)

                    def norm_apply(lane, layer):
                        dve.wait_ge(rstd_ready[lane], rstd_ready.upto(layer, 1))
                        ts(xn[lane][:, :], x[lane][:, :], mean_var[lane][:, 0, 0:1], rstd[lane][:, 0:1],
                           ALU.subtract, ALU.mult).then_inc(xn_ready[lane], 1)

                    def norms(layer):
                        for lane in LANES:
                            norm_stats(lane, layer)
                        for lane in LANES:
                            norm_apply(lane, layer)

                    def x_done(lane, layer, ins):
                        ins.then_inc(x_ready[lane], 1)
                        dve.wait_ge(x_ready[lane], x_ready.upto(layer, 1))

                    def add_output(lane, layer, psum):
                        dve.wait_ge(out_psum[lane], out_psum.upto(layer, 1))
                        x_done(lane, layer, tt(x[lane][:, :], psum, x[lane][:, :], ALU.add))

                    def top2(lane, groups, values):
                        n = groups * E

                        def g(i):
                            return route[lane][:, i, 0:n].rearrange("p (g e) -> p g e", e=E)

                        def each(i):
                            return per_head[lane][:, i, 0:groups].unsqueeze(2).broadcast_to([128, groups, E])
                        order = part["const", "first"].unsqueeze(1).broadcast_to([128, groups, E])
                        left = values
                        for n_th in range(2):
                            link(nc.vector.tensor_reduce(per_head[lane][:, 2 * n_th, 0:groups], left, AX.X, ALU.max))
                            link(tt(g(3), left, each(2 * n_th), ALU.is_equal))
                            link(tt(g(3), g(3), order, ALU.mult))
                            link(nc.vector.tensor_reduce(per_head[lane][:, 1, 0:groups], g(3), AX.X, ALU.max))
                            link(tt(g(4 + n_th), g(3), each(1), ALU.is_equal))
                            if n_th == 0:
                                link(nc.vector.scalar_tensor_tensor(route[lane][:, 2, 0:n], route[lane][:, 4, 0:n], GONE,
                                                                    left.rearrange("p g e -> p (g e)"), ALU.mult, ALU.add))
                                left = g(2)
                        link(tt(g(5), g(4), g(5), ALU.add))

                    for lane in LANES:
                        link(nc.vector.tensor_copy(x[lane][:, :], x_all[:, bass.ds((b + lane) * D, D)]))
                    norms(L0X)
                    for lane in LANES:
                        dve.wait_ge(kv_psum[lane], kv_psum.upto(L0X, 2))
                        tt(v[lane][0:K, 0:D], bank[lane][2][0:K, 0:D], part["L0x", "bv"][0:K, :], ALU.add)\
                            .then_inc(v_ready[lane], 1)
                    for lane in LANES:
                        dve.wait_ge(scores_psum[lane], scores_psum.upto(L0X, 1))
                        link(nc.vector.reduce_max(max_neg[lane][:, 0:1], bank[lane][0][:, 0:K], AX.X))
                        ts(max_neg[lane][:, 0:1], max_neg[lane][:, 0:1], -D ** -0.5, None, ALU.mult)\
                            .then_inc(max_ready[lane], 1)
                    for lane in LANES:
                        dve.wait_ge(probs_ready[lane], probs_ready.upto(L0X, 1))
                        link(nc.vector.reciprocal(row_inv[lane][:, 0:1], row_sum[lane][:, 0:1]))
                    for lane in LANES:
                        dve.wait_ge(x_bias_ready[lane], x_bias_ready.upto(L0X, 1))
                        dve.wait_ge(out_psum[lane], out_psum.upto(L0X, 1))
                        x_done(lane, L0X, nc.vector.scalar_tensor_tensor(
                            x[lane][:, :], bank[lane][3][:, 0:D], row_inv[lane][:, 0:1], x_bias[lane][:, :],
                            ALU.mult, ALU.add))

                    norms(L0F)
                    for lane in LANES:
                        dve.wait_ge(logits_ready[lane], logits_ready.upto(L0F, 1))
                        e1 = route[lane][:, 1, :]
                        link(ts(e1, e1, 1.0, None, ALU.add))
                        link(nc.vector.reciprocal(route[lane][:, 6, :], e1))
                        top2(lane, 16, route[lane][:, 0, :].rearrange("p (g e) -> p g e", e=E))
                        s8 = route[lane][:, 6, :].rearrange("p (g e) -> p g e", e=E)
                        link(tt(route[lane][:, 6, :], route[lane][:, 6, :], route[lane][:, 5, :], ALU.mult))
                        link(nc.vector.tensor_reduce(per_head[lane][:, 1, :], s8, AX.X, ALU.add))
                        link(ts(per_head[lane][:, 1, :], per_head[lane][:, 1, :], 1e-9, None, ALU.max))
                        link(nc.vector.reciprocal(per_head[lane][:, 2, :], per_head[lane][:, 1, :]))
                        link(ts(per_head[lane][:, 2, :], per_head[lane][:, 2, :], part["L0f", "route"], None, ALU.mult))
                        link(tt(gate[lane][:, :].rearrange("p (g e) -> p g e", e=E), s8,
                                per_head[lane][:, 2, :].unsqueeze(2).broadcast_to([128, 16, E]), ALU.mult))
                    for lane in LANES:
                        for half in range(2):
                            dve.wait_ge(scores_psum[lane], scores_psum.upto(L0F, half + 1))
                            link(nc.vector.tensor_reduce(max_neg[lane][:, 4 * half:4 * half + 4],
                                                         bank[lane][2 + half][:, :].rearrange("p (h k) -> p h k", k=S),
                                                         AX.X, ALU.max))
                        ts(max_neg[lane][:, 0:H0F], max_neg[lane][:, 0:H0F], -D ** -0.5, None, ALU.mult)\
                            .then_inc(max_ready[lane], 1)

                    def gated(lane, done, banks_of, h, half, column, to, fresh):
                        for c in range(4):
                            e = 4 * half + c
                            y = banks_of[:, 128 * c:128 * c + 128]
                            g = gate[lane][:, column + E * h + e:column + E * h + e + 1]
                            if fresh and e == 0:
                                ins = ts(to, y, g, None, ALU.mult)
                            else:
                                ins = nc.vector.scalar_tensor_tensor(to, y, g, to, ALU.mult, ALU.add)
                            if c == 3:
                                ins.then_inc(done[lane], 1)
                                dve.wait_ge(done[lane], done.upto(L0F, 2 * h + half + 1))
                            else:
                                link(ins)

                    for h in range(H0F):
                        for lane in LANES:
                            for half in range(2):
                                dve.wait_ge(v_psum[lane], v_psum.upto(L0F, 2 * h + half + 1))
                                gated(lane, v_mixed, bank[lane][2 * (h % 2) + half], h, half, 0,
                                      v[lane][:, 128 * h:128 * h + 128], True)
                    for lane in LANES:
                        dve.wait_ge(probs_ready[lane], probs_ready.upto(L0F, 1))
                        link(nc.vector.reciprocal(row_inv[lane][:, 0:H0F], row_sum[lane][:, 0:H0F]))
                        g_out = gate[lane][:, 64:128].rearrange("p (h e) -> p h e", e=E)
                        link(tt(g_out, g_out, row_inv[lane][:, 0:H0F].unsqueeze(2).broadcast_to([128, H0F, E]), ALU.mult))
                    for h in range(H0F):
                        for lane in LANES:
                            for half in range(2):
                                dve.wait_ge(out_psum[lane], out_psum.upto(L0F, 2 * h + half + 1))
                                gated(lane, out_mixed, bank[lane][2 * (h % 2) + half], h, half, 64, x[lane][:, :], False)

                    norms(L1X)
                    for lane in LANES:
                        dve.wait_ge(kv_psum[lane], kv_psum.upto(L1X, 2))
                        tt(v[lane][0:K, 0:D], bank[lane][2][0:K, 0:D], part["L1x", "bv"][0:K, :], ALU.add)\
                            .then_inc(v_ready[lane], 1)
                    for lane in LANES:
                        dve.wait_ge(masks_ready[lane], 1)
                        for i in range(4):
                            dve.wait_ge(scores_psum[lane], scores_psum.upto(L1X, i + 1))
                            s3 = wide_b[lane][:, 4 * K * i:4 * K * (i + 1)].rearrange("p (h k) -> p h k", k=K)
                            link(tt(s3, bank[lane][i][:, 0:4 * K].rearrange("p (h k) -> p h k", k=K),
                                    mask1[lane][:, :].unsqueeze(1).broadcast_to([128, 4, K]), ALU.add))
                        link(nc.vector.tensor_reduce(max_neg[lane][:, :],
                                                     wide_b[lane][:, 0:H1X * K].rearrange("p (h k) -> p h k", k=K),
                                                     AX.X, ALU.max))
                        ts(max_neg[lane][:, :], max_neg[lane][:, :], -8 ** -0.5, None, ALU.mult).then_inc(max_ready[lane], 1)
                    for lane in LANES:
                        dve.wait_ge(probs_ready[lane], probs_ready.upto(L1X, 1))
                        link(nc.vector.reciprocal(row_inv[lane][:, :], row_sum[lane][:, :]))
                        link(ts(row_inv[lane][:, :], row_inv[lane][:, :], row_ok[lane][:, 1:2], None, ALU.mult))
                    for lane in LANES:
                        dve.wait_ge(mix_psum[lane], mix_psum.upto(L1X, 1))
                        tt(small[lane][:, 256:384].rearrange("p (h c) -> p h c", c=8),
                           bank[lane][0][:, 0:D].rearrange("p (h c) -> p h c", c=8),
                           row_inv[lane][:, :].unsqueeze(2).broadcast_to([128, H1X, 8]), ALU.mult)\
                            .then_inc(mix_scaled[lane], 1)
                    for lane in LANES:
                        dve.wait_ge(x_bias_ready[lane], x_bias_ready.upto(L1X, 1))
                        dve.wait_ge(out_psum[lane], out_psum.upto(L1X, 1))
                        x_done(lane, L1X, tt(x[lane][:, :], bank[lane][2][:, 0:D], x_bias[lane][:, :], ALU.add))

                    norms(L1F)
                    for lane in LANES:
                        dve.wait_ge(hidden_ready[lane], hidden_ready.upto(L1F, 1))
                        link(nc.vector.bn_stats(stats[lane][:, 1, :], wide_b[lane][:, 0:512]))
                        link(nc.vector.bn_aggr(mean_var[lane][:, 1, :], stats[lane][:, 1, :]))
                        ts(var_eps[lane][:, 0:1], mean_var[lane][:, 1, 1:2], 1e-5, None, ALU.add)\
                            .then_inc(var_ready[lane], 1)
                    for lane in LANES:
                        dve.wait_ge(rstd_ready[lane], rstd_ready.upto(L1F, 2))
                        ts(wide_b[lane][:, 512:1024], wide_b[lane][:, 0:512], mean_var[lane][:, 1, 0:1],
                           rstd[lane][:, 0:1], ALU.subtract, ALU.mult).then_inc(hidden_normed[lane], 1)
                    for lane in LANES:
                        dve.wait_ge(hiddenT_psum[lane], hiddenT_psum.upto(L1F, 1))
                        for c in range(4):
                            last = ts(wide_a[lane][:, 128 * c:128 * c + 128], bank[lane][2][:, 128 * c:128 * c + 128],
                                      part["L1f", "lnw"][:, c:c + 1], part["L1f", "lnb"][:, c:c + 1], ALU.mult, ALU.add)
                        last.then_inc(hiddenT_ready[lane], 1)
                    for lane in LANES:
                        add_output(lane, L1F, bank[lane][3][:, 0:D])

                    norms(L2X)
                    for lane in LANES:
                        dve.wait_ge(kv_ready[lane], kv_ready.upto(L2X, 1))
                        dve.wait_ge(q_ready[lane], q_ready.upto(L2X, 1))
                        for h in range(H2X):
                            nc.vector.bn_stats(stats[lane][:, h, :], small[lane][:, 256 + 64 * h:256 + 64 * h + 64])
                            link(nc.vector.bn_stats(stats[lane][0:K, 2 + h, :], v[lane][0:K, 64 * h:64 * h + 64]))
                        for h in range(H2X):
                            nc.vector.bn_aggr(mean_var[lane][:, h, :], stats[lane][:, h, :])
                            link(nc.vector.bn_aggr(mean_var[lane][0:K, 2 + h, :], stats[lane][0:K, 2 + h, :]))
                        ts(var_eps[lane][:, 0:2], mean_var[lane][:, 0:2, 1], 1e-6, None, ALU.add)
                        ts(var_eps[lane][0:K, 2:4], mean_var[lane][0:K, 2:4, 1], 1e-6, None, ALU.add)\
                            .then_inc(var_ready[lane], 1)
                    for lane in LANES:
                        dve.wait_ge(rstd_ready[lane], rstd_ready.upto(L2X, 3))
                        for h in range(H2X):
                            ts(small[lane][:, 64 * h:64 * h + 64], small[lane][:, 256 + 64 * h:256 + 64 * h + 64],
                               mean_var[lane][:, h, 0:1], rstd[lane][:, h:h + 1], ALU.subtract, ALU.mult)
                            last = ts(small[lane][0:K, 128 + 64 * h:128 + 64 * h + 64], v[lane][0:K, 64 * h:64 * h + 64],
                                      mean_var[lane][0:K, 2 + h, 0:1], rstd[lane][0:K, 2 + h:3 + h],
                                      ALU.subtract, ALU.mult)
                        last.then_inc(qk_normed[lane], 1)
                    for lane in LANES:
                        dve.wait_ge(scores_psum[lane], scores_psum.upto(L2X, 1))
                        for h in range(H2X):
                            link(tt(wide_b[lane][:, K * h:K * h + K], bank[lane][h][:, 0:K], mask2[lane][:, :], ALU.add))
                        link(nc.vector.tensor_reduce(max_neg[lane][:, 0:2],
                                                     wide_b[lane][:, 0:2 * K].rearrange("p (h k) -> p h k", k=K),
                                                     AX.X, ALU.max))
                        link(ts(row_ok[lane][:, 2:4], max_neg[lane][:, 0:2], 0.1 * MASKED, None, ALU.is_gt))
                        ts(max_neg[lane][:, 0:2], max_neg[lane][:, 0:2], -64 ** -0.5, None, ALU.mult)\
                            .then_inc(max_ready[lane], 1)
                    for lane in LANES:
                        dve.wait_ge(probs_ready[lane], probs_ready.upto(L2X, 1))
                        link(tt(row_sum[lane][:, 0:2], row_sum[lane][:, 0:2], row_ok[lane][:, 2:4], ALU.mult))
                        link(nc.vector.reciprocal(row_inv[lane][:, 0:2], row_sum[lane][:, 0:2]))
                        for h in range(H2X):
                            p = wide_b[lane][:, K * h:K * h + K]
                            last = ts(p, p, row_ok[lane][:, 2 + h:3 + h], row_inv[lane][:, h:h + 1], ALU.mult, ALU.mult)
                        last.then_inc(probs_normed[lane], 1)
                    for lane in LANES:
                        add_output(lane, L2X, bank[lane][0][:, 0:D])

                    norms(L2F)
                    for lane in LANES:
                        dve.wait_ge(gate_psum[lane], gate_psum.upto(L2F, 1))
                        link(nc.vector.tensor_copy(route[lane][:, 0, 0:E], bank[lane][1][:, 0:E]))
                        nc.vector.tensor_reduce(max_neg[lane][:, 0:1], route[lane][:, 0, 0:E], AX.X, ALU.max, negate=True)\
                            .then_inc(logits_ready[lane], 1)
                    for lane in LANES:
                        top2(lane, 1, route[lane][:, 0, 0:E].unsqueeze(1))
                        dve.wait_ge(gate_exp[lane], gate_exp.upto(L2F, 1))
                        w = route[lane][:, 6, 0:E]
                        link(tt(w, route[lane][:, 1, 0:E], route[lane][:, 5, 0:E], ALU.mult))
                        link(nc.vector.tensor_reduce(per_head[lane][:, 1, 0:1], w, AX.X, ALU.add))
                        link(nc.vector.reciprocal(per_head[lane][:, 2, 0:1], per_head[lane][:, 1, 0:1]))
                        ts(gate[lane][:, 0:E], w, per_head[lane][:, 2, 0:1], None, ALU.mult).then_inc(gate_ready[lane], 1)
                    for lane in LANES:
                        dve.wait_ge(gate_ready[lane], gate_ready.upto(L2F, 1))
                        for e in range(E):
                            if e % 4 == 0:
                                dve.wait_ge(out_psum[lane], out_psum.upto(L2F, e // 4 + 1))
                            link(nc.vector.scalar_tensor_tensor(
                                x[lane][:, :], bank[lane][2 + e // 4][:, 128 * (e % 4):128 * (e % 4) + 128],
                                gate[lane][:, e:e + 1], x[lane][:, :], ALU.mult, ALU.add))
                    for lane in LANES:
                        dve.wait_ge(out_psum[lane], out_psum.upto(L2F, 3))
                        x_done(lane, L2F, tt(x[lane][:, :], bank[lane][1][:, 0:D], x[lane][:, :], ALU.add))

                    norms(L3X)
                    for lane in LANES:
                        for i in range(4):
                            dve.wait_ge(scores_psum[lane], scores_psum.upto(L3X, i + 1))
                            s3 = wide_b[lane][:, 4 * K * i:4 * K * (i + 1)].rearrange("p (h k) -> p h k", k=K)
                            link(nc.vector.scalar_tensor_tensor(
                                s3, bank[lane][i][:, 0:4 * K].rearrange("p (h k) -> p h k", k=K), D ** -0.5,
                                part["L3x", "bias"].unsqueeze(1).broadcast_to([128, 4, K]), ALU.mult, ALU.add))
                        nc.vector.tensor_reduce(max_neg[lane][:, :],
                                                wide_b[lane][:, 0:H3X * K].rearrange("p (h k) -> p h k", k=K),
                                                AX.X, ALU.max, negate=True).then_inc(max_ready[lane], 1)
                    for lane in LANES:
                        dve.wait_ge(probs_ready[lane], probs_ready.upto(L3X, 1))
                        nc.vector.reciprocal(row_inv[lane][:, :], row_sum[lane][:, :]).then_inc(inv_ready[lane], 1)
                    for lane in LANES:
                        add_output(lane, L3X, bank[lane][2][:, 0:D])

                    norms(L3F)
                    for lane in LANES:
                        dve.wait_ge(logits_ready[lane], logits_ready.upto(L3F, 1))
                        r = [route[lane][:, i, 0:E] for i in range(8)]
                        r2 = [route[lane][:, i, 0:E].rearrange("p (g e) -> p g e", g=2) for i in range(8)]
                        h2 = [per_head[lane][:, i, 0:2] for i in range(4)]

                        def both(t):
                            return t.unsqueeze(2).broadcast_to([128, 2, 4])
                        link(ts(r[1], r[1], 1.0, None, ALU.add))
                        link(nc.vector.reciprocal(r[6], r[1]))
                        link(tt(r[0], r[6], part["L3f", "cb"], ALU.add))
                        link(nc.vector.tensor_reduce(h2[0], r2[0], AX.X, ALU.max))
                        link(tt(r2[3], r2[0], both(h2[0]), ALU.is_equal))
                        link(tt(r[3], r[3], part["const", "first"], ALU.mult))
                        link(nc.vector.tensor_reduce(h2[1], r2[3], AX.X, ALU.max))
                        link(tt(r2[4], r2[3], both(h2[1]), ALU.is_equal))
                        link(nc.vector.scalar_tensor_tensor(r[2], r[4], GONE, r[0], ALU.mult, ALU.add))
                        link(nc.vector.tensor_reduce(h2[1], r2[2], AX.X, ALU.max))
                        link(tt(h2[0], h2[0], h2[1], ALU.add))
                        link(tt(h2[3][:, 0:1], h2[0][:, 0:1], h2[0][:, 1:2], ALU.is_ge))
                        link(ts(h2[3][:, 1:2], h2[3][:, 0:1], -1.0, 1.0, ALU.mult, ALU.add))
                        link(tt(r2[0], r2[0], both(h2[3]), ALU.mult))
                        top2(lane, 1, route[lane][:, 0, 0:E].unsqueeze(1))
                        link(tt(r[6], r[6], r[5], ALU.mult))
                        link(nc.vector.tensor_reduce(per_head[lane][:, 1, 0:1], r[6], AX.X, ALU.add))
                        link(ts(per_head[lane][:, 1, 0:1], per_head[lane][:, 1, 0:1], 1e-20, None, ALU.add))
                        link(nc.vector.reciprocal(per_head[lane][:, 2, 0:1], per_head[lane][:, 1, 0:1]))
                        link(ts(gate[lane][:, 0:E], r[6], per_head[lane][:, 2, 0:1], None, ALU.mult))
                    for lane in LANES:
                        dve.wait_ge(expert_psum[lane], expert_psum.upto(L3F, 1))
                        g_all = gate[lane][:, 0:E].rearrange("p (c o) -> p o c", o=2)
                        for odd in range(2):
                            link(tt(wide_b[lane][:, 1024 + 256 * odd:1280 + 256 * odd].rearrange("p (c u) -> p c u", u=64),
                                    bank[lane][2 * odd][:, 0:256].rearrange("p (c u) -> p c u", u=64),
                                    g_all[:, odd, :].unsqueeze(2).broadcast_to([128, 4, 64]), ALU.mult))
                        nc.vector.tensor_reduce(gate[lane][:, 64:128],
                                                wide_b[lane][:, 1024:1536].rearrange("p (e u) -> p u e", u=64),
                                                AX.X, ALU.add).then_inc(expert_mixed[lane], 1)
                    for lane in LANES:
                        add_output(lane, L3F, bank[lane][3][:, 0:D])

            nc.gpsimd.sem_clear(range(numbers[0], numbers[-1] + 1))
            nc.gpsimd.sem_clear(out_stored)
            nc.all_engine_barrier()


def kernel(**inputs):
    import numpy as np
    import concourse.bacc as bacc
    from concourse.bass_utils import run_bass_kernel_spmd

    a = {name: np.asarray(value) for name, value in inputs.items()}

    def rows(vector, n=128):
        return np.broadcast_to(vector[None, :], (n, vector.shape[0]))

    def pad(t):
        return np.concatenate([t, np.zeros((128 - t.shape[0], t.shape[1]), t.dtype)])

    def inner(t):
        return t.reshape(-1, 128, t.shape[1]).transpose(1, 0, 2).reshape(128, -1)

    def stacked(t):
        return t.transpose(1, 0, 2).reshape(128, -1)

    q, k = np.arange(128)[:, None], np.arange(K)[None, :]
    f = np.float32
    parts = {
        "const": [np.eye(128, dtype=f), np.where(k > q, f(MASKED), f(0)), rows(np.arange(K, dtype=f)), q.astype(f),
                  rows(np.arange(E, 0, -1).astype(f)), (q // 8 == np.arange(H1X)[None, :]).astype(f),
                  np.ones((128, 128), f), np.full((128, 4), -0.5, f)],
        "L0x": [a["L0_xattn_Wk"].T, a["L0_xattn_Wv"].T, a["L0_xattn_Wq"].T, a["L0_xattn_Wo"].T,
                a["L0_xattn_bq"][:, None], rows(a["L0_xattn_bv"]), rows(a["L0_xattn_bo"])],
        "L0f": [a["L0_ffn_sel_v_w"].T, a["L0_ffn_sel_o_w"].T, a["L0_ffn_q_w"].T, a["L0_ffn_k_w"].T,
                rows(a["L0_ffn_route_scale"])],
        "L0v": [stacked(a["L0_ffn_v_w"])],
        "L0o": [stacked(a["L0_ffn_o_w"])],
        "L1x": [a["L1_xattn_W_K"], a["L1_xattn_W_V"], a["L1_xattn_W_Q"], a["L1_xattn_W_O"],
                a["L1_xattn_b_Q"][:, None], a["L1_xattn_b_K"][:, None], rows(a["L1_xattn_b_V"]), rows(a["L1_xattn_b_O"])],
        "L1f": [a["L1_ffn_W_fc"].T, inner(a["L1_ffn_W_proj"].T), a["L1_ffn_ln_w"].reshape(4, 128).T,
                a["L1_ffn_ln_b"].reshape(4, 128).T],
        "L2x": [a["L2_xattn_Wkv"], a["L2_xattn_Wq"], a["L2_xattn_Wo"], a["L2_xattn_qn_w"].reshape(128, 1),
                a["L2_xattn_kn_w"].reshape(128, 1)],
        "L2f": [a["L2_ffn_Wg"], stacked(a["L2_ffn_W1"]), a["L2_ffn_b1"].reshape(16, 128).T,
                inner(a["L2_ffn_W2"].reshape(2048, 128)), pad(a["L2_ffn_b2"])],
        "L3x": [a["L3_xattn_Wk"].T, a["L3_xattn_Wv"].T, a["L3_xattn_Wq"].T, inner(a["L3_xattn_Wp"].T),
                a["fside_1x1xSxS2_0"].reshape(S, K)],
        "L3f": [a["L3_ffn_gate"].T, rows(a["L3_ffn_corr_bias"]), a["L3_ffn_fc1_w"].T,
                pad(a["L3_ffn_w1"].transpose(2, 0, 1).reshape(64, 512)),
                a["L3_ffn_w2"].reshape(4, 2, 64, 64).transpose(1, 3, 0, 2).reshape(128, 256),
                pad(a["L3_ffn_fc2_w"].T), a["L3_ffn_up_w"].T, inner(a["L3_ffn_down_w"].T)],
    }
    arrays = {f"in_{name}": np.ascontiguousarray(np.concatenate(ps, axis=1)) for name, ps in parts.items()}
    for name in parts:
        assert arrays[f"in_{name}"].shape == (128, width(name)), (name, arrays[f"in_{name}"].shape)
    arrays["in_x"] = np.ascontiguousarray(a["x"].transpose(1, 0, 2).reshape(S, B * D))
    arrays["in_ctx"] = np.ascontiguousarray(a["ctx_1024"].transpose(2, 0, 1).reshape(D, B * K))
    arrays["in_q_mask"] = np.ascontiguousarray(rows(a["mask_BxS2_if1"].reshape(B * K)))
    arrays["in_k_mask"] = np.ascontiguousarray(rows(a["mask_BxS2_ik0"].reshape(B * K)))
    arrays["in_pair_mask"] = np.ascontiguousarray(a["mask_BxSxS2_bk0"].transpose(1, 0, 2).reshape(S, B * K))

    nc = bacc.Bacc("TRN2", target_bir_lowering=False, num_devices=1)
    d = {name: nc.dram_tensor(name, t.shape, mybir.dt.from_np(t.dtype), kind="ExternalInput").ap()
         for name, t in arrays.items()}
    out = nc.dram_tensor("out_0", (S, B * D), F32, kind="ExternalOutput").ap()
    build(nc, d["in_x"], d["in_ctx"], d["in_q_mask"], d["in_k_mask"], d["in_pair_mask"],
          {name: d[f"in_{name}"] for name in parts}, out)
    r = run_bass_kernel_spmd(nc, [arrays], core_ids=[0])
    return r.results[0]["out_0"].reshape(S, B, D).transpose(1, 0, 2)
```

```python
from contextlib import ExitStack

import concourse.bass as bass
from concourse import mybir

F32 = mybir.dt.float32
ALU = mybir.AluOpType
ACT = mybir.ActivationFunctionType
AX = mybir.AxisListType

B, S, K, D = 8, 128, 120, 128
E = 8
LANES = (0, 1)
L0X, L0F, L1X, L1F, L2X, L2F, L3X, L3F = range(8)
H0F, H1X, H2X, H3X = 8, 16, 2, 16
MASKED = -1e30
GONE = -1e30

PACKS = {
    "const": [("ident", 128), ("causal", K), ("iota_k", K), ("iota_q", 1), ("first", E), ("head_rows", H1X),
              ("ones", 128), ("minus_half", 4)],
    "L0x": [("wk", D), ("wv", D), ("wq", D), ("wo", D), ("bq", 1), ("bv", D), ("bo", D)],
    "L0f": [("sel", 2 * H0F * E), ("qk", 2 * H0F * D), ("route", 1)],
    "L0v": [("v", H0F * E * D)],
    "L0o": [("o", H0F * E * D)],
    "L1x": [("wk", D), ("wv", D), ("wq", D), ("wo", D), ("bq", 1), ("bk", 1), ("bv", D), ("bo", D)],
    "L1f": [("fc", 512), ("proj", 512), ("lnw", 4), ("lnb", 4)],
    "L2x": [("wkv", 2 * D), ("wq", D), ("wo", D), ("qn", 1), ("kn", 1)],
    "L2f": [("wg", E), ("w1", 2048), ("b1", 16), ("w2", 2048), ("b2", D)],
    "L3x": [("wk", 1024), ("wv", 1024), ("wq", 1024), ("wp", 1024), ("bias", K)],
    "L3f": [("gate", E), ("cb", E), ("fc1", 64), ("w1", 512), ("w2", 256), ("fc2", D), ("up", 512), ("down", 512)],
}


def width(pack):
    return sum(n for _, n in PACKS[pack])


def build(nc, x_in, ctx_in, q_mask, k_mask, pair_mask, packs, out):
    with ExitStack() as stack:
        def sb(name, shape, dt=F32):
            return stack.enter_context(nc.sbuf_tensor(name, shape, dt))

        def sem(name):
            return stack.enter_context(nc.semaphore(name))

        class Step:

            def __init__(self, name, per_layer, joint=False):
                self.sems = [sem(name)] * 2 if joint else [sem(f"{name}_{lane}") for lane in LANES]
                self.per_layer = per_layer

            def __getitem__(self, lane):
                return self.sems[lane]

            def upto(self, layer, n):
                assert 1 <= n <= self.per_layer[layer]
                return sum(self.per_layer[:layer]) + n

        part, loaded = {}, {}
        for pack, members in PACKS.items():
            t = sb(f"w_{pack}", [128, width(pack)])
            at = 0
            for name, n in members:
                part[pack, name] = t[:, at:at + n]
                at += n
            part[pack] = t
            loaded[pack] = sem(f"loaded_{pack}")
        inputs_loaded = sem("inputs_loaded")
        masks_loaded = sem("masks_loaded")
        out_stored = sem("out_stored")
        setup_chain = sem("setup_chain")
        abs_summed = sem("abs_summed")
        abs_total = sem("abs_total")
        ident = part["const", "ident"]
        x_all = sb("x_all", [128, B * D])
        ctx_all = sb("ctx_all", [128, B * K])
        qm = sb("qm", [128, B * K], mybir.dt.int32)
        km = sb("km", [128, B * K], mybir.dt.int32)
        pm = sb("pm", [128, B * K], mybir.dt.uint8)
        abs_sum = sb("abs_sum", [128, 2])
        threshold = sb("threshold", [128, 4])

        def lanes(name, shape):
            return [sb(f"{name}_{lane}", shape) for lane in LANES]

        x = lanes("x", [128, D])
        x_bias = lanes("x_bias", [128, D])
        xn = lanes("xn", [128, D])
        xnT = lanes("xnT", [128, D])
        ctxT = lanes("ctxT", [128, K])
        wide_a = lanes("wide_a", [128, 2048])
        wide_b = lanes("wide_b", [128, 2048])
        v = lanes("v", [128, 1024])
        small = lanes("small", [128, 512])
        scaled = [wide_b[lane][:, 1024:1536].rearrange("p (e d) -> p e d", d=D) for lane in LANES]
        pooled = x_bias
        stats = lanes("stats", [128, 4, 6])
        mean_var = lanes("mean_var", [128, 4, 2])
        var_eps = lanes("var_eps", [128, 4])
        rstd = lanes("rstd", [128, 4])
        max_neg = lanes("max_neg", [128, 16])
        row_sum = lanes("row_sum", [128, 16])
        row_inv = lanes("row_inv", [128, 16])
        route = sb("route", [128, 7, 256])
        per_group = sb("per_group", [128, 4, 32])
        gate = sb("gate", [128, 256])
        comb = lanes("comb", [128, 64])
        mask1 = lanes("mask1", [128, K])
        mask2 = lanes("mask2", [128, K])
        lens = lanes("lens", [128, 2])
        row_ok = lanes("row_ok", [128, 4])
        gateT = lanes("gateT", [128, S])
        bank = [[stack.enter_context(nc.psum_tensor(f"bank{lane}{i}", [128, 512], F32)) for i in range(4)]
                for lane in LANES]

        once = [1] * 8
        var_ready = Step("var_ready", [1, 1, 1, 2, 2, 1, 1, 1])
        rstd_ready = Step("rstd_ready", [1, 1, 1, 2, 3, 1, 1, 1])
        xn_ready = Step("xn_ready", once)
        xnT_psum = Step("xnT_psum", once)
        xnT_ready = Step("xnT_ready", once)
        lane_ready = Step("lane_ready", [1] + [0] * 7)
        masks_ready = Step("masks_ready", [0, 0, 1, 0, 0, 0, 0, 0])
        x_bias_ready = Step("x_bias_ready", [1, 0, 1, 0, 0, 0, 0, 0])
        x_ready = Step("x_ready", [1, 1, 1, 1, 1, 1, 1, 1])
        kv_psum = Step("kv_psum", [2, 0, 0, 0, 1, 0, 4, 0])
        kv_ready = Step("kv_ready", [1, 0, 0, 0, 1, 0, 4, 0])
        v_ready = Step("v_ready", [1, 0, 0, 0, 0, 0, 0, 0])
        v_mixed = Step("v_mixed", [0, 2 * H0F, 0, 0, 0, 0, 0, 0])
        scaled_ready = Step("scaled_ready", [0, 2 * H0F, 0, 0, 0, 0, 0, 0])
        v_summed = Step("v_summed", [0, H0F, 0, 0, 0, 0, 0, 0])
        out_summed = Step("out_summed", [0, H0F, 0, 0, 0, 0, 0, 0])
        lens_ready = Step("lens_ready", [1, 0, 0, 0, 0, 0, 0, 0])
        k_blocks = Step("k_blocks", [0, 0, 1, 0, 0, 0, 0, 0])
        q_psum = Step("q_psum", [1, 4, 1, 0, 1, 0, 2, 0])
        q_ready = Step("q_ready", [1, 4, 1, 0, 1, 0, 2, 0])
        qk_normed = Step("qk_normed", [0, 0, 0, 0, 1, 0, 0, 0])
        qkT_psum = Step("qkT_psum", [0, 0, 0, 0, 1, 0, 0, 0])
        qkT_ready = Step("qkT_ready", [0, 0, 0, 0, 1, 0, 0, 0])
        scores_psum = Step("scores_psum", [1, 2, 4, 0, 1, 0, 4, 0])
        max_ready = Step("max_ready", [1, 1, 4, 0, 1, 0, 4, 0])
        probs_ready = Step("probs_ready", [1, 1, 4, 0, 1, 0, 4, 0])
        probs_normed = Step("probs_normed", [0, 0, 0, 0, 1, 0, 4, 0])
        inv_ready = Step("inv_ready", [0, 0, 0, 0, 0, 0, 4, 0])
        pT_psum = Step("pT_psum", [1, 2, 4, 0, 1, 0, 4, 0])
        pT_ready = Step("pT_ready", [1, 2, 4, 0, 1, 0, 4, 0])
        mix_psum = Step("mix_psum", [1, 2, 1, 0, 1, 0, 1, 0])
        mix_scaled = Step("mix_scaled", [0, 0, 1, 0, 0, 0, 0, 0])
        mixT_psum = Step("mixT_psum", [0, 0, 1, 0, 0, 0, 0, 0])
        mixT_ready = Step("mixT_ready", [1, 2, 1, 0, 1, 0, 2, 0])
        out_psum = Step("out_psum", [1, 2 * H0F, 1, 1, 1, 3, 1, 1])
        out_mixed = Step("out_mixed", [0, 2 * H0F, 0, 0, 0, 0, 0, 0])
        gate_psum = Step("gate_psum", [0, 1, 0, 0, 0, 1, 0, 1])
        logits_ready = Step("logits_ready", [0, 1, 0, 0, 0, 0, 0, 1])
        logits_taken = Step("logits_taken", [0, 0, 0, 0, 0, 1, 0, 0], joint=True)
        gate_exp = Step("gate_exp", [0, 0, 0, 0, 0, 1, 0, 0])
        gate_ready = Step("gate_ready", [0, 2, 0, 0, 0, 1, 0, 0], joint=True)
        gateT_psum = Step("gateT_psum", [0, 0, 0, 0, 0, 1, 0, 0])
        gateT_ready = Step("gateT_ready", [0, 0, 0, 0, 0, 1, 0, 0])
        v_psum = Step("v_psum", [0, 2 * H0F, 0, 0, 0, 0, 0, 0])
        hidden_psum = Step("hidden_psum", [0, 0, 0, 1, 0, 4, 0, 3])
        hidden_ready = Step("hidden_ready", [0, 0, 0, 1, 0, 4, 0, 3])
        hidden_normed = Step("hidden_normed", [0, 0, 0, 1, 0, 0, 0, 0])
        hiddenT_psum = Step("hiddenT_psum", [0, 0, 0, 1, 0, 0, 0, 0])
        hiddenT_ready = Step("hiddenT_ready", [0, 0, 0, 1, 0, 0, 0, 0])
        squared = Step("squared", [0, 0, 0, 0, 0, 0, 0, 2])
        expert_psum = Step("expert_psum", [0, 0, 0, 0, 0, 0, 0, 1])
        expert_mixed = Step("expert_mixed", [0, 0, 0, 0, 0, 0, 0, 1])
        expertT_psum = Step("expertT_psum", [0, 0, 0, 0, 0, 0, 0, 1])
        expertT_ready = Step("expertT_ready", [0, 0, 0, 0, 0, 0, 0, 1])
        dve_chain = sem("dve_chain")
        pool_chain = sem("pool_chain")
        turn_sems = [s for st in (
            var_ready, rstd_ready, xn_ready, xnT_psum, xnT_ready, lane_ready, masks_ready, x_bias_ready, x_ready,
            kv_psum, kv_ready, v_ready, v_mixed, scaled_ready, v_summed, out_summed, lens_ready, k_blocks, q_psum, q_ready, qk_normed, qkT_psum, qkT_ready,
            scores_psum, max_ready, probs_ready, probs_normed, inv_ready, pT_psum, pT_ready, mix_psum, mix_scaled,
            mixT_psum, mixT_ready, out_psum, out_mixed, gate_psum, logits_ready, logits_taken, gate_exp, gate_ready, gateT_psum,
            gateT_ready, v_psum, hidden_psum, hidden_ready, hidden_normed, hiddenT_psum, hiddenT_ready, squared,
            expert_psum, expert_mixed, expertT_psum, expertT_ready) for s in dict.fromkeys(st.sems)] + [dve_chain, pool_chain]
        numbers = sorted(s.num for s in turn_sems)
        assert numbers[-1] - numbers[0] + 1 == len(numbers)

        with nc.Block() as block:
            @block.sync
            def _(sp):
                sp.dma_start(part["const"][:, :], packs["const"]).then_inc(loaded["const"], 16)
                sp.dma_start(x_all[:, :], x_in).then_inc(inputs_loaded, 16)
                sp.dma_start(ctx_all[:, :], ctx_in).then_inc(inputs_loaded, 16)
                for pack in ("L0x", "L1x", "L0f", "L0v", "L2x", "L3x"):
                    sp.dma_start(part[pack][:, :], packs[pack]).then_inc(loaded[pack], 16)

            @block.scalar
            def _(act):
                act.dma_start(part["L1f"][:, :], packs["L1f"]).then_inc(loaded["L1f"], 16)
                act.dma_start(qm[:, :], q_mask).then_inc(masks_loaded, 16)
                act.dma_start(km[:, :], k_mask).then_inc(masks_loaded, 16)
                act.dma_start(pm[:, :], pair_mask).then_inc(masks_loaded, 16)
                for pack in ("L0o", "L2f", "L3f"):
                    act.dma_start(part[pack][:, :], packs[pack]).then_inc(loaded[pack], 16)

            @block.vector
            def _(dve):
                chain = [0]

                def link(ins):
                    chain[0] += 1
                    ins.then_inc(setup_chain, 1)
                    dve.wait_ge(setup_chain, chain[0])

                dve.wait_ge(loaded["L1f"], 16)
                for i, name in enumerate(("fc", "proj")):
                    last = nc.vector.tensor_reduce(abs_sum[:, i:i + 1], part["L1f", name], AX.X, ALU.add,
                                                   apply_absolute_value=True)
                last.then_inc(abs_summed, 1)
                dve.wait_ge(abs_total, 1)
                link(nc.vector.tensor_scalar(threshold[:, 0:2], bank[0][0][:, 0:2], 1.0 / (512 * D), 1e-6, ALU.mult, ALU.add))
                link(nc.vector.tensor_scalar(threshold[:, 2:4], threshold[:, 0:2], -0.5, None, ALU.mult))
                link(nc.vector.tensor_scalar(threshold[:, 0:2], threshold[:, 0:2], 0.5, None, ALU.mult))
                for i, name in enumerate(("fc", "proj")):
                    w = part["L1f", name]
                    below = wide_b[0][:, 512 * i:512 * (i + 1)]
                    link(nc.vector.tensor_scalar(below, w, threshold[:, 2 + i:3 + i], None, ALU.is_lt))
                    link(nc.vector.tensor_scalar(w, w, threshold[:, i:i + 1], None, ALU.is_gt))
                    link(nc.vector.tensor_tensor(w, w, below, ALU.subtract))

            @block.tensor
            def _(pe):
                pe.wait_ge(loaded["const"], 16)
                pe.wait_ge(abs_summed, 1)
                nc.tensor.matmul(bank[0][0][:, 0:2], part["const", "ones"], abs_sum[:, :],
                                 start=True, stop=True).then_inc(abs_total, 1)

        with nc.Fori(0, B // len(LANES)) as turn:
            b = turn * len(LANES)
            with nc.Block() as block:
                @block.sync
                def _(sp):
                    for lane in LANES:
                        sp.wait_ge(x_ready[lane], x_ready.upto(L3F, 1))
                        cols = bass.ds((b + lane) * D, D)
                        sp.dma_start(out[:, cols], x_all[:, cols]).then_inc(out_stored, 16)

                @block.tensor
                def _(pe):
                    def mm(o, lhsT, rhs, first=True, last=True):
                        return nc.tensor.matmul(o, lhsT, rhs, start=first, stop=last)

                    def turn_x(lane, layer):
                        pe.wait_ge(xn_ready[lane], xn_ready.upto(layer, 1))
                        nc.tensor.transpose(bank[lane][0][:, 0:S], xn[lane][:, :], ident)\
                            .then_inc(xnT_psum[lane], 1)

                    def in_turn(banks, behind, first, then):
                        steps = [(i, lane) for i in range(banks) for lane in LANES]
                        for n in range(len(steps) + behind):
                            if n < len(steps):
                                first(*steps[n])
                            if n >= behind:
                                then(*steps[n - behind])

                    def transpose_probs(ready, layer):
                        def step(i, lane):
                            pe.wait_ge(ready[lane], ready.upto(layer, i + 1))
                            for c in range(4):
                                h = 4 * i + c
                                last = nc.tensor.transpose(bank[lane][i][0:K, 128 * c:128 * c + 128],
                                                           wide_b[lane][:, K * h:K * h + K], ident)
                            last.then_inc(pT_psum[lane], 1)
                        return step

                    pe.wait_ge(loaded["L0x"], 16)
                    pe.wait_ge(loaded["L1x"], 16)
                    for lane in LANES:
                        pe.wait_ge(lane_ready[lane], 1)
                        mm(bank[lane][1][:, 0:K], part["L0x", "wk"], ctxT[lane][:, :])
                        mm(bank[lane][1][:, 128:128 + K], part["L1x", "wk"], ctxT[lane][:, :]).then_inc(kv_psum[lane], 1)
                        mm(bank[lane][2][0:K, 0:D], ctxT[lane][:, :], part["L0x", "wv"])
                        mm(bank[lane][2][0:K, D:2 * D], ctxT[lane][:, :], part["L1x", "wv"]).then_inc(kv_psum[lane], 1)
                        turn_x(lane, L0X)
                    for lane in LANES:
                        pe.wait_ge(xnT_ready[lane], xnT_ready.upto(L0X, 1))
                        mm(bank[lane][3][:, 0:S], part["L0x", "wq"], xnT[lane][:, :]).then_inc(q_psum[lane], 1)
                    for lane in LANES:
                        pe.wait_ge(kv_ready[lane], kv_ready.upto(L0X, 1))
                        pe.wait_ge(q_ready[lane], q_ready.upto(L0X, 1))
                        mm(bank[lane][0][:, 0:K], wide_a[lane][:, 0:S], wide_a[lane][:, 1024:1024 + K])\
                            .then_inc(scores_psum[lane], 1)
                    for lane in LANES:
                        pe.wait_ge(probs_ready[lane], probs_ready.upto(L0X, 1))
                        nc.tensor.transpose(bank[lane][1][0:K, 0:S], wide_b[lane][:, 0:K], ident)\
                            .then_inc(pT_psum[lane], 1)
                    for lane in LANES:
                        pe.wait_ge(v_ready[lane], v_ready.upto(L0X, 1))
                        pe.wait_ge(pT_ready[lane], pT_ready.upto(L0X, 1))
                        mm(bank[lane][2][:, 0:S], v[lane][0:K, 0:D], wide_a[lane][0:K, 0:S]).then_inc(mix_psum[lane], 1)
                    for lane in LANES:
                        pe.wait_ge(mixT_ready[lane], mixT_ready.upto(L0X, 1))
                        mm(bank[lane][3][:, 0:D], wide_b[lane][:, 0:S], part["L0x", "wo"]).then_inc(out_psum[lane], 1)

                    pe.wait_ge(loaded["L0f"], 16)
                    for lane in LANES:
                        turn_x(lane, L0F)
                    for lane in LANES:
                        pe.wait_ge(xnT_ready[lane], xnT_ready.upto(L0F, 1))
                        mm(bank[lane][1][:, 0:128], xnT[lane][:, :], part["L0f", "sel"]).then_inc(gate_psum[lane], 1)
                    for lane in LANES:
                        for i, b_to in enumerate((2, 3, 0, 1)):
                            if b_to == 1:
                                pe.wait_ge(logits_ready[lane], logits_ready.upto(L0F, 1))
                            for c in range(4):
                                at = 512 * i + 128 * c
                                last = mm(bank[lane][b_to][:, 128 * c:128 * c + 128],
                                          part["L0f", "qk"][:, at:at + 128], xnT[lane][:, :])
                            last.then_inc(q_psum[lane], 1)
                    for lane in LANES:
                        pe.wait_ge(q_ready[lane], q_ready.upto(L0F, 4))
                        for h in range(H0F):
                            last = mm(bank[lane][2 + h // 4][:, 128 * (h % 4):128 * (h % 4) + 128],
                                      wide_a[lane][:, 128 * h:128 * h + 128],
                                      wide_a[lane][:, 1024 + 128 * h:1024 + 128 * h + 128])
                            if h % 4 == 3:
                                last.then_inc(scores_psum[lane], 1)
                    pe.wait_ge(loaded["L0v"], 16)
                    for h in range(H0F):
                        for half in range(2):
                            for lane in LANES:
                                if h == 1 and half == 0:
                                    pe.wait_ge(probs_ready[lane], probs_ready.upto(L0F, 1))
                                if h >= 2:
                                    pe.wait_ge(v_mixed[lane], v_mixed.upto(L0F, 2 * (h - 2) + half + 1))
                                at = (2 * h + half) * 512
                                mm(bank[lane][2 * (h % 2) + half][:, :], xnT[lane][:, :],
                                   part["L0v", "v"][:, at:at + 512]).then_inc(v_psum[lane], 1)
                    for lane in LANES:
                        for half in range(2):
                            pe.wait_ge(v_mixed[lane], v_mixed.upto(L0F, 2 * (H0F - 2) + half + 1))
                            for c in range(4):
                                h = 4 * half + c
                                last = nc.tensor.transpose(bank[lane][half][:, 128 * c:128 * c + 128],
                                                           wide_b[lane][:, 128 * h:128 * h + 128], ident)
                            last.then_inc(pT_psum[lane], 1)
                    for lane in LANES:
                        for half in range(2):
                            pe.wait_ge(pT_ready[lane], pT_ready.upto(L0F, half + 1))
                            pe.wait_ge(v_mixed[lane], v_mixed.upto(L0F, 2 * H0F))
                            pe.wait_ge(v_summed[lane], v_summed.upto(L0F, 4 * half + 4))
                            for c in range(4):
                                h = 4 * half + c
                                last = mm(bank[lane][2 + half][:, 128 * c:128 * c + 128],
                                          v[lane][:, 128 * h:128 * h + 128], wide_a[lane][:, 128 * h:128 * h + 128])
                            last.then_inc(mix_psum[lane], 1)
                    pe.wait_ge(loaded["L0o"], 16)
                    for h in range(H0F):
                        for half in range(2):
                            for lane in LANES:
                                if h in (0, 1) and half == 0:
                                    pe.wait_ge(mixT_ready[lane], mixT_ready.upto(L0F, h + 1))
                                if h >= 2:
                                    pe.wait_ge(out_mixed[lane], out_mixed.upto(L0F, 2 * (h - 2) + half + 1))
                                at = (2 * h + half) * 512
                                mm(bank[lane][2 * (h % 2) + half][:, :], wide_b[lane][:, 128 * h:128 * h + 128],
                                   part["L0o", "o"][:, at:at + 512]).then_inc(out_psum[lane], 1)

                    for lane in LANES:
                        pe.wait_ge(out_mixed[lane], out_mixed.upto(L0F, 2 * H0F))
                        turn_x(lane, L1X)
                    for lane in LANES:
                        pe.wait_ge(xnT_ready[lane], xnT_ready.upto(L1X, 1))
                        mm(bank[lane][3][:, 0:S], part["L1x", "wq"], xnT[lane][:, :]).then_inc(q_psum[lane], 1)
                    for lane in LANES:
                        pe.wait_ge(q_ready[lane], q_ready.upto(L1X, 1))
                        pe.wait_ge(k_blocks[lane], k_blocks.upto(L1X, 1))
                    for i in range(4):
                        for lane in LANES:
                            mm(bank[lane][i][:, 0:4 * K], small[lane][:, 0:S],
                               wide_a[lane][:, 4 * K * i:4 * K * (i + 1)]).then_inc(scores_psum[lane], 1)

                    def mix_l1(i, lane):
                        pe.wait_ge(pT_ready[lane], pT_ready.upto(L1X, i + 1))
                        for h in range(4 * i, 4 * i + 4):
                            last = mm(bank[lane][0][:, 8 * h:8 * h + 8], wide_a[lane][0:K, 128 * h:128 * h + 128],
                                      small[lane][0:K, 384 + 8 * h:392 + 8 * h])
                        if i == 3:
                            last.then_inc(mix_psum[lane], 1)
                    in_turn(4, 3, transpose_probs(probs_ready, L1X), mix_l1)
                    for lane in LANES:
                        pe.wait_ge(mix_scaled[lane], mix_scaled.upto(L1X, 1))
                        nc.tensor.transpose(bank[lane][1][:, 0:S], small[lane][:, 256:384], ident)\
                            .then_inc(mixT_psum[lane], 1)
                    for lane in LANES:
                        pe.wait_ge(mixT_ready[lane], mixT_ready.upto(L1X, 1))
                        mm(bank[lane][2][:, 0:D], wide_b[lane][:, 0:S], part["L1x", "wo"]).then_inc(out_psum[lane], 1)

                    for lane in LANES:
                        turn_x(lane, L1F)
                    for lane in LANES:
                        pe.wait_ge(xnT_ready[lane], xnT_ready.upto(L1F, 1))
                        mm(bank[lane][1][:, :], xnT[lane][:, :], part["L1f", "fc"]).then_inc(hidden_psum[lane], 1)
                    for lane in LANES:
                        pe.wait_ge(hidden_normed[lane], hidden_normed.upto(L1F, 1))
                        for c in range(4):
                            last = nc.tensor.transpose(bank[lane][2][:, 128 * c:128 * c + 128],
                                                       wide_b[lane][:, 512 + 128 * c:512 + 128 * c + 128], ident)
                        last.then_inc(hiddenT_psum[lane], 1)
                    for lane in LANES:
                        pe.wait_ge(hiddenT_ready[lane], hiddenT_ready.upto(L1F, 1))
                        for c in range(4):
                            last = mm(bank[lane][3][:, 0:D], wide_a[lane][:, 128 * c:128 * c + 128],
                                      part["L1f", "proj"][:, 128 * c:128 * c + 128], c == 0, c == 3)
                        last.then_inc(out_psum[lane], 1)

                    pe.wait_ge(loaded["L2x"], 16)
                    for lane in LANES:
                        mm(bank[lane][1][0:K, 0:2 * D], ctxT[lane][:, :], part["L2x", "wkv"]).then_inc(kv_psum[lane], 1)
                    for lane in LANES:
                        turn_x(lane, L2X)
                    for lane in LANES:
                        pe.wait_ge(xnT_ready[lane], xnT_ready.upto(L2X, 1))
                        mm(bank[lane][2][:, 0:D], xnT[lane][:, :], part["L2x", "wq"]).then_inc(q_psum[lane], 1)
                    for lane in LANES:
                        pe.wait_ge(qk_normed[lane], qk_normed.upto(L2X, 1))
                        nc.tensor.transpose(bank[lane][3][:, 0:S], small[lane][:, 0:D], ident)
                        nc.tensor.transpose(bank[lane][3][:, S:S + K], small[lane][0:K, D:2 * D], ident[0:K, 0:K])\
                            .then_inc(qkT_psum[lane], 1)
                    for lane in LANES:
                        pe.wait_ge(qkT_ready[lane], qkT_ready.upto(L2X, 1))
                        for h in range(H2X):
                            r = slice(64 * h, 64 * h + 64)
                            last = mm(bank[lane][h][:, 0:K], wide_a[lane][r, 0:S], wide_a[lane][r, S:S + K])
                        last.then_inc(scores_psum[lane], 1)
                    for lane in LANES:
                        pe.wait_ge(probs_normed[lane], probs_normed.upto(L2X, 1))
                        for h in range(H2X):
                            last = nc.tensor.transpose(bank[lane][2][0:K, 128 * h:128 * h + 128],
                                                       wide_b[lane][:, K * h:K * h + K], ident)
                        last.then_inc(pT_psum[lane], 1)
                    for lane in LANES:
                        pe.wait_ge(pT_ready[lane], pT_ready.upto(L2X, 1))
                        for h in range(H2X):
                            r = slice(64 * h, 64 * h + 64)
                            last = mm(bank[lane][3][r, 0:S], v[lane][0:K, D + 64 * h:D + 64 * h + 64],
                                      wide_a[lane][0:K, 256 + 128 * h:256 + 128 * h + 128])
                        last.then_inc(mix_psum[lane], 1)
                    for lane in LANES:
                        pe.wait_ge(mixT_ready[lane], mixT_ready.upto(L2X, 1))
                        mm(bank[lane][0][:, 0:D], wide_b[lane][:, 0:S], part["L2x", "wo"]).then_inc(out_psum[lane], 1)

                    pe.wait_ge(loaded["L2f"], 16)
                    for lane in LANES:
                        turn_x(lane, L2F)
                    for lane in LANES:
                        pe.wait_ge(xnT_ready[lane], xnT_ready.upto(L2F, 1))
                        mm(bank[lane][1][:, 0:E], xnT[lane][:, :], part["L2f", "wg"]).then_inc(gate_psum[lane], 1)
                    for lane in LANES:
                        for i, b_to in enumerate((2, 3, 0, 1)):
                            if b_to == 1:
                                pe.wait_ge(logits_taken[lane], logits_taken.upto(L2F, 1))
                            for c in range(4):
                                at = 512 * i + 128 * c
                                last = mm(bank[lane][b_to][:, 128 * c:128 * c + 128],
                                          part["L2f", "w1"][:, at:at + 128], xnT[lane][:, :])
                            last.then_inc(hidden_psum[lane], 1)
                    for lane in LANES:
                        for e in range(E):
                            if e % 2 == 0:
                                pe.wait_ge(hidden_ready[lane], hidden_ready.upto(L2F, e // 2 + 1))
                            for c in range(2):
                                at = 256 * e + 128 * c
                                last = mm(bank[lane][2 + e // 4][:, 128 * (e % 4):128 * (e % 4) + 128],
                                          wide_a[lane][:, at:at + 128], part["L2f", "w2"][:, at:at + 128],
                                          c == 0, c == 1)
                            if e % 4 == 3:
                                last.then_inc(out_psum[lane], 1)
                    for lane in LANES:
                        pe.wait_ge(gate_ready[lane], gate_ready.upto(L2F, 1))
                        nc.tensor.transpose(bank[lane][0][0:E, 0:S], gate[:, E * lane:E * lane + E], ident)\
                            .then_inc(gateT_psum[lane], 1)
                    for lane in LANES:
                        pe.wait_ge(gateT_ready[lane], gateT_ready.upto(L2F, 1))
                        mm(bank[lane][1][:, 0:D], gateT[lane][0:E, :], part["L2f", "b2"][0:E, :])\
                            .then_inc(out_psum[lane], 1)

                    pe.wait_ge(loaded["L3x"], 16)
                    for lane in LANES:
                        pe.wait_ge(x_ready[lane], x_ready.upto(L2F, 1))
                        for half in range(2):
                            for c in range(4):
                                at = 512 * half + 128 * c
                                last = mm(bank[lane][1 + half][:, 128 * c:128 * c + K],
                                          part["L3x", "wk"][:, at:at + 128], ctxT[lane][:, :])
                            last.then_inc(kv_psum[lane], 1)
                        mm(bank[lane][3][0:K, :], ctxT[lane][:, :], part["L3x", "wv"][:, 0:512])\
                            .then_inc(kv_psum[lane], 1)
                    for lane in LANES:
                        turn_x(lane, L3X)
                        pe.wait_ge(kv_ready[lane], kv_ready.upto(L3X, 1))
                        mm(bank[lane][1][0:K, :], ctxT[lane][:, :], part["L3x", "wv"][:, 512:1024])\
                            .then_inc(kv_psum[lane], 1)
                    for lane in LANES:
                        pe.wait_ge(xnT_ready[lane], xnT_ready.upto(L3X, 1))
                        for half in range(2):
                            pe.wait_ge(kv_ready[lane], kv_ready.upto(L3X, half + 2))
                            for c in range(4):
                                at = 512 * half + 128 * c
                                last = mm(bank[lane][2 + half][:, 128 * c:128 * c + 128],
                                          part["L3x", "wq"][:, at:at + 128], xnT[lane][:, :])
                            last.then_inc(q_psum[lane], 1)
                    for lane in LANES:
                        pe.wait_ge(kv_ready[lane], kv_ready.upto(L3X, 4))
                        pe.wait_ge(q_ready[lane], q_ready.upto(L3X, 2))
                    for i in range(4):
                        for lane in LANES:
                            for c in range(4):
                                odd, chunk = i // 2, 4 * (i % 2) + c
                                r = slice(64 * odd, 64 * odd + 64)
                                last = mm(bank[lane][i][:, K * c:K * c + K],
                                          wide_a[lane][r, 128 * chunk:128 * chunk + 128],
                                          wide_a[lane][r, 1024 + 128 * chunk:1024 + 128 * chunk + K])
                            last.then_inc(scores_psum[lane], 1)

                    def mix_l3(i, lane):
                        pe.wait_ge(pT_ready[lane], pT_ready.upto(L3X, i + 1))
                        for c in range(4):
                            odd, chunk = i // 2, 4 * (i % 2) + c
                            h = 2 * chunk + odd
                            last = mm(bank[lane][i % 2][64 * odd:64 * odd + 64, 128 * c:128 * c + 128],
                                      v[lane][0:K, 64 * h:64 * h + 64],
                                      wide_a[lane][0:K, 128 * (4 * i + c):128 * (4 * i + c) + 128])
                        if i == 3:
                            last.then_inc(mix_psum[lane], 1)
                    in_turn(4, 4, transpose_probs(probs_normed, L3X), mix_l3)
                    for lane in LANES:
                        for c in range(8):
                            if c % 4 == 0:
                                pe.wait_ge(mixT_ready[lane], mixT_ready.upto(L3X, c // 4 + 1))
                            last = mm(bank[lane][2][:, 0:D], wide_b[lane][:, 128 * c:128 * c + 128],
                                      part["L3x", "wp"][:, 128 * c:128 * c + 128], c == 0, c == 7)
                        last.then_inc(out_psum[lane], 1)

                    pe.wait_ge(loaded["L3f"], 16)
                    for lane in LANES:
                        turn_x(lane, L3F)
                    for lane in LANES:
                        pe.wait_ge(xnT_ready[lane], xnT_ready.upto(L3F, 1))
                        mm(bank[lane][1][:, 0:E], xnT[lane][:, :], part["L3f", "gate"]).then_inc(gate_psum[lane], 1)
                    for lane in LANES:
                        mm(bank[lane][2][0:64, 0:S], part["L3f", "fc1"], xnT[lane][:, :]).then_inc(hidden_psum[lane], 1)
                        for c in range(4):
                            last = mm(bank[lane][3][:, 128 * c:128 * c + 128],
                                      part["L3f", "up"][:, 128 * c:128 * c + 128], xnT[lane][:, :])
                        last.then_inc(hidden_psum[lane], 1)
                    for lane in LANES:
                        pe.wait_ge(hidden_ready[lane], hidden_ready.upto(L3F, 1))
                        pe.wait_ge(logits_ready[lane], logits_ready.upto(L3F, 1))
                        for p in range(4):
                            last = mm(bank[lane][1][:, 128 * p:128 * p + 128],
                                      part["L3f", "w1"][0:64, 128 * p:128 * p + 128], small[lane][0:64, 0:S])
                        last.then_inc(hidden_psum[lane], 1)
                    for lane in LANES:
                        pe.wait_ge(squared[lane], squared.upto(L3F, 2))
                        for odd in range(2):
                            r = slice(64 * odd, 64 * odd + 64)
                            for p in range(4):
                                last = mm(bank[lane][2 * odd][:, 64 * p:64 * p + 64],
                                          wide_a[lane][r, 512 + 128 * p:512 + 128 * p + 128],
                                          part["L3f", "w2"][r, 64 * p:64 * p + 64])
                        last.then_inc(expert_psum[lane], 1)
                    for lane in LANES:
                        for c in range(4):
                            mm(bank[lane][3][:, 0:D], wide_a[lane][:, 128 * c:128 * c + 128],
                               part["L3f", "down"][:, 128 * c:128 * c + 128], c == 0, False)
                    for lane in LANES:
                        pe.wait_ge(expert_mixed[lane], expert_mixed.upto(L3F, 1))
                        nc.tensor.transpose(bank[lane][1][0:64, 0:S], comb[lane][:, :], ident)\
                            .then_inc(expertT_psum[lane], 1)
                    for lane in LANES:
                        pe.wait_ge(expertT_ready[lane], expertT_ready.upto(L3F, 1))
                        mm(bank[lane][3][:, 0:D], gateT[lane][0:64, :], part["L3f", "fc2"][0:64, :], False, True)\
                            .then_inc(out_psum[lane], 1)

                @block.scalar
                def _(act):
                    def copy(o, i, bias=0.0, scale=1.0):
                        return nc.scalar.activation(o, i, ACT.Identity, bias=bias, scale=scale)

                    def take_xT(lane, layer):
                        act.wait_ge(xnT_psum[lane], xnT_psum.upto(layer, 1))
                        copy(xnT[lane][:, :], bank[lane][0][:, 0:S]).then_inc(xnT_ready[lane], 1)

                    def exponentials(lane, layer, heads, scores, cols, scale, n=1):
                        act.wait_ge(max_ready[lane], max_ready.upto(layer, n))
                        for h in heads:
                            last = nc.scalar.activation(wide_b[lane][:, cols * h:cols * h + cols], scores(lane, h), ACT.Exp,
                                                        bias=max_neg[lane][:, h:h + 1], scale=scale,
                                                        accum_out=row_sum[lane][:, h:h + 1])
                        last.then_inc(probs_ready[lane], 1)

                    for lane in LANES:
                        act.wait_ge(kv_psum[lane], kv_psum.upto(L0X, 1))
                        copy(small[lane][:, 128:128 + K], bank[lane][1][:, 128:128 + K], bias=part["L1x", "bk"])
                        copy(wide_a[lane][:, 1024:1024 + K], bank[lane][1][:, 0:K]).then_inc(kv_ready[lane], 1)
                        take_xT(lane, L0X)
                    for lane in LANES:
                        act.wait_ge(q_psum[lane], q_psum.upto(L0X, 1))
                        copy(wide_a[lane][:, 0:S], bank[lane][3][:, 0:S], bias=part["L0x", "bq"]).then_inc(q_ready[lane], 1)
                    for lane in LANES:
                        exponentials(lane, L0X, [0], lambda n, h: bank[n][0][:, 0:K], K, D ** -0.5)
                    for lane in LANES:
                        act.wait_ge(pT_psum[lane], pT_psum.upto(L0X, 1))
                        copy(wide_a[lane][0:K, 0:S], bank[lane][1][0:K, 0:S]).then_inc(pT_ready[lane], 1)
                    for lane in LANES:
                        act.wait_ge(mix_psum[lane], mix_psum.upto(L0X, 1))
                        copy(wide_b[lane][:, 0:S], bank[lane][2][:, 0:S]).then_inc(mixT_ready[lane], 1)

                    for lane in LANES:
                        take_xT(lane, L0F)
                    for lane in LANES:
                        act.wait_ge(gate_psum[lane], gate_psum.upto(L0F, 1))
                        logits = bank[lane][1][:, 0:128].rearrange("p (t c) -> p t c", t=2)

                        def mine(i):
                            return route[:, i, :].rearrange("p (t n c) -> p n t c", t=2, n=2)[:, lane]
                        nc.scalar.activation(mine(1), logits, ACT.Exp, scale=-1.0)
                        copy(mine(0), logits).then_inc(logits_ready[lane], 1)
                    for lane in LANES:
                        for i, b_to in enumerate((2, 3, 0, 1)):
                            act.wait_ge(q_psum[lane], q_psum.upto(L0F, i + 1))
                            copy(wide_a[lane][:, 512 * i:512 * i + 512], bank[lane][b_to][:, :]).then_inc(q_ready[lane], 1)
                    for lane in LANES:
                        exponentials(lane, L0F, range(H0F),
                                     lambda n, h: bank[n][2 + h // 4][:, 128 * (h % 4):128 * (h % 4) + 128], S, D ** -0.5)

                    def scale_experts(h, psum, column, first):
                        for lane in LANES:
                            act.wait_ge(psum[lane], psum.upto(L0F, 2 * h + 2))
                            if not first or h >= 2:
                                done = v_summed if first else out_summed
                                if not first and h < 2:
                                    act.wait_ge(v_summed[lane], v_summed.upto(L0F, H0F - 1 + h))
                                else:
                                    act.wait_ge(done[lane], done.upto(L0F, h - 1))
                            for e in (6, 7):
                                g = column + 64 * lane + E * h + e
                                last = nc.scalar.activation(scaled[lane][:, 2 * (h % 2) + e - 6, :],
                                                            bank[lane][2 * (h % 2) + 1][:, 128 * (e - 4):128 * (e - 4) + 128],
                                                            ACT.Copy, scale=gate[:, g:g + 1])
                            last.then_inc(scaled_ready[lane], 1)
                    act.wait_ge(gate_ready[0], gate_ready.upto(L0F, 1))
                    for h in range(H0F):
                        scale_experts(h, v_psum, 0, True)
                    for lane in LANES:
                        for half in range(2):
                            act.wait_ge(pT_psum[lane], pT_psum.upto(L0F, half + 1))
                            copy(wide_a[lane][:, 512 * half:512 * half + 512], bank[lane][half][:, :])\
                                .then_inc(pT_ready[lane], 1)
                    for lane in LANES:
                        for half in range(2):
                            act.wait_ge(mix_psum[lane], mix_psum.upto(L0F, half + 1))
                            copy(wide_b[lane][:, 512 * half:512 * half + 512], bank[lane][2 + half][:, :])\
                                .then_inc(mixT_ready[lane], 1)

                    act.wait_ge(gate_ready[0], gate_ready.upto(L0F, 2))
                    for h in range(H0F):
                        scale_experts(h, out_psum, 128, False)

                    for lane in LANES:
                        take_xT(lane, L1X)
                    for lane in LANES:
                        act.wait_ge(q_psum[lane], q_psum.upto(L1X, 1))
                        copy(small[lane][:, 0:S], bank[lane][3][:, 0:S], bias=part["L1x", "bq"]).then_inc(q_ready[lane], 1)
                    for i in range(4):
                        for lane in LANES:
                            exponentials(lane, L1X, range(4 * i, 4 * i + 4), lambda n, h: wide_b[n][:, K * h:K * h + K],
                                         K, 1.0, i + 1)
                    for lane in LANES:
                        act.wait_ge(mixT_psum[lane], mixT_psum.upto(L1X, 1))
                        copy(wide_b[lane][:, 0:S], bank[lane][1][:, 0:S]).then_inc(mixT_ready[lane], 1)

                    for lane in LANES:
                        take_xT(lane, L1F)
                    for lane in LANES:
                        act.wait_ge(hidden_psum[lane], hidden_psum.upto(L1F, 1))
                        nc.scalar.activation(wide_b[lane][:, 0:512], bank[lane][1][:, :], ACT.Gelu)\
                            .then_inc(hidden_ready[lane], 1)

                    for lane in LANES:
                        act.wait_ge(kv_psum[lane], kv_psum.upto(L2X, 1))
                        copy(v[lane][0:K, 0:2 * D], bank[lane][1][0:K, 0:2 * D]).then_inc(kv_ready[lane], 1)
                    for lane in LANES:
                        take_xT(lane, L2X)
                    for lane in LANES:
                        act.wait_ge(q_psum[lane], q_psum.upto(L2X, 1))
                        copy(small[lane][:, 256:256 + D], bank[lane][2][:, 0:D]).then_inc(q_ready[lane], 1)
                    for lane in LANES:
                        act.wait_ge(qkT_psum[lane], qkT_psum.upto(L2X, 1))
                        copy(wide_a[lane][:, 0:S], bank[lane][3][:, 0:S], scale=part["L2x", "qn"])
                        copy(wide_a[lane][:, S:S + K], bank[lane][3][:, S:S + K], scale=part["L2x", "kn"])\
                            .then_inc(qkT_ready[lane], 1)
                    for lane in LANES:
                        exponentials(lane, L2X, range(H2X), lambda n, h: wide_b[n][:, K * h:K * h + K], K, 64 ** -0.5)
                    for lane in LANES:
                        act.wait_ge(pT_psum[lane], pT_psum.upto(L2X, 1))
                        copy(wide_a[lane][0:K, 256:512], bank[lane][2][0:K, 0:256]).then_inc(pT_ready[lane], 1)
                    for lane in LANES:
                        act.wait_ge(mix_psum[lane], mix_psum.upto(L2X, 1))
                        copy(wide_b[lane][:, 0:S], bank[lane][3][:, 0:S]).then_inc(mixT_ready[lane], 1)

                    for lane in LANES:
                        take_xT(lane, L2F)
                    for lane in LANES:
                        act.wait_ge(logits_taken[lane], logits_taken.upto(L2F, 1))
                        nc.scalar.activation(route[:, 1, E * lane:E * lane + E], route[:, 0, E * lane:E * lane + E], ACT.Exp,
                                             bias=per_group[:, 3, lane:lane + 1]).then_inc(gate_exp[lane], 1)
                    for lane in LANES:
                        for i, b_to in enumerate((2, 3, 0, 1)):
                            act.wait_ge(hidden_psum[lane], hidden_psum.upto(L2F, i + 1))
                            for c in range(4):
                                j = 4 * i + c
                                last = nc.scalar.activation(wide_a[lane][:, 128 * j:128 * j + 128],
                                                            bank[lane][b_to][:, 128 * c:128 * c + 128], ACT.Gelu,
                                                            bias=part["L2f", "b1"][:, j:j + 1])
                            last.then_inc(hidden_ready[lane], 1)
                    for lane in LANES:
                        act.wait_ge(gateT_psum[lane], gateT_psum.upto(L2F, 1))
                        copy(gateT[lane][0:E, :], bank[lane][0][0:E, 0:S]).then_inc(gateT_ready[lane], 1)

                    for lane in LANES:
                        for half in range(2):
                            act.wait_ge(kv_psum[lane], kv_psum.upto(L3X, half + 1))
                            copy(wide_a[lane][:, 1024 + 512 * half:1536 + 512 * half].rearrange("p (c k) -> p c k", c=4)[:, :, 0:K],
                                 bank[lane][1 + half][:, :].rearrange("p (c k) -> p c k", c=4)[:, :, 0:K])\
                                .then_inc(kv_ready[lane], 1)
                        act.wait_ge(kv_psum[lane], kv_psum.upto(L3X, 3))
                        copy(v[lane][0:K, 0:512], bank[lane][3][0:K, :]).then_inc(kv_ready[lane], 1)
                    for lane in LANES:
                        take_xT(lane, L3X)
                        act.wait_ge(kv_psum[lane], kv_psum.upto(L3X, 4))
                        copy(v[lane][0:K, 512:1024], bank[lane][1][0:K, :]).then_inc(kv_ready[lane], 1)
                    for lane in LANES:
                        for half in range(2):
                            act.wait_ge(q_psum[lane], q_psum.upto(L3X, half + 1))
                            copy(wide_a[lane][:, 512 * half:512 * half + 512], bank[lane][2 + half][:, :])\
                                .then_inc(q_ready[lane], 1)
                    for i in range(4):
                        for lane in LANES:
                            exponentials(lane, L3X, range(4 * i, 4 * i + 4), lambda n, h: wide_b[n][:, K * h:K * h + K],
                                         K, 1.0, i + 1)
                    for lane in LANES:
                        for half in range(2):
                            act.wait_ge(mix_psum[lane], mix_psum.upto(L3X, 1))
                            copy(wide_b[lane][:, 512 * half:512 * half + 512], bank[lane][half][:, :])\
                                .then_inc(mixT_ready[lane], 1)

                    for lane in LANES:
                        take_xT(lane, L3F)
                    for lane in LANES:
                        act.wait_ge(gate_psum[lane], gate_psum.upto(L3F, 1))
                        nc.scalar.activation(route[:, 1, E * lane:E * lane + E], bank[lane][1][:, 0:E], ACT.Exp,
                                             scale=-1.0).then_inc(logits_ready[lane], 1)
                    for lane in LANES:
                        act.wait_ge(hidden_psum[lane], hidden_psum.upto(L3F, 1))
                        copy(small[lane][0:64, 0:S], bank[lane][2][0:64, 0:S]).then_inc(hidden_ready[lane], 1)
                    for n, b_from in enumerate((3, 1)):
                        cols = slice(512 * n, 512 * n + 512)
                        for lane in LANES:
                            act.wait_ge(hidden_psum[lane], hidden_psum.upto(L3F, n + 2))
                            nc.scalar.activation(wide_b[lane][:, cols], bank[lane][b_from][:, :], ACT.Relu)\
                                .then_inc(hidden_ready[lane], 1)
                        for lane in LANES:
                            act.wait_ge(hidden_ready[lane], hidden_ready.upto(L3F, n + 2))
                            nc.scalar.activation(wide_a[lane][:, cols], wide_b[lane][:, cols], ACT.Square)\
                                .then_inc(squared[lane], 1)
                    for lane in LANES:
                        act.wait_ge(expertT_psum[lane], expertT_psum.upto(L3F, 1))
                        copy(gateT[lane][0:64, :], bank[lane][1][0:64, 0:S]).then_inc(expertT_ready[lane], 1)

                @block.gpsimd
                def _(pool):
                    chain = [0]

                    def link(ins):
                        chain[0] += 1
                        ins.then_inc(pool_chain, 1)
                        pool.wait_ge(pool_chain, chain[0])

                    def inverse_root(lane, layer, n, cols, rows=128):
                        pool.wait_ge(var_ready[lane], var_ready.upto(layer, n))
                        nc.gpsimd.tensor_tensor(rstd[lane][0:rows, cols], var_eps[lane][0:rows, cols],
                                                part["const", "minus_half"][0:rows, 0:cols.stop - cols.start], ALU.pow)\
                            .then_inc(rstd_ready[lane], 1)

                    one = slice(0, 1)
                    pool.wait_ge(inputs_loaded, 2 * 16)
                    for lane in LANES:
                        nc.gpsimd.tensor_copy(ctxT[lane][:, :], ctx_all[:, bass.ds((b + lane) * K, K)])\
                            .then_inc(lane_ready[lane], 1)
                    for lane in LANES:
                        inverse_root(lane, L0X, 1, one)
                    pool.wait_ge(loaded["L0x"], 16)
                    pool.wait_ge(loaded["L1x"], 16)
                    for lane in LANES:
                        nc.gpsimd.tensor_tensor(x_bias[lane][:, :], x[lane][:, :], part["L0x", "bo"], ALU.add)\
                            .then_inc(x_bias_ready[lane], 1)
                    for lane in LANES:
                        pool.wait_ge(lens_ready[lane], 1)
                        link(nc.gpsimd.tensor_scalar(mask1[lane][:, :], part["const", "iota_k"], lens[lane][:, 1:2], MASKED,
                                                     ALU.is_ge, ALU.mult))
                        link(nc.gpsimd.tensor_tensor(mask1[lane][:, :], mask1[lane][:, :], part["const", "causal"], ALU.add))
                        link(nc.gpsimd.tensor_scalar(row_ok[lane][:, 0:1], lens[lane][:, 1:2], 1.0, None, ALU.is_ge))
                        link(nc.gpsimd.tensor_scalar(row_ok[lane][:, 1:2], part["const", "iota_q"], lens[lane][:, 0:1],
                                                     row_ok[lane][:, 0:1], ALU.is_lt, ALU.mult))
                        pool.wait_ge(masks_loaded, 3 * 16)
                        link(nc.gpsimd.tensor_copy(mask2[lane][:, :], pm[:, bass.ds((b + lane) * K, K)]))
                        link(nc.gpsimd.tensor_scalar(mask2[lane][:, :], mask2[lane][:, :], 0.5, None, ALU.is_lt))
                        nc.gpsimd.tensor_scalar(mask2[lane][:, :], mask2[lane][:, :], MASKED, None, ALU.mult)\
                            .then_inc(masks_ready[lane], 1)
                    for lane in LANES:
                        inverse_root(lane, L0F, 1, one)
                    for h in range(H0F):
                        for lane in LANES:
                            two = scaled[lane][:, 2 * (h % 2):2 * (h % 2) + 2, :]
                            pool.wait_ge(scaled_ready[lane], scaled_ready.upto(L0F, h + 1))
                            link(nc.gpsimd.tensor_tensor(two[:, 0, :], two[:, 0, :], two[:, 1, :], ALU.add))
                            pool.wait_ge(v_mixed[lane], v_mixed.upto(L0F, 2 * h + 2))
                            v_h = v[lane][:, 128 * h:128 * h + 128]
                            nc.gpsimd.tensor_tensor(v_h, v_h, two[:, 0, :], ALU.add).then_inc(v_summed[lane], 1)
                    for lane in LANES:
                        pool.wait_ge(mix_psum[lane], mix_psum.upto(L0F, 2))
                        nc.gpsimd.tensor_tensor(
                            wide_a[lane][:, 0:H1X * K].rearrange("p (h k) -> p h k", k=K),
                            small[lane][:, 128:128 + K].unsqueeze(1).broadcast_to([128, H1X, K]),
                            part["const", "head_rows"].unsqueeze(2).broadcast_to([128, H1X, K]), ALU.mult)\
                            .then_inc(k_blocks[lane], 1)
                    for h in range(H0F):
                        for lane in LANES:
                            two = scaled[lane][:, 2 * (h % 2):2 * (h % 2) + 2, :]
                            pool.wait_ge(scaled_ready[lane], scaled_ready.upto(L0F, H0F + h + 1))
                            if h == 0:
                                nc.gpsimd.tensor_tensor(pooled[lane][:, :], two[:, 0, :], two[:, 1, :], ALU.add)\
                                    .then_inc(out_summed[lane], 1)
                            else:
                                link(nc.gpsimd.tensor_tensor(two[:, 0, :], two[:, 0, :], two[:, 1, :], ALU.add))
                                nc.gpsimd.tensor_tensor(pooled[lane][:, :], pooled[lane][:, :], two[:, 0, :], ALU.add)\
                                    .then_inc(out_summed[lane], 1)
                                pool.wait_ge(out_summed[lane], out_summed.upto(L0F, h + 1))
                    for lane in LANES:
                        inverse_root(lane, L1X, 1, one)
                    for lane in LANES:
                        nc.gpsimd.tensor_tensor(x_bias[lane][:, :], x[lane][:, :], part["L1x", "bo"], ALU.add)\
                            .then_inc(x_bias_ready[lane], 1)
                    for lane in LANES:
                        inverse_root(lane, L1F, 1, one)
                    for lane in LANES:
                        inverse_root(lane, L1F, 2, one)
                    for lane in LANES:
                        inverse_root(lane, L2X, 1, one)
                    for lane in LANES:
                        inverse_root(lane, L2X, 2, slice(0, 2))
                        inverse_root(lane, L2X, 2, slice(2, 4), K)
                    for lane in LANES:
                        inverse_root(lane, L2F, 1, one)
                    for lane in LANES:
                        inverse_root(lane, L3X, 1, one)
                    for i in range(4):
                        for lane in LANES:
                            pool.wait_ge(inv_ready[lane], inv_ready.upto(L3X, i + 1))
                            p3 = wide_b[lane][:, 4 * K * i:4 * K * (i + 1)].rearrange("p (h k) -> p h k", k=K)
                            nc.gpsimd.tensor_tensor(
                                p3, p3, row_inv[lane][:, 4 * i:4 * i + 4].unsqueeze(2).broadcast_to([128, 4, K]),
                                ALU.mult).then_inc(probs_normed[lane], 1)
                    for lane in LANES:
                        inverse_root(lane, L3F, 1, one)

                @block.vector
                def _(dve):
                    chain = [0]

                    def link(ins):
                        chain[0] += 1
                        ins.then_inc(dve_chain, 1)
                        dve.wait_ge(dve_chain, chain[0])

                    def ts(o, i, s1, s2, op0, op1=None):
                        if op1 is None:
                            return nc.vector.tensor_scalar(o, i, s1, None, op0)
                        return nc.vector.tensor_scalar(o, i, s1, s2, op0, op1)

                    def tt(o, a, c, op):
                        return nc.vector.tensor_tensor(o, a, c, op)

                    def norm_stats(lane, layer):
                        link(nc.vector.bn_stats(stats[lane][:, 0, :], x[lane][:, :]))
                        link(nc.vector.bn_aggr(mean_var[lane][:, 0, :], stats[lane][:, 0, :]))
                        ts(var_eps[lane][:, 0:1], mean_var[lane][:, 0, 1:2], 1e-5, None, ALU.add)\
                            .then_inc(var_ready[lane], 1)

                    def norm_apply(lane, layer):
                        dve.wait_ge(rstd_ready[lane], rstd_ready.upto(layer, 1))
                        ts(xn[lane][:, :], x[lane][:, :], mean_var[lane][:, 0, 0:1], rstd[lane][:, 0:1],
                           ALU.subtract, ALU.mult).then_inc(xn_ready[lane], 1)

                    def x_done(lane, layer, ins):
                        ins.then_inc(x_ready[lane], 1)
                        dve.wait_ge(x_ready[lane], x_ready.upto(layer, 1))
                        if layer < L3F:
                            norm_stats(lane, layer + 1)

                    def add_output(lane, layer, psum):
                        dve.wait_ge(out_psum[lane], out_psum.upto(layer, 1))
                        x_done(lane, layer, tt(x[lane][:, :], psum, x[lane][:, :], ALU.add))

                    def top2(groups, values, at=0):
                        cols = slice(at, at + groups * E)

                        def g(i):
                            return route[:, i, cols].rearrange("p (g e) -> p g e", e=E)

                        def each(i):
                            return per_group[:, i, 0:groups].unsqueeze(2).broadcast_to([128, groups, E])
                        order = part["const", "first"].unsqueeze(1).broadcast_to([128, groups, E])
                        left = values
                        for nth in range(2):
                            link(nc.vector.tensor_reduce(per_group[:, 0, 0:groups], g(left), AX.X, ALU.max))
                            link(tt(g(3), g(left), each(0), ALU.is_equal))
                            link(tt(g(3), g(3), order, ALU.mult))
                            link(nc.vector.tensor_reduce(per_group[:, 1, 0:groups], g(3), AX.X, ALU.max))
                            link(tt(g(4 + nth), g(3), each(1), ALU.is_equal))
                            if nth == 0:
                                link(nc.vector.scalar_tensor_tensor(route[:, 2, cols], route[:, 4, cols], GONE,
                                                                    route[:, left, cols], ALU.mult, ALU.add))
                                left = 2
                        link(tt(g(5), g(4), g(5), ALU.add))

                    def sum_of(groups, i, at=0):
                        link(nc.vector.tensor_reduce(per_group[:, 1, 0:groups],
                                                     route[:, i, at:at + groups * E].rearrange("p (g e) -> p g e", e=E),
                                                     AX.X, ALU.add))

                    def times_inverse(groups, i, at=0):
                        return tt(gate[:, at:at + groups * E].rearrange("p (g e) -> p g e", e=E),
                                  route[:, i, at:at + groups * E].rearrange("p (g e) -> p g e", e=E),
                                  per_group[:, 2, 0:groups].unsqueeze(2).broadcast_to([128, groups, E]), ALU.mult)

                    def l0_gates(t):
                        at = 128 * t
                        cols = slice(at, at + 128)
                        link(ts(route[:, 1, cols], route[:, 1, cols], 1.0, None, ALU.add))
                        link(nc.vector.reciprocal(route[:, 6, cols], route[:, 1, cols]))
                        top2(16, 0, at)
                        link(tt(route[:, 6, cols], route[:, 6, cols], route[:, 5, cols], ALU.mult))
                        sum_of(16, 6, at)
                        link(ts(per_group[:, 1, 0:16], per_group[:, 1, 0:16], 1e-9, None, ALU.max))
                        link(nc.vector.reciprocal(per_group[:, 2, 0:16], per_group[:, 1, 0:16]))
                        link(ts(per_group[:, 2, 0:16], per_group[:, 2, 0:16], part["L0f", "route"], None, ALU.mult))
                        return times_inverse(16, 6, at)

                    def in_order(lane, before, ins):
                        chain[0] += 1
                        ins.then_inc(dve_chain, 1)
                        before[lane] = chain[0]

                    dve.wait_ge(inputs_loaded, 2 * 16)
                    for lane in LANES:
                        link(nc.vector.tensor_copy(x[lane][:, :], x_all[:, bass.ds((b + lane) * D, D)]))
                        norm_stats(lane, L0X)
                    for lane in LANES:
                        norm_apply(lane, L0X)
                    for lane in LANES:
                        dve.wait_ge(kv_psum[lane], kv_psum.upto(L0X, 2))
                        tt(small[lane][0:K, 384:512], bank[lane][2][0:K, D:2 * D], part["L1x", "bv"][0:K, :], ALU.add)
                        tt(v[lane][0:K, 0:D], bank[lane][2][0:K, 0:D], part["L0x", "bv"][0:K, :], ALU.add)\
                            .then_inc(v_ready[lane], 1)
                    dve.wait_ge(masks_loaded, 3 * 16)
                    for lane in LANES:
                        cols = bass.ds((b + lane) * K, K)
                        nc.vector.tensor_reduce(lens[lane][:, 0:1], qm[:, cols], AX.X, ALU.add)
                        nc.vector.tensor_reduce(lens[lane][:, 1:2], km[:, cols], AX.X, ALU.add).then_inc(lens_ready[lane], 1)
                    for lane in LANES:
                        dve.wait_ge(scores_psum[lane], scores_psum.upto(L0X, 1))
                        link(nc.vector.reduce_max(max_neg[lane][:, 0:1], bank[lane][0][:, 0:K], AX.X))
                        ts(max_neg[lane][:, 0:1], max_neg[lane][:, 0:1], -D ** -0.5, None, ALU.mult)\
                            .then_inc(max_ready[lane], 1)
                    for lane in LANES:
                        dve.wait_ge(probs_ready[lane], probs_ready.upto(L0X, 1))
                        link(nc.vector.reciprocal(row_inv[lane][:, 0:1], row_sum[lane][:, 0:1]))
                    for lane in LANES:
                        dve.wait_ge(x_bias_ready[lane], x_bias_ready.upto(L0X, 1))
                        dve.wait_ge(out_psum[lane], out_psum.upto(L0X, 1))
                        x_done(lane, L0X, nc.vector.scalar_tensor_tensor(
                            x[lane][:, :], bank[lane][3][:, 0:D], row_inv[lane][:, 0:1], x_bias[lane][:, :],
                            ALU.mult, ALU.add))

                    for lane in LANES:
                        norm_apply(lane, L0F)
                    for lane in LANES:
                        dve.wait_ge(logits_ready[lane], logits_ready.upto(L0F, 1))
                    l0_gates(0).then_inc(gate_ready[0], 1)
                    for lane in LANES:
                        for half in range(2):
                            dve.wait_ge(scores_psum[lane], scores_psum.upto(L0F, half + 1))
                            link(nc.vector.tensor_reduce(max_neg[lane][:, 4 * half:4 * half + 4],
                                                         bank[lane][2 + half][:, :].rearrange("p (h k) -> p h k", k=S),
                                                         AX.X, ALU.max))
                        ts(max_neg[lane][:, 0:H0F], max_neg[lane][:, 0:H0F], -D ** -0.5, None, ALU.mult)\
                            .then_inc(max_ready[lane], 1)

                    def mix_experts(h, psum, done, column, to, fresh):
                        before = [chain[0], chain[0]]
                        for e in range(6):
                            half = e // 4
                            for lane in LANES:
                                if e % 4 == 0:
                                    dve.wait_ge(psum[lane], psum.upto(L0F, 2 * h + half + 1))
                                if e == 4:
                                    dve.wait_ge(scaled_ready[lane], scaled_ready.upto(L0F, (0 if fresh else H0F) + h + 1))
                                y = bank[lane][2 * (h % 2) + half][:, 128 * (e % 4):128 * (e % 4) + 128]
                                at = column + 64 * lane + E * h + e
                                g = gate[:, at:at + 1]
                                if e == 4:
                                    dve.wait_ge(done[lane], done.upto(L0F, 2 * h + 1))
                                elif e > 0:
                                    dve.wait_ge(dve_chain, before[lane])
                                elif not fresh and h > 0:
                                    dve.wait_ge(done[lane], done.upto(L0F, 2 * h))
                                if fresh and e == 0:
                                    ins = ts(to(lane), y, g, None, ALU.mult)
                                else:
                                    ins = nc.vector.scalar_tensor_tensor(to(lane), y, g, to(lane), ALU.mult, ALU.add)
                                if e in (3, 5):
                                    ins.then_inc(done[lane], 1)
                                else:
                                    in_order(lane, before, ins)

                    dve.wait_ge(gate_ready[0], gate_ready.upto(L0F, 1))
                    for h in range(H0F):
                        mix_experts(h, v_psum, v_mixed, 0, lambda lane: v[lane][:, 128 * h:128 * h + 128], True)
                    link(l0_gates(1))
                    for lane in LANES:
                        dve.wait_ge(probs_ready[lane], probs_ready.upto(L0F, 1))
                        link(nc.vector.reciprocal(row_inv[lane][:, 0:H0F], row_sum[lane][:, 0:H0F]))
                        g_out = gate[:, 128 + 64 * lane:192 + 64 * lane].rearrange("p (h e) -> p h e", e=E)
                        last = tt(g_out, g_out, row_inv[lane][:, 0:H0F].unsqueeze(2).broadcast_to([128, H0F, E]), ALU.mult)
                        if lane == 0:
                            link(last)
                    last.then_inc(gate_ready[0], 1)
                    dve.wait_ge(gate_ready[0], gate_ready.upto(L0F, 2))
                    for h in range(H0F):
                        mix_experts(h, out_psum, out_mixed, 128, lambda lane: x[lane][:, :], False)
                    for lane in LANES:
                        dve.wait_ge(out_mixed[lane], out_mixed.upto(L0F, 2 * H0F))
                        dve.wait_ge(out_summed[lane], out_summed.upto(L0F, H0F))
                        x_done(lane, L0F, tt(x[lane][:, :], x[lane][:, :], pooled[lane][:, :], ALU.add))

                    for lane in LANES:
                        norm_apply(lane, L1X)
                    def in_turn(banks, behind, first, then):
                        steps = [(i, lane) for i in range(banks) for lane in LANES]
                        for n in range(len(steps) + behind):
                            if n < len(steps):
                                first(*steps[n])
                            if n >= behind:
                                then(*steps[n - behind])

                    def take_scores(layer, scale, added):
                        def step(i, lane):
                            dve.wait_ge(scores_psum[lane], scores_psum.upto(layer, i + 1))
                            s3 = wide_b[lane][:, 4 * K * i:4 * K * (i + 1)].rearrange("p (h k) -> p h k", k=K)
                            link(nc.vector.scalar_tensor_tensor(
                                s3, bank[lane][i][:, 0:4 * K].rearrange("p (h k) -> p h k", k=K), scale,
                                added(lane).unsqueeze(1).broadcast_to([128, 4, K]), ALU.mult, ALU.add))
                            nc.vector.tensor_reduce(max_neg[lane][:, 4 * i:4 * i + 4], s3, AX.X, ALU.max, negate=True)\
                                .then_inc(max_ready[lane], 1)
                        return step

                    def take_transposed(layer, i, lane):
                        dve.wait_ge(pT_psum[lane], pT_psum.upto(layer, i + 1))
                        nc.vector.tensor_copy(wide_a[lane][0:K, 512 * i:512 * i + 512], bank[lane][i][0:K, :])\
                            .then_inc(pT_ready[lane], 1)

                    for lane in LANES:
                        dve.wait_ge(masks_ready[lane], 1)
                    in_turn(4, 3, take_scores(L1X, 8 ** -0.5, lambda lane: mask1[lane][:, :]),
                            lambda i, lane: take_transposed(L1X, i, lane))
                    for lane in LANES:
                        dve.wait_ge(probs_ready[lane], probs_ready.upto(L1X, 4))
                        link(nc.vector.reciprocal(row_inv[lane][:, :], row_sum[lane][:, :]))
                        link(ts(row_inv[lane][:, :], row_inv[lane][:, :], row_ok[lane][:, 1:2], None, ALU.mult))
                    for lane in LANES:
                        dve.wait_ge(mix_psum[lane], mix_psum.upto(L1X, 1))
                        tt(small[lane][:, 256:384].rearrange("p (h c) -> p h c", c=8),
                           bank[lane][0][:, 0:D].rearrange("p (h c) -> p h c", c=8),
                           row_inv[lane][:, :].unsqueeze(2).broadcast_to([128, H1X, 8]), ALU.mult)\
                            .then_inc(mix_scaled[lane], 1)
                    for lane in LANES:
                        dve.wait_ge(x_bias_ready[lane], x_bias_ready.upto(L1X, 1))
                        dve.wait_ge(out_psum[lane], out_psum.upto(L1X, 1))
                        x_done(lane, L1X, tt(x[lane][:, :], bank[lane][2][:, 0:D], x_bias[lane][:, :], ALU.add))

                    for lane in LANES:
                        norm_apply(lane, L1F)
                    for lane in LANES:
                        dve.wait_ge(hidden_ready[lane], hidden_ready.upto(L1F, 1))
                        link(nc.vector.bn_stats(stats[lane][:, 1, :], wide_b[lane][:, 0:512]))
                        link(nc.vector.bn_aggr(mean_var[lane][:, 1, :], stats[lane][:, 1, :]))
                        ts(var_eps[lane][:, 0:1], mean_var[lane][:, 1, 1:2], 1e-5, None, ALU.add)\
                            .then_inc(var_ready[lane], 1)
                    for lane in LANES:
                        dve.wait_ge(rstd_ready[lane], rstd_ready.upto(L1F, 2))
                        ts(wide_b[lane][:, 512:1024], wide_b[lane][:, 0:512], mean_var[lane][:, 1, 0:1],
                           rstd[lane][:, 0:1], ALU.subtract, ALU.mult).then_inc(hidden_normed[lane], 1)
                    for lane in LANES:
                        dve.wait_ge(hiddenT_psum[lane], hiddenT_psum.upto(L1F, 1))
                        for c in range(4):
                            last = ts(wide_a[lane][:, 128 * c:128 * c + 128], bank[lane][2][:, 128 * c:128 * c + 128],
                                      part["L1f", "lnw"][:, c:c + 1], part["L1f", "lnb"][:, c:c + 1], ALU.mult, ALU.add)
                        last.then_inc(hiddenT_ready[lane], 1)
                    for lane in LANES:
                        add_output(lane, L1F, bank[lane][3][:, 0:D])

                    for lane in LANES:
                        norm_apply(lane, L2X)
                    for lane in LANES:
                        dve.wait_ge(kv_ready[lane], kv_ready.upto(L2X, 1))
                        dve.wait_ge(q_ready[lane], q_ready.upto(L2X, 1))
                        for h in range(H2X):
                            nc.vector.bn_stats(stats[lane][:, h, :], small[lane][:, 256 + 64 * h:256 + 64 * h + 64])
                            link(nc.vector.bn_stats(stats[lane][0:K, 2 + h, :], v[lane][0:K, 64 * h:64 * h + 64]))
                        for h in range(H2X):
                            nc.vector.bn_aggr(mean_var[lane][:, h, :], stats[lane][:, h, :])
                            link(nc.vector.bn_aggr(mean_var[lane][0:K, 2 + h, :], stats[lane][0:K, 2 + h, :]))
                        ts(var_eps[lane][:, 0:2], mean_var[lane][:, 0:2, 1], 1e-6, None, ALU.add)
                        ts(var_eps[lane][0:K, 2:4], mean_var[lane][0:K, 2:4, 1], 1e-6, None, ALU.add)\
                            .then_inc(var_ready[lane], 1)
                    for lane in LANES:
                        dve.wait_ge(rstd_ready[lane], rstd_ready.upto(L2X, 3))
                        for h in range(H2X):
                            ts(small[lane][:, 64 * h:64 * h + 64], small[lane][:, 256 + 64 * h:256 + 64 * h + 64],
                               mean_var[lane][:, h, 0:1], rstd[lane][:, h:h + 1], ALU.subtract, ALU.mult)
                            last = ts(small[lane][0:K, 128 + 64 * h:128 + 64 * h + 64], v[lane][0:K, 64 * h:64 * h + 64],
                                      mean_var[lane][0:K, 2 + h, 0:1], rstd[lane][0:K, 2 + h:3 + h],
                                      ALU.subtract, ALU.mult)
                        last.then_inc(qk_normed[lane], 1)
                    for lane in LANES:
                        dve.wait_ge(scores_psum[lane], scores_psum.upto(L2X, 1))
                        for h in range(H2X):
                            link(tt(wide_b[lane][:, K * h:K * h + K], bank[lane][h][:, 0:K], mask2[lane][:, :], ALU.add))
                        link(nc.vector.tensor_reduce(max_neg[lane][:, 0:2],
                                                     wide_b[lane][:, 0:2 * K].rearrange("p (h k) -> p h k", k=K),
                                                     AX.X, ALU.max))
                        link(ts(row_ok[lane][:, 2:4], max_neg[lane][:, 0:2], 0.1 * MASKED, None, ALU.is_gt))
                        ts(max_neg[lane][:, 0:2], max_neg[lane][:, 0:2], -64 ** -0.5, None, ALU.mult)\
                            .then_inc(max_ready[lane], 1)
                    for lane in LANES:
                        dve.wait_ge(probs_ready[lane], probs_ready.upto(L2X, 1))
                        link(tt(row_sum[lane][:, 0:2], row_sum[lane][:, 0:2], row_ok[lane][:, 2:4], ALU.mult))
                        link(nc.vector.reciprocal(row_inv[lane][:, 0:2], row_sum[lane][:, 0:2]))
                        for h in range(H2X):
                            p = wide_b[lane][:, K * h:K * h + K]
                            last = ts(p, p, row_ok[lane][:, 2 + h:3 + h], row_inv[lane][:, h:h + 1], ALU.mult, ALU.mult)
                        last.then_inc(probs_normed[lane], 1)
                    for lane in LANES:
                        add_output(lane, L2X, bank[lane][0][:, 0:D])

                    for lane in LANES:
                        norm_apply(lane, L2F)
                    for lane in LANES:
                        dve.wait_ge(gate_psum[lane], gate_psum.upto(L2F, 1))
                        link(nc.vector.tensor_copy(route[:, 0, E * lane:E * lane + E], bank[lane][1][:, 0:E]))
                    nc.vector.tensor_reduce(per_group[:, 3, 0:2], route[:, 0, 0:2 * E].rearrange("p (g e) -> p g e", e=E),
                                            AX.X, ALU.max, negate=True).then_inc(logits_taken[0], 1)
                    top2(2, 0)
                    for lane in LANES:
                        dve.wait_ge(gate_exp[lane], gate_exp.upto(L2F, 1))
                    link(tt(route[:, 6, 0:2 * E], route[:, 1, 0:2 * E], route[:, 5, 0:2 * E], ALU.mult))
                    sum_of(2, 6)
                    link(nc.vector.reciprocal(per_group[:, 2, 0:2], per_group[:, 1, 0:2]))
                    times_inverse(2, 6).then_inc(gate_ready[0], 1)
                    dve.wait_ge(gate_ready[0], gate_ready.upto(L2F, 1))
                    before = [chain[0], chain[0]]
                    for e in range(E):
                        for lane in LANES:
                            if e % 4 == 0:
                                dve.wait_ge(out_psum[lane], out_psum.upto(L2F, e // 4 + 1))
                            dve.wait_ge(dve_chain, before[lane])
                            in_order(lane, before, nc.vector.scalar_tensor_tensor(
                                x[lane][:, :], bank[lane][2 + e // 4][:, 128 * (e % 4):128 * (e % 4) + 128],
                                gate[:, E * lane + e:E * lane + e + 1], x[lane][:, :], ALU.mult, ALU.add))
                    dve.wait_ge(dve_chain, before[1])
                    for lane in LANES:
                        dve.wait_ge(out_psum[lane], out_psum.upto(L2F, 3))
                        x_done(lane, L2F, tt(x[lane][:, :], bank[lane][1][:, 0:D], x[lane][:, :], ALU.add))

                    for lane in LANES:
                        norm_apply(lane, L3X)
                    def invert_sums(i, lane):
                        dve.wait_ge(probs_ready[lane], probs_ready.upto(L3X, i + 1))
                        nc.vector.reciprocal(row_inv[lane][:, 4 * i:4 * i + 4], row_sum[lane][:, 4 * i:4 * i + 4])\
                            .then_inc(inv_ready[lane], 1)

                    scores_step = take_scores(L3X, D ** -0.5, lambda lane: part["L3x", "bias"])
                    steps = [(i, lane) for i in range(4) for lane in LANES]
                    for n in range(len(steps) + 4):
                        if n < len(steps):
                            scores_step(*steps[n])
                        if 2 <= n < len(steps) + 2:
                            invert_sums(*steps[n - 2])
                        if n >= 4:
                            take_transposed(L3X, *steps[n - 4])
                    for lane in LANES:
                        add_output(lane, L3X, bank[lane][2][:, 0:D])

                    for lane in LANES:
                        norm_apply(lane, L3F)
                    for lane in LANES:
                        dve.wait_ge(logits_ready[lane], logits_ready.upto(L3F, 1))
                    both = 2 * E
                    r = [route[:, i, 0:both] for i in range(7)]
                    halves = [r[i].rearrange("p (g e) -> p g e", e=4) for i in range(7)]
                    worth = [per_group[:, i, 0:4] for i in range(4)]

                    def to_halves(t):
                        return t.unsqueeze(2).broadcast_to([128, 4, 4])

                    def of_lanes(t):
                        return t.unsqueeze(1).broadcast_to([128, 2, E])
                    as_lanes = [r[i].rearrange("p (n e) -> p n e", e=E) for i in range(7)]
                    link(ts(r[1], r[1], 1.0, None, ALU.add))
                    link(nc.vector.reciprocal(r[6], r[1]))
                    link(tt(as_lanes[0], as_lanes[6], of_lanes(part["L3f", "cb"]), ALU.add))
                    link(nc.vector.tensor_reduce(worth[0], halves[0], AX.X, ALU.max))
                    link(tt(halves[3], halves[0], to_halves(worth[0]), ALU.is_equal))
                    link(tt(as_lanes[3], as_lanes[3], of_lanes(part["const", "first"]), ALU.mult))
                    link(nc.vector.tensor_reduce(worth[1], halves[3], AX.X, ALU.max))
                    link(tt(halves[4], halves[3], to_halves(worth[1]), ALU.is_equal))
                    link(nc.vector.scalar_tensor_tensor(r[2], r[4], GONE, r[0], ALU.mult, ALU.add))
                    link(nc.vector.tensor_reduce(worth[1], halves[2], AX.X, ALU.max))
                    link(tt(worth[0], worth[0], worth[1], ALU.add))
                    first_group, second_group = slice(0, 4, 2), slice(1, 4, 2)
                    link(tt(worth[3][:, first_group], worth[0][:, first_group], worth[0][:, second_group], ALU.is_ge))
                    link(ts(worth[3][:, second_group], worth[3][:, first_group], -1.0, 1.0, ALU.mult, ALU.add))
                    link(tt(halves[0], halves[0], to_halves(worth[3]), ALU.mult))
                    top2(2, 0)
                    link(tt(r[6], r[6], r[5], ALU.mult))
                    sum_of(2, 6)
                    link(ts(per_group[:, 1, 0:2], per_group[:, 1, 0:2], 1e-20, None, ALU.add))
                    link(nc.vector.reciprocal(per_group[:, 2, 0:2], per_group[:, 1, 0:2]))
                    link(times_inverse(2, 6))
                    for lane in LANES:
                        dve.wait_ge(expert_psum[lane], expert_psum.upto(L3F, 1))
                        g_all = gate[:, E * lane:E * lane + E].rearrange("p (c o) -> p o c", o=2)
                        for odd in range(2):
                            last = tt(wide_b[lane][:, 1024 + 256 * odd:1280 + 256 * odd].rearrange("p (c u) -> p c u", u=64),
                                      bank[lane][2 * odd][:, 0:256].rearrange("p (c u) -> p c u", u=64),
                                      g_all[:, odd, :].unsqueeze(2).broadcast_to([128, 4, 64]), ALU.mult)
                        link(last)
                        nc.vector.tensor_reduce(comb[lane][:, :],
                                                wide_b[lane][:, 1024:1536].rearrange("p (e u) -> p u e", u=64),
                                                AX.X, ALU.add).then_inc(expert_mixed[lane], 1)
                    for lane in LANES:
                        dve.wait_ge(out_psum[lane], out_psum.upto(L3F, 1))
                        tt(x_all[:, bass.ds((b + lane) * D, D)], bank[lane][3][:, 0:D], x[lane][:, :], ALU.add)\
                            .then_inc(x_ready[lane], 1)

            nc.gpsimd.sem_clear(range(numbers[0], numbers[-1] + 1))
            nc.all_engine_barrier()
        nc.sync.wait_ge(out_stored, 16 * B)


def kernel(**inputs):
    import numpy as np
    import concourse.bacc as bacc
    from concourse.bass_utils import run_bass_kernel_spmd

    a = {name: np.asarray(value) for name, value in inputs.items()}

    def rows(vector, n=128):
        return np.broadcast_to(vector[None, :], (n, vector.shape[0]))

    def pad(t):
        return np.concatenate([t, np.zeros((128 - t.shape[0], t.shape[1]), t.dtype)])

    def inner(t):
        return t.reshape(-1, 128, t.shape[1]).transpose(1, 0, 2).reshape(128, -1)

    def stacked(t):
        return t.transpose(1, 0, 2).reshape(128, -1)

    q, k = np.arange(128)[:, None], np.arange(K)[None, :]
    f = np.float32
    parts = {
        "const": [np.eye(128, dtype=f), np.where(k > q, f(MASKED), f(0)), rows(np.arange(K, dtype=f)), q.astype(f),
                  rows(np.arange(E, 0, -1).astype(f)), (q // 8 == np.arange(H1X)[None, :]).astype(f),
                  np.ones((128, 128), f), np.full((128, 4), -0.5, f)],
        "L0x": [a["L0_xattn_Wk"].T, a["L0_xattn_Wv"].T, a["L0_xattn_Wq"].T, a["L0_xattn_Wo"].T,
                a["L0_xattn_bq"][:, None], rows(a["L0_xattn_bv"]), rows(a["L0_xattn_bo"])],
        "L0f": [a["L0_ffn_sel_v_w"].T, a["L0_ffn_sel_o_w"].T, a["L0_ffn_q_w"].T, a["L0_ffn_k_w"].T,
                rows(a["L0_ffn_route_scale"])],
        "L0v": [stacked(a["L0_ffn_v_w"])],
        "L0o": [stacked(a["L0_ffn_o_w"])],
        "L1x": [a["L1_xattn_W_K"], a["L1_xattn_W_V"], a["L1_xattn_W_Q"], a["L1_xattn_W_O"],
                a["L1_xattn_b_Q"][:, None], a["L1_xattn_b_K"][:, None], rows(a["L1_xattn_b_V"]), rows(a["L1_xattn_b_O"])],
        "L1f": [a["L1_ffn_W_fc"].T, inner(a["L1_ffn_W_proj"].T), a["L1_ffn_ln_w"].reshape(4, 128).T,
                a["L1_ffn_ln_b"].reshape(4, 128).T],
        "L2x": [a["L2_xattn_Wkv"], a["L2_xattn_Wq"], a["L2_xattn_Wo"], a["L2_xattn_qn_w"].reshape(128, 1),
                a["L2_xattn_kn_w"].reshape(128, 1)],
        "L2f": [a["L2_ffn_Wg"], stacked(a["L2_ffn_W1"]), a["L2_ffn_b1"].reshape(16, 128).T,
                inner(a["L2_ffn_W2"].reshape(2048, 128)), pad(a["L2_ffn_b2"])],
        "L3x": [a["L3_xattn_Wk"].T, a["L3_xattn_Wv"].T, a["L3_xattn_Wq"].T, inner(a["L3_xattn_Wp"].T),
                a["fside_1x1xSxS2_0"].reshape(S, K)],
        "L3f": [a["L3_ffn_gate"].T, rows(a["L3_ffn_corr_bias"]), a["L3_ffn_fc1_w"].T,
                pad(a["L3_ffn_w1"].transpose(2, 0, 1).reshape(64, 512)),
                a["L3_ffn_w2"].reshape(4, 2, 64, 64).transpose(1, 3, 0, 2).reshape(128, 256),
                pad(a["L3_ffn_fc2_w"].T), a["L3_ffn_up_w"].T, inner(a["L3_ffn_down_w"].T)],
    }
    arrays = {f"in_{name}": np.ascontiguousarray(np.concatenate(ps, axis=1)) for name, ps in parts.items()}
    for name in parts:
        assert arrays[f"in_{name}"].shape == (128, width(name)), (name, arrays[f"in_{name}"].shape)
    arrays["in_x"] = np.ascontiguousarray(a["x"].transpose(1, 0, 2).reshape(S, B * D))
    arrays["in_ctx"] = np.ascontiguousarray(a["ctx_1024"].transpose(2, 0, 1).reshape(D, B * K))
    arrays["in_q_mask"] = np.ascontiguousarray(rows(a["mask_BxS2_if1"].reshape(B * K)))
    arrays["in_k_mask"] = np.ascontiguousarray(rows(a["mask_BxS2_ik0"].reshape(B * K)))
    arrays["in_pair_mask"] = np.ascontiguousarray(a["mask_BxSxS2_bk0"].transpose(1, 0, 2).reshape(S, B * K))

    nc = bacc.Bacc("TRN2", target_bir_lowering=False, num_devices=1)
    d = {name: nc.dram_tensor(name, t.shape, mybir.dt.from_np(t.dtype), kind="ExternalInput").ap()
         for name, t in arrays.items()}
    out = nc.dram_tensor("out_0", (S, B * D), F32, kind="ExternalOutput").ap()
    build(nc, d["in_x"], d["in_ctx"], d["in_q_mask"], d["in_k_mask"], d["in_pair_mask"],
          {name: d[f"in_{name}"] for name in parts}, out)
    r = run_bass_kernel_spmd(nc, [arrays], core_ids=[0])
    return r.results[0]["out_0"].reshape(S, B, D).transpose(1, 0, 2)
```

```python
from contextlib import ExitStack

import concourse.bass as bass
from concourse import mybir

F32 = mybir.dt.float32
ALU = mybir.AluOpType
ACT = mybir.ActivationFunctionType
AX = mybir.AxisListType

B, S, K, D = 8, 128, 120, 128
E = 8
LANES = (0, 1)
L0X, L0F, L1X, L1F, L2X, L2F, L3X, L3F = range(8)
H0F, H1X, H2X, H3X = 8, 16, 2, 16
MASKED = -1e30
GONE = -1e30

PACKS = {
    "const": [("ident", 128), ("causal", K), ("iota_k", K), ("iota_q", 1), ("first", E), ("head_rows", H1X),
              ("ones", 128), ("minus_half", 4), ("head_cols", 128)],
    "L0x": [("wk", D), ("wv", D), ("wq", D), ("wo", D), ("bq", 1), ("bv", D), ("bo", D)],
    "L0f": [("sel", 2 * H0F * E), ("qk", 2 * H0F * D), ("route", 1)],
    "L0v": [("v", H0F * E * D)],
    "L0o": [("o", H0F * E * D)],
    "L1x": [("wk", D), ("wv", D), ("wq", D), ("wo", D), ("bq", 1), ("bk", 1), ("bv", D), ("bo", D)],
    "L1f": [("fc", 512), ("proj", 512), ("lnw", 4), ("lnb", 4)],
    "L2x": [("wkv", 2 * D), ("wq", D), ("wo", D), ("qn", 1), ("kn", 1)],
    "L2f": [("wg", E), ("w1", 2048), ("b1", 16), ("w2", 2048), ("b2", D)],
    "L3x": [("wk", 1024), ("wv", 1024), ("wq", 1024), ("wp", 1024), ("bias", K)],
    "L3f": [("gate", E), ("cb", E), ("fc1", 64), ("w1", 512), ("w2", 256), ("fc2", D), ("up", 512), ("down", 512)],
}


def width(pack):
    return sum(n for _, n in PACKS[pack])


def build(nc, x_in, ctx_in, q_mask, k_mask, pair_mask, packs, out):
    with ExitStack() as stack:
        def sb(name, shape, dt=F32):
            return stack.enter_context(nc.sbuf_tensor(name, shape, dt))

        def sem(name):
            return stack.enter_context(nc.semaphore(name))

        class Step:

            def __init__(self, name, per_layer, joint=False):
                self.sems = [sem(name)] * 2 if joint else [sem(f"{name}_{lane}") for lane in LANES]
                self.per_layer = per_layer

            def __getitem__(self, lane):
                return self.sems[lane]

            def upto(self, layer, n):
                assert 1 <= n <= self.per_layer[layer]
                return sum(self.per_layer[:layer]) + n

        part, loaded = {}, {}
        for pack, members in PACKS.items():
            t = sb(f"w_{pack}", [128, width(pack)])
            at = 0
            for name, n in members:
                part[pack, name] = t[:, at:at + n]
                at += n
            part[pack] = t
            loaded[pack] = sem(f"loaded_{pack}")
        inputs_loaded = sem("inputs_loaded")
        again_loaded = sem("again_loaded")
        masks_loaded = sem("masks_loaded")
        first_var = sem("first_var")
        first_rstd = sem("first_rstd")
        out_stored = sem("out_stored")
        setup_chain = sem("setup_chain")
        abs_summed = sem("abs_summed")
        abs_total = sem("abs_total")
        qk_product = sem("qk_product")
        qk_product_ready = sem("qk_product_ready")
        ident = part["const", "ident"]
        x_all = sb("x_all", [128, (B + len(LANES)) * D])
        ctx_all = sb("ctx_all", [128, (B + len(LANES)) * K])
        qm = sb("qm", [128, B * K], mybir.dt.int32)
        km = sb("km", [128, B * K], mybir.dt.int32)
        pm = sb("pm", [128, B * K], mybir.dt.uint8)
        abs_sum = sb("abs_sum", [128, 2])
        threshold = sb("threshold", [128, 4])

        def lanes(name, shape):
            return [sb(f"{name}_{lane}", shape) for lane in LANES]

        x = lanes("x", [128, D])
        x_bias = lanes("x_bias", [128, D])
        xn = lanes("xn", [128, D])
        xnT = lanes("xnT", [128, D])
        ctxT = lanes("ctxT", [128, K])
        wide_a = lanes("wide_a", [128, 2048])
        wide_b = lanes("wide_b", [128, 2048])
        v = lanes("v", [128, 1024])
        small = lanes("small", [128, 512])
        scaled = [wide_b[lane][:, 1024:1536].rearrange("p (e d) -> p e d", d=D) for lane in LANES]
        pooled = x_bias
        stats = lanes("stats", [128, 4, 6])
        mean_var = lanes("mean_var", [128, 4, 2])
        var_eps = lanes("var_eps", [128, 4])
        rstd = lanes("rstd", [128, 4])
        max_neg = lanes("max_neg", [128, 16])
        row_sum = lanes("row_sum", [128, 16])
        row_inv = lanes("row_inv", [128, 16])
        route = sb("route", [128, 7, 256])
        per_group = sb("per_group", [128, 4, 32])
        gate = sb("gate", [128, 256])
        comb = [small[lane][:, 256:320] for lane in LANES]
        mask1 = lanes("mask1", [128, K])
        mask2 = lanes("mask2", [128, K])
        lens = lanes("lens", [128, 2])
        row_ok = lanes("row_ok", [128, 4])
        gateT = lanes("gateT", [128, S])
        bank = [[stack.enter_context(nc.psum_tensor(f"bank{lane}{i}", [128, 512], F32)) for i in range(4)]
                for lane in LANES]

        once = [1] * 8
        var_ready = Step("var_ready", [0, 1, 1, 2, 2, 1, 1, 2])
        rstd_ready = Step("rstd_ready", [0, 1, 1, 2, 3, 1, 1, 2])
        xn_ready = Step("xn_ready", [0] + [1] * 7)
        xnT_psum = Step("xnT_psum", once)
        xnT_ready = Step("xnT_ready", once)
        masks_ready = Step("masks_ready", [0, 0, 1, 0, 0, 0, 0, 0])
        x_bias_ready = Step("x_bias_ready", [1, 0, 1, 0, 0, 0, 0, 0])
        x_ready = Step("x_ready", [1, 1, 1, 1, 1, 1, 1, 1])
        kv_psum = Step("kv_psum", [3, 0, 1, 1, 3, 0, 0, 0])
        kv_ready = Step("kv_ready", [1, 0, 1, 1, 3, 0, 0, 0])
        v_ready = Step("v_ready", [2, 0, 0, 0, 0, 0, 0, 0])
        v_mixed = Step("v_mixed", [0, 2 * H0F, 0, 0, 0, 0, 0, 0])
        scaled_ready = Step("scaled_ready", [0, 2 * H0F, 0, 0, 0, 0, 0, 0])
        v_summed = Step("v_summed", [0, H0F, 0, 0, 0, 0, 0, 0])
        out_summed = Step("out_summed", [0, H0F, 0, 0, 0, 0, 0, 0])
        lens_ready = Step("lens_ready", [1, 0, 0, 0, 0, 0, 0, 0])
        k_blocks = Step("k_blocks", [0, 0, 1, 0, 0, 0, 0, 0])
        v_blocks = Step("v_blocks", [0, 0, 1, 0, 0, 0, 0, 0])
        q_psum = Step("q_psum", [1, 2, 1, 0, 1, 0, 2, 0])
        q_ready = Step("q_ready", [1, 2, 1, 0, 1, 0, 2, 0])
        qk_normed = Step("qk_normed", [0, 0, 0, 0, 1, 0, 0, 0])
        qkT_psum = Step("qkT_psum", [0, 0, 0, 0, 1, 0, 0, 0])
        qkT_ready = Step("qkT_ready", [0, 0, 0, 0, 1, 0, 0, 0])
        scores_psum = Step("scores_psum", [1, 2, 4, 0, 1, 0, 4, 0])
        max_ready = Step("max_ready", [1, 1, 4, 0, 1, 0, 4, 0])
        probs_ready = Step("probs_ready", [1, 1, 4, 0, 1, 0, 4, 0])
        probs_normed = Step("probs_normed", [0, 0, 4, 0, 1, 0, 4, 0])
        inv_ready = Step("inv_ready", [0, 0, 4, 0, 0, 0, 4, 0])
        pT_psum = Step("pT_psum", [1, 2, 4, 0, 1, 0, 4, 0])
        pT_ready = Step("pT_ready", [1, 2, 4, 0, 1, 0, 4, 0])
        mix_psum = Step("mix_psum", [1, 2, 1, 0, 1, 0, 2, 0])
        mixT_ready = Step("mixT_ready", [1, 2, 1, 0, 1, 0, 2, 0])
        out_psum = Step("out_psum", [1, 2 * H0F, 1, 1, 1, 3, 1, 1])
        out_mixed = Step("out_mixed", [0, 2 * H0F, 0, 0, 0, 0, 0, 0])
        gate_psum = Step("gate_psum", [0, 1, 0, 0, 0, 1, 0, 1])
        logits_ready = Step("logits_ready", [0, 1, 0, 0, 0, 0, 0, 1])
        logits_taken = Step("logits_taken", [0, 0, 0, 0, 0, 1, 0, 0], joint=True)
        gate_exp = Step("gate_exp", [0, 0, 0, 0, 0, 1, 0, 0])
        gate_ready = Step("gate_ready", [0, 2, 0, 0, 0, 1, 0, 0], joint=True)
        gateT_psum = Step("gateT_psum", [0, 0, 0, 0, 0, 1, 0, 0])
        gateT_ready = Step("gateT_ready", [0, 0, 0, 0, 0, 1, 0, 0])
        v_psum = Step("v_psum", [0, 2 * H0F, 0, 0, 0, 0, 0, 0])
        hidden_psum = Step("hidden_psum", [0, 0, 0, 1, 0, 4, 0, 3])
        hidden_biased = Step("hidden_biased", [0, 0, 0, 0, 0, 4, 0, 0])
        hidden_ready = Step("hidden_ready", [0, 0, 0, 1, 0, 4, 0, 3])
        hidden_normed = Step("hidden_normed", [0, 0, 0, 1, 0, 0, 0, 0])
        hiddenT_psum = Step("hiddenT_psum", [0, 0, 0, 1, 0, 0, 0, 0])
        hiddenT_ready = Step("hiddenT_ready", [0, 0, 0, 1, 0, 0, 0, 0])
        squared = Step("squared", [0, 0, 0, 0, 0, 0, 0, 2])
        expert_psum = Step("expert_psum", [0, 0, 0, 0, 0, 0, 0, 1])
        expert_mixed = Step("expert_mixed", [0, 0, 0, 0, 0, 0, 0, 1])
        expertT_psum = Step("expertT_psum", [0, 0, 0, 0, 0, 0, 0, 1])
        expertT_ready = Step("expertT_ready", [0, 0, 0, 0, 0, 0, 0, 1])
        dve_chain = sem("dve_chain")
        pool_chain = sem("pool_chain")
        turn_sems = [s for st in (
            var_ready, rstd_ready, xn_ready, xnT_psum, xnT_ready, masks_ready, x_bias_ready, x_ready, kv_psum,
            kv_ready, v_ready, v_mixed, scaled_ready, v_summed, out_summed, lens_ready, k_blocks, v_blocks,
            q_psum, q_ready, qk_normed, qkT_psum, qkT_ready, scores_psum, max_ready, probs_ready, probs_normed,
            inv_ready, pT_psum, pT_ready, mix_psum, mixT_ready, out_psum, out_mixed, gate_psum, logits_ready,
            logits_taken, gate_exp, gate_ready, gateT_psum, gateT_ready, v_psum, hidden_psum, hidden_biased,
            hidden_ready, hidden_normed, hiddenT_psum, hiddenT_ready, squared, expert_psum, expert_mixed,
            expertT_psum, expertT_ready)
            for s in dict.fromkeys(st.sems)] + [dve_chain, pool_chain]
        numbers = sorted(s.num for s in turn_sems)
        assert numbers[-1] - numbers[0] + 1 == len(numbers)

        with nc.Block() as block:
            @block.sync
            def _(sp):
                sp.dma_start(part["const"][:, :], packs["const"]).then_inc(loaded["const"], 16)
                sp.dma_start(x_all[:, 0:B * D], x_in).then_inc(inputs_loaded, 16)
                sp.dma_start(ctx_all[:, 0:B * K], ctx_in).then_inc(inputs_loaded, 16)
                for pack in ("L0x", "L1x", "L0v", "L2x", "L3x"):
                    sp.dma_start(part[pack][:, :], packs[pack]).then_inc(loaded[pack], 16)
                sp.dma_start(x_all[:, B * D:], x_in[:, 0:len(LANES) * D]).then_inc(again_loaded, 16)
                sp.dma_start(ctx_all[:, B * K:], ctx_in[:, 0:len(LANES) * K]).then_inc(again_loaded, 16)

            @block.scalar
            def _(act):
                act.dma_start(part["L1f"][:, :], packs["L1f"]).then_inc(loaded["L1f"], 16)
                act.dma_start(part["L0f"][:, :], packs["L0f"]).then_inc(loaded["L0f"], 16)
                act.dma_start(qm[:, :], q_mask).then_inc(masks_loaded, 16)
                act.dma_start(km[:, :], k_mask).then_inc(masks_loaded, 16)
                act.dma_start(pm[:, :], pair_mask).then_inc(masks_loaded, 16)
                for pack in ("L0o", "L2f", "L3f"):
                    act.dma_start(part[pack][:, :], packs[pack]).then_inc(loaded[pack], 16)
                for half in range(2):
                    act.wait_ge(qk_product, half + 1)
                    nc.scalar.activation(part["L0f", "qk"][:, 512 * half:512 * half + 512], bank[1][half][:, :],
                                         ACT.Identity).then_inc(qk_product_ready, 1)

            @block.vector
            def _(dve):
                chain = [0]

                def link(ins):
                    chain[0] += 1
                    ins.then_inc(setup_chain, 1)
                    dve.wait_ge(setup_chain, chain[0])

                dve.wait_ge(inputs_loaded, 2 * 16)
                for lane in LANES:
                    x_first = x_all[:, lane * D:lane * D + D]
                    link(nc.vector.bn_stats(stats[lane][:, 0, :], x_first))
                    link(nc.vector.bn_aggr(mean_var[lane][:, 0, :], stats[lane][:, 0, :]))
                    nc.vector.tensor_scalar(var_eps[lane][:, 0:1], mean_var[lane][:, 0, 1:2], 1e-5, None, ALU.add)\
                        .then_inc(first_var, 1)
                for lane in LANES:
                    dve.wait_ge(first_rstd, lane + 1)
                    nc.vector.tensor_scalar(xn[lane][:, :], x_all[:, lane * D:lane * D + D], mean_var[lane][:, 0, 0:1],
                                            rstd[lane][:, 0:1], ALU.subtract, ALU.mult)
                dve.wait_ge(loaded["L1f"], 16)
                for i, name in enumerate(("fc", "proj")):
                    last = nc.vector.tensor_reduce(abs_sum[:, i:i + 1], part["L1f", name], AX.X, ALU.add,
                                                   apply_absolute_value=True)
                last.then_inc(abs_summed, 1)
                dve.wait_ge(abs_total, 1)
                link(nc.vector.tensor_scalar(threshold[:, 0:2], bank[0][0][:, 0:2], 1.0 / (512 * D), 1e-6, ALU.mult, ALU.add))
                link(nc.vector.tensor_scalar(threshold[:, 2:4], threshold[:, 0:2], -0.5, None, ALU.mult))
                link(nc.vector.tensor_scalar(threshold[:, 0:2], threshold[:, 0:2], 0.5, None, ALU.mult))
                for i, name in enumerate(("fc", "proj")):
                    w = part["L1f", name]
                    below = wide_b[0][:, 512 * i:512 * (i + 1)]
                    link(nc.vector.tensor_scalar(below, w, threshold[:, 2 + i:3 + i], None, ALU.is_lt))
                    link(nc.vector.tensor_scalar(w, w, threshold[:, i:i + 1], None, ALU.is_gt))
                    link(nc.vector.tensor_tensor(w, w, below, ALU.subtract))

            @block.gpsimd
            def _(pool):
                pool.wait_ge(loaded["const"], 16)
                for lane in LANES:
                    pool.wait_ge(first_var, lane + 1)
                    nc.gpsimd.tensor_tensor(rstd[lane][:, 0:1], var_eps[lane][:, 0:1],
                                            part["const", "minus_half"][:, 0:1], ALU.pow).then_inc(first_rstd, 1)
                pool.wait_ge(inputs_loaded, 2 * 16)
                for lane in LANES:
                    nc.gpsimd.tensor_copy(ctxT[lane][:, :], ctx_all[:, lane * K:lane * K + K])

            @block.tensor
            def _(pe):
                pe.wait_ge(loaded["const"], 16)
                pe.wait_ge(abs_summed, 1)
                nc.tensor.matmul(bank[0][0][:, 0:2], part["const", "ones"], abs_sum[:, :],
                                 start=True, stop=True).then_inc(abs_total, 1)
                pe.wait_ge(loaded["L0f"], 16)
                for half in range(2):
                    for h in range(4 * half, 4 * half + 4):
                        last = nc.tensor.matmul(bank[1][half][:, 128 * (h % 4):128 * (h % 4) + 128],
                                                part["L0f", "qk"][:, 128 * h:128 * h + 128],
                                                part["L0f", "qk"][:, D * (H0F + h):D * (H0F + h + 1)],
                                                start=True, stop=True)
                    last.then_inc(qk_product, 1)

        with nc.Fori(0, B // len(LANES)) as turn:
            b = turn * len(LANES)
            with nc.Block() as block:
                @block.sync
                def _(sp):
                    for lane in LANES:
                        sp.wait_ge(x_ready[lane], x_ready.upto(L3F, 1))
                        cols = bass.ds((b + lane) * D, D)
                        sp.dma_start(out[:, cols], x_all[:, cols]).then_inc(out_stored, 16)

                @block.tensor
                def _(pe):
                    def mm(o, lhsT, rhs, first=True, last=True):
                        return nc.tensor.matmul(o, lhsT, rhs, start=first, stop=last)

                    def stay_warm(free, products):
                        for _ in range(products):
                            mm(bank[0][free][:, :], ident, part["const"][:, 0:512])

                    def turn_x(lane, layer):
                        if layer != L0X:
                            pe.wait_ge(xn_ready[lane], xn_ready.upto(layer, 1))
                        nc.tensor.transpose(bank[lane][0][:, 0:S], xn[lane][:, :], ident)\
                            .then_inc(xnT_psum[lane], 1)

                    def in_turn(banks, behind, first, then):
                        steps = [(i, lane) for i in range(banks) for lane in LANES]
                        for n in range(len(steps) + behind):
                            if n < len(steps):
                                first(*steps[n])
                            if n >= behind:
                                then(*steps[n - behind])

                    def transpose_probs(ready, layer):
                        def step(i, lane):
                            pe.wait_ge(ready[lane], ready.upto(layer, i + 1))
                            for c in range(4):
                                h = 4 * i + c
                                last = nc.tensor.transpose(bank[lane][i][0:K, 128 * c:128 * c + 128],
                                                           wide_b[lane][:, K * h:K * h + K], ident)
                            last.then_inc(pT_psum[lane], 1)
                        return step

                    pe.wait_ge(loaded["L0x"], 16)
                    for lane in LANES:
                        turn_x(lane, L0X)
                    for lane in LANES:
                        mm(bank[lane][1][:, 0:K], part["L0x", "wk"], ctxT[lane][:, :]).then_inc(kv_psum[lane], 1)
                        mm(bank[lane][2][0:K, 0:D], ctxT[lane][:, :], part["L0x", "wv"]).then_inc(kv_psum[lane], 1)
                    for lane in LANES:
                        pe.wait_ge(xnT_ready[lane], xnT_ready.upto(L0X, 1))
                        mm(bank[lane][3][:, 0:S], part["L0x", "wq"], xnT[lane][:, :]).then_inc(q_psum[lane], 1)
                    for lane in LANES:
                        pe.wait_ge(kv_ready[lane], kv_ready.upto(L0X, 1))
                        pe.wait_ge(q_ready[lane], q_ready.upto(L0X, 1))
                        mm(bank[lane][0][:, 0:K], wide_a[lane][:, 0:S], wide_a[lane][:, 1024:1024 + K])\
                            .then_inc(scores_psum[lane], 1)
                    for lane in LANES:
                        pe.wait_ge(probs_ready[lane], probs_ready.upto(L0X, 1))
                        nc.tensor.transpose(bank[lane][1][0:K, 0:S], wide_b[lane][:, 0:K], ident)\
                            .then_inc(pT_psum[lane], 1)
                    for lane in LANES:
                        pe.wait_ge(v_ready[lane], v_ready.upto(L0X, 1))
                        pe.wait_ge(pT_ready[lane], pT_ready.upto(L0X, 1))
                        mm(bank[lane][2][:, 0:S], v[lane][0:K, 0:D], wide_a[lane][0:K, 0:S]).then_inc(mix_psum[lane], 1)
                    for lane in LANES:
                        pe.wait_ge(mixT_ready[lane], mixT_ready.upto(L0X, 1))
                        mm(bank[lane][3][:, 0:D], wide_b[lane][:, 0:S], part["L0x", "wo"]).then_inc(out_psum[lane], 1)

                    pe.wait_ge(loaded["L1x"], 16)
                    for lane in LANES:
                        mm(bank[lane][0][:, 0:K], part["L1x", "wk"], ctxT[lane][:, :])
                        mm(bank[lane][0][0:K, 128:256], ctxT[lane][:, :], part["L1x", "wv"]).then_inc(kv_psum[lane], 1)
                    stay_warm(1, 1)

                    pe.wait_ge(qk_product_ready, 2)
                    for lane in LANES:
                        turn_x(lane, L0F)
                    for lane in LANES:
                        pe.wait_ge(xnT_ready[lane], xnT_ready.upto(L0F, 1))
                        mm(bank[lane][1][:, 0:128], xnT[lane][:, :], part["L0f", "sel"]).then_inc(gate_psum[lane], 1)
                    for lane in LANES:
                        for half in range(2):
                            for c in range(4):
                                at = 512 * half + 128 * c
                                last = mm(bank[lane][2 + half][:, 128 * c:128 * c + 128],
                                          part["L0f", "qk"][:, at:at + 128], xnT[lane][:, :])
                            last.then_inc(q_psum[lane], 1)
                    for lane in LANES:
                        for half in range(2):
                            pe.wait_ge(q_ready[lane], q_ready.upto(L0F, half + 1))
                            for c in range(4):
                                last = mm(bank[lane][2 + half][:, 128 * c:128 * c + 128],
                                          wide_a[lane][:, 512 * half + 128 * c:512 * half + 128 * c + 128], xnT[lane][:, :])
                            last.then_inc(scores_psum[lane], 1)
                        pe.wait_ge(logits_ready[lane], logits_ready.upto(L0F, 1))
                    pe.wait_ge(loaded["L0v"], 16)
                    for h in range(H0F):
                        for half in range(2):
                            for lane in LANES:
                                if h == 1 and half == 0:
                                    pe.wait_ge(probs_ready[lane], probs_ready.upto(L0F, 1))
                                if h >= 2:
                                    pe.wait_ge(v_mixed[lane], v_mixed.upto(L0F, 2 * (h - 2) + half + 1))
                                at = (2 * h + half) * 512
                                mm(bank[lane][2 * (h % 2) + half][:, :], xnT[lane][:, :],
                                   part["L0v", "v"][:, at:at + 512]).then_inc(v_psum[lane], 1)
                    for lane in LANES:
                        for half in range(2):
                            pe.wait_ge(v_mixed[lane], v_mixed.upto(L0F, 2 * (H0F - 2) + half + 1))
                            for c in range(4):
                                h = 4 * half + c
                                last = nc.tensor.transpose(bank[lane][half][:, 128 * c:128 * c + 128],
                                                           wide_b[lane][:, 128 * h:128 * h + 128], ident)
                            last.then_inc(pT_psum[lane], 1)
                    for lane in LANES:
                        for half in range(2):
                            pe.wait_ge(pT_ready[lane], pT_ready.upto(L0F, half + 1))
                            pe.wait_ge(v_mixed[lane], v_mixed.upto(L0F, 2 * H0F))
                            pe.wait_ge(v_summed[lane], v_summed.upto(L0F, 4 * half + 4))
                            for c in range(4):
                                h = 4 * half + c
                                last = mm(bank[lane][2 + half][:, 128 * c:128 * c + 128],
                                          v[lane][:, 128 * h:128 * h + 128], wide_a[lane][:, 128 * h:128 * h + 128])
                            last.then_inc(mix_psum[lane], 1)
                    pe.wait_ge(loaded["L0o"], 16)
                    for h in range(H0F):
                        for half in range(2):
                            for lane in LANES:
                                if h in (0, 1) and half == 0:
                                    pe.wait_ge(mixT_ready[lane], mixT_ready.upto(L0F, h + 1))
                                if h >= 2:
                                    pe.wait_ge(out_mixed[lane], out_mixed.upto(L0F, 2 * (h - 2) + half + 1))
                                at = (2 * h + half) * 512
                                mm(bank[lane][2 * (h % 2) + half][:, :], wide_b[lane][:, 128 * h:128 * h + 128],
                                   part["L0o", "o"][:, at:at + 512]).then_inc(out_psum[lane], 1)

                    pe.wait_ge(out_mixed[0], out_mixed.upto(L0F, 2 * (H0F - 2) + 1))
                    stay_warm(0, 2)

                    for lane in LANES:
                        pe.wait_ge(out_mixed[lane], out_mixed.upto(L0F, 2 * H0F))
                        turn_x(lane, L1X)
                    for lane in LANES:
                        pe.wait_ge(xnT_ready[lane], xnT_ready.upto(L1X, 1))
                        mm(bank[lane][3][:, 0:S], part["L1x", "wq"], xnT[lane][:, :]).then_inc(q_psum[lane], 1)
                    for lane in LANES:
                        pe.wait_ge(q_ready[lane], q_ready.upto(L1X, 1))
                        pe.wait_ge(k_blocks[lane], k_blocks.upto(L1X, 1))
                    for i in range(4):
                        for lane in LANES:
                            mm(bank[lane][i][:, 0:4 * K], small[lane][:, 0:S],
                               wide_a[lane][:, 4 * K * i:4 * K * (i + 1)]).then_inc(scores_psum[lane], 1)

                    def mix_l1(i, lane):
                        pe.wait_ge(pT_ready[lane], pT_ready.upto(L1X, i + 1))
                        for c in range(4):
                            h = 4 * i + c
                            last = mm(bank[lane][0][32 * i:32 * i + 32, 0:S], v[lane][0:K, 32 * h:32 * h + 32],
                                      wide_a[lane][0:K, 128 * h:128 * h + 128], c == 0, c == 3)
                        if i == 3:
                            last.then_inc(mix_psum[lane], 1)
                    for lane in LANES:
                        pe.wait_ge(v_blocks[lane], v_blocks.upto(L1X, 1))
                    in_turn(4, 3, transpose_probs(probs_normed, L1X), mix_l1)
                    pe.wait_ge(loaded["L3x"], 16)
                    for lane in LANES:
                        mm(bank[lane][3][0:K, :], ctxT[lane][:, :], part["L3x", "wv"][:, 0:512])\
                            .then_inc(kv_psum[lane], 1)
                    for lane in LANES:
                        pe.wait_ge(mixT_ready[lane], mixT_ready.upto(L1X, 1))
                        mm(bank[lane][2][:, 0:D], wide_b[lane][:, 0:S], part["L1x", "wo"]).then_inc(out_psum[lane], 1)

                    stay_warm(1, 2)

                    for lane in LANES:
                        turn_x(lane, L1F)
                    for lane in LANES:
                        pe.wait_ge(xnT_ready[lane], xnT_ready.upto(L1F, 1))
                        mm(bank[lane][1][:, :], xnT[lane][:, :], part["L1f", "fc"]).then_inc(hidden_psum[lane], 1)
                    for lane in LANES:
                        mm(bank[lane][0][0:K, :], ctxT[lane][:, :], part["L3x", "wv"][:, 512:1024])\
                            .then_inc(kv_psum[lane], 1)
                    pe.wait_ge(loaded["L2x"], 16)
                    for lane in LANES:
                        pe.wait_ge(hidden_ready[lane], hidden_ready.upto(L1F, 1))
                        mm(bank[lane][1][0:K, 0:2 * D], ctxT[lane][:, :], part["L2x", "wkv"]).then_inc(kv_psum[lane], 1)
                    for lane in LANES:
                        pe.wait_ge(hidden_normed[lane], hidden_normed.upto(L1F, 1))
                        for c in range(4):
                            last = nc.tensor.transpose(bank[lane][2][:, 128 * c:128 * c + 128],
                                                       wide_b[lane][:, 512 + 128 * c:512 + 128 * c + 128], ident)
                        last.then_inc(hiddenT_psum[lane], 1)
                    for lane in LANES:
                        pe.wait_ge(kv_ready[lane], kv_ready.upto(L1X, 1))
                        pe.wait_ge(hiddenT_ready[lane], hiddenT_ready.upto(L1F, 1))
                        for c in range(4):
                            last = mm(bank[lane][3][:, 0:D], wide_a[lane][:, 128 * c:128 * c + 128],
                                      part["L1f", "proj"][:, 128 * c:128 * c + 128], c == 0, c == 3)
                        last.then_inc(out_psum[lane], 1)

                    stay_warm(2, 2)

                    for lane in LANES:
                        pe.wait_ge(kv_ready[lane], kv_ready.upto(L1F, 1))
                        turn_x(lane, L2X)
                    for lane in LANES:
                        pe.wait_ge(xnT_ready[lane], xnT_ready.upto(L2X, 1))
                        mm(bank[lane][2][:, 0:D], xnT[lane][:, :], part["L2x", "wq"]).then_inc(q_psum[lane], 1)
                    for lane in LANES:
                        pe.wait_ge(kv_ready[lane], kv_ready.upto(L2X, 1))
                        for half in range(2):
                            for c in range(4):
                                at = 512 * half + 128 * c
                                last = mm(bank[lane][half][:, K * c:K * c + K],
                                          part["L3x", "wk"][:, at:at + 128], ctxT[lane][:, :])
                            last.then_inc(kv_psum[lane], 1)
                    for lane in LANES:
                        pe.wait_ge(qk_normed[lane], qk_normed.upto(L2X, 1))
                        nc.tensor.transpose(bank[lane][3][:, 0:S], small[lane][:, 0:D], ident)
                        nc.tensor.transpose(bank[lane][3][:, S:S + K], small[lane][0:K, D:2 * D], ident[0:K, 0:K])\
                            .then_inc(qkT_psum[lane], 1)
                    for lane in LANES:
                        pe.wait_ge(qkT_ready[lane], qkT_ready.upto(L2X, 1))
                        pe.wait_ge(kv_ready[lane], kv_ready.upto(L2X, 3))
                        for h in range(H2X):
                            r = slice(64 * h, 64 * h + 64)
                            last = mm(bank[lane][h][:, 0:K], wide_a[lane][r, 0:S], wide_a[lane][r, S:S + K])
                        last.then_inc(scores_psum[lane], 1)
                    for lane in LANES:
                        pe.wait_ge(probs_normed[lane], probs_normed.upto(L2X, 1))
                        for h in range(H2X):
                            last = nc.tensor.transpose(bank[lane][2][0:K, 128 * h:128 * h + 128],
                                                       wide_b[lane][:, K * h:K * h + K], ident)
                        last.then_inc(pT_psum[lane], 1)
                    for lane in LANES:
                        pe.wait_ge(pT_ready[lane], pT_ready.upto(L2X, 1))
                        for h in range(H2X):
                            r = slice(64 * h, 64 * h + 64)
                            last = mm(bank[lane][3][r, 0:S], wide_a[lane][0:K, 1152 + 64 * h:1152 + 64 * h + 64],
                                      wide_a[lane][0:K, 256 + 128 * h:256 + 128 * h + 128])
                        last.then_inc(mix_psum[lane], 1)
                    for lane in LANES:
                        pe.wait_ge(mixT_ready[lane], mixT_ready.upto(L2X, 1))
                        mm(bank[lane][0][:, 0:D], wide_b[lane][:, 0:S], part["L2x", "wo"]).then_inc(out_psum[lane], 1)

                    stay_warm(2, 2)

                    pe.wait_ge(loaded["L2f"], 16)
                    for lane in LANES:
                        turn_x(lane, L2F)
                    for lane in LANES:
                        pe.wait_ge(xnT_ready[lane], xnT_ready.upto(L2F, 1))
                        mm(bank[lane][1][:, 0:E], xnT[lane][:, :], part["L2f", "wg"]).then_inc(gate_psum[lane], 1)
                    for lane in LANES:
                        for i, b_to in enumerate((2, 3, 0, 1)):
                            if b_to == 1:
                                pe.wait_ge(logits_taken[lane], logits_taken.upto(L2F, 1))
                            for c in range(4):
                                at = 512 * i + 128 * c
                                last = mm(bank[lane][b_to][:, 128 * c:128 * c + 128],
                                          part["L2f", "w1"][:, at:at + 128], xnT[lane][:, :])
                            last.then_inc(hidden_psum[lane], 1)
                    for half in range(2):
                        for lane in LANES:
                            for e in range(4 * half, 4 * half + 4):
                                if e % 2 == 0:
                                    pe.wait_ge(hidden_ready[lane], hidden_ready.upto(L2F, e // 2 + 1))
                                for c in range(2):
                                    at = 256 * e + 128 * c
                                    last = mm(bank[lane][2 + half][:, 128 * (e % 4):128 * (e % 4) + 128],
                                              wide_a[lane][:, at:at + 128], part["L2f", "w2"][:, at:at + 128],
                                              c == 0, c == 1)
                            last.then_inc(out_psum[lane], 1)
                            if half == 1:
                                pe.wait_ge(gate_ready[lane], gate_ready.upto(L2F, 1))
                                nc.tensor.transpose(bank[lane][0][0:E, 0:S], gate[:, E * lane:E * lane + E], ident)\
                                    .then_inc(gateT_psum[lane], 1)
                    for lane in LANES:
                        pe.wait_ge(gateT_ready[lane], gateT_ready.upto(L2F, 1))
                        mm(bank[lane][1][:, 0:D], gateT[lane][0:E, :], part["L2f", "b2"][0:E, :])\
                            .then_inc(out_psum[lane], 1)

                    stay_warm(0, 2)

                    for lane in LANES:
                        turn_x(lane, L3X)
                    def queries_l3(half, lane):
                        for c in range(4):
                            at = 512 * half + 128 * c
                            last = mm(bank[lane][2 + half][:, 128 * c:128 * c + 128],
                                      part["L3x", "wq"][:, at:at + 128], xnT[lane][:, :])
                        last.then_inc(q_psum[lane], 1)

                    def scores_l3(i, lane):
                        pe.wait_ge(q_ready[lane], q_ready.upto(L3X, min(i + 1, 2)))
                        for c in range(4):
                            odd, chunk = i // 2, 4 * (i % 2) + c
                            r = slice(64 * odd, 64 * odd + 64)
                            last = mm(bank[lane][i][:, K * c:K * c + K],
                                      wide_a[lane][r, 128 * chunk:128 * chunk + 128],
                                      wide_b[lane][r, 1024 + K * chunk:1024 + K * chunk + K])
                        last.then_inc(scores_psum[lane], 1)
                    for lane in LANES:
                        pe.wait_ge(xnT_ready[lane], xnT_ready.upto(L3X, 1))
                        queries_l3(0, lane)
                    for lane in LANES:
                        scores_l3(0, lane)
                        queries_l3(1, lane)
                    for i in range(1, 4):
                        for lane in LANES:
                            scores_l3(i, lane)

                    def mix_l3(i, lane):
                        pe.wait_ge(pT_ready[lane], pT_ready.upto(L3X, i + 1))
                        for c in range(4):
                            odd, chunk = i // 2, 4 * (i % 2) + c
                            h = 2 * chunk + odd
                            last = mm(bank[lane][i % 2][64 * odd:64 * odd + 64, 128 * c:128 * c + 128],
                                      v[lane][0:K, 64 * h:64 * h + 64],
                                      wide_a[lane][0:K, 128 * (4 * i + c):128 * (4 * i + c) + 128])
                        if i >= 2:
                            last.then_inc(mix_psum[lane], 1)
                    in_turn(4, 2, transpose_probs(probs_normed, L3X), mix_l3)
                    for lane in LANES:
                        for c in range(8):
                            if c % 4 == 0:
                                pe.wait_ge(mixT_ready[lane], mixT_ready.upto(L3X, c // 4 + 1))
                            last = mm(bank[lane][2][:, 0:D], wide_b[lane][:, 128 * c:128 * c + 128],
                                      part["L3x", "wp"][:, 128 * c:128 * c + 128], c == 0, c == 7)
                        last.then_inc(out_psum[lane], 1)

                    stay_warm(3, 2)

                    pe.wait_ge(loaded["L3f"], 16)
                    for lane in LANES:
                        turn_x(lane, L3F)
                    for lane in LANES:
                        pe.wait_ge(xnT_ready[lane], xnT_ready.upto(L3F, 1))
                        mm(bank[lane][1][:, 0:E], xnT[lane][:, :], part["L3f", "gate"]).then_inc(gate_psum[lane], 1)
                    for lane in LANES:
                        mm(bank[lane][2][0:64, 0:S], part["L3f", "fc1"], xnT[lane][:, :]).then_inc(hidden_psum[lane], 1)
                    for lane in LANES:
                        for c in range(4):
                            last = mm(bank[lane][3][:, 128 * c:128 * c + 128],
                                      part["L3f", "up"][:, 128 * c:128 * c + 128], xnT[lane][:, :])
                        last.then_inc(hidden_psum[lane], 1)
                        pe.wait_ge(hidden_ready[lane], hidden_ready.upto(L3F, 1))
                        pe.wait_ge(logits_ready[lane], logits_ready.upto(L3F, 1))
                        for p in range(4):
                            last = mm(bank[lane][1][:, 128 * p:128 * p + 128],
                                      part["L3f", "w1"][0:64, 128 * p:128 * p + 128], small[lane][0:64, 0:S])
                        last.then_inc(hidden_psum[lane], 1)

                    def shared_l3(lane):
                        pe.wait_ge(squared[lane], squared.upto(L3F, 1))
                        for c in range(4):
                            mm(bank[lane][3][:, 0:D], wide_a[lane][:, 128 * c:128 * c + 128],
                               part["L3f", "down"][:, 128 * c:128 * c + 128], c == 0, False)

                    shared_l3(0)
                    for lane in LANES:
                        pe.wait_ge(squared[lane], squared.upto(L3F, 2))
                        for odd in range(2):
                            r = slice(64 * odd, 64 * odd + 64)
                            for p in range(4):
                                last = mm(bank[lane][2 * odd][:, 64 * p:64 * p + 64],
                                          wide_a[lane][r, 512 + 128 * p:512 + 128 * p + 128],
                                          part["L3f", "w2"][r, 64 * p:64 * p + 64])
                        last.then_inc(expert_psum[lane], 1)
                    shared_l3(1)
                    for lane in LANES:
                        pe.wait_ge(expert_mixed[lane], expert_mixed.upto(L3F, 1))
                        nc.tensor.transpose(bank[lane][1][0:64, 0:S], comb[lane], ident)\
                            .then_inc(expertT_psum[lane], 1)
                    for lane in LANES:
                        pe.wait_ge(expertT_ready[lane], expertT_ready.upto(L3F, 1))
                        mm(bank[lane][3][:, 0:D], gateT[lane][0:64, :], part["L3f", "fc2"][0:64, :], False, True)\
                            .then_inc(out_psum[lane], 1)

                @block.scalar
                def _(act):
                    def copy(o, i, bias=0.0, scale=1.0):
                        return nc.scalar.activation(o, i, ACT.Identity, bias=bias, scale=scale)

                    def take_xT(lane, layer):
                        act.wait_ge(xnT_psum[lane], xnT_psum.upto(layer, 1))
                        copy(xnT[lane][:, :], bank[lane][0][:, 0:S]).then_inc(xnT_ready[lane], 1)

                    def exponentials(lane, layer, heads, scores, cols, scale, n=1):
                        act.wait_ge(max_ready[lane], max_ready.upto(layer, n))
                        for h in heads:
                            last = nc.scalar.activation(wide_b[lane][:, cols * h:cols * h + cols], scores(lane, h), ACT.Exp,
                                                        bias=max_neg[lane][:, h:h + 1], scale=scale,
                                                        accum_out=row_sum[lane][:, h:h + 1])
                        last.then_inc(probs_ready[lane], 1)

                    def exponentials_of_banks(layer, behind):
                        steps = [(i, lane) for i in range(4) for lane in LANES]
                        for n in range(len(steps) + behind):
                            if n < len(steps):
                                i, lane = steps[n]
                                exponentials(lane, layer, range(4 * i, 4 * i + 4),
                                             lambda n, h: wide_b[n][:, K * h:K * h + K], K, 1.0, i + 1)
                            if n >= behind and steps[n - behind][1] == 1:
                                i, lane = steps[n - behind]
                                act.wait_ge(pT_psum[lane], pT_psum.upto(layer, i + 1))
                                copy(wide_a[lane][0:K, 512 * i:512 * i + 512], bank[lane][i][0:K, :])\
                                    .then_inc(pT_ready[lane], 1)

                    for lane in LANES:
                        take_xT(lane, L0X)
                    for lane in LANES:
                        act.wait_ge(kv_psum[lane], kv_psum.upto(L0X, 1))
                        copy(wide_a[lane][:, 1024:1024 + K], bank[lane][1][:, 0:K]).then_inc(kv_ready[lane], 1)
                    for lane in LANES:
                        act.wait_ge(q_psum[lane], q_psum.upto(L0X, 1))
                        copy(wide_a[lane][:, 0:S], bank[lane][3][:, 0:S], bias=part["L0x", "bq"]).then_inc(q_ready[lane], 1)
                    for lane in LANES:
                        exponentials(lane, L0X, [0], lambda n, h: bank[n][0][:, 0:K], K, D ** -0.5)
                    for lane in LANES:
                        act.wait_ge(pT_psum[lane], pT_psum.upto(L0X, 1))
                        copy(wide_a[lane][0:K, 0:S], bank[lane][1][0:K, 0:S]).then_inc(pT_ready[lane], 1)
                    for lane in LANES:
                        act.wait_ge(mix_psum[lane], mix_psum.upto(L0X, 1))
                        copy(wide_b[lane][:, 0:S], bank[lane][2][:, 0:S]).then_inc(mixT_ready[lane], 1)

                    for lane in LANES:
                        take_xT(lane, L0F)
                    for lane in LANES:
                        act.wait_ge(gate_psum[lane], gate_psum.upto(L0F, 1))
                        logits = bank[lane][1][:, 0:128].rearrange("p (t c) -> p t c", t=2)

                        def mine(i):
                            return route[:, i, :].rearrange("p (t n c) -> p n t c", t=2, n=2)[:, lane]
                        nc.scalar.activation(mine(1), logits, ACT.Exp, scale=-1.0)
                        copy(mine(0), logits).then_inc(logits_ready[lane], 1)
                    for lane in LANES:
                        for half in range(2):
                            act.wait_ge(q_psum[lane], q_psum.upto(L0F, half + 1))
                            copy(wide_a[lane][:, 512 * half:512 * half + 512], bank[lane][2 + half][:, :])\
                                .then_inc(q_ready[lane], 1)
                    for lane in LANES:
                        exponentials(lane, L0F, range(H0F),
                                     lambda n, h: bank[n][2 + h // 4][:, 128 * (h % 4):128 * (h % 4) + 128], S, D ** -0.5)

                    def scale_experts(h, psum, column, first):
                        for lane in LANES:
                            act.wait_ge(psum[lane], psum.upto(L0F, 2 * h + 2))
                            if not first or h >= 2:
                                done = v_summed if first else out_summed
                                if not first and h < 2:
                                    act.wait_ge(v_summed[lane], v_summed.upto(L0F, H0F - 1 + h))
                                else:
                                    act.wait_ge(done[lane], done.upto(L0F, h - 1))
                            for e in (6, 7):
                                g = column + 64 * lane + E * h + e
                                last = nc.scalar.activation(scaled[lane][:, 2 * (h % 2) + e - 6, :],
                                                            bank[lane][2 * (h % 2) + 1][:, 128 * (e - 4):128 * (e - 4) + 128],
                                                            ACT.Copy, scale=gate[:, g:g + 1])
                            last.then_inc(scaled_ready[lane], 1)
                    act.wait_ge(gate_ready[0], gate_ready.upto(L0F, 1))
                    for h in range(H0F):
                        scale_experts(h, v_psum, 0, True)
                    for lane in LANES:
                        for half in range(2):
                            act.wait_ge(pT_psum[lane], pT_psum.upto(L0F, half + 1))
                            copy(wide_a[lane][:, 512 * half:512 * half + 512], bank[lane][half][:, :])\
                                .then_inc(pT_ready[lane], 1)
                    for lane in LANES:
                        for half in range(2):
                            act.wait_ge(mix_psum[lane], mix_psum.upto(L0F, half + 1))
                            copy(wide_b[lane][:, 512 * half:512 * half + 512], bank[lane][2 + half][:, :])\
                                .then_inc(mixT_ready[lane], 1)

                    act.wait_ge(gate_ready[0], gate_ready.upto(L0F, 2))
                    for h in range(H0F):
                        scale_experts(h, out_psum, 128, False)

                    for lane in LANES:
                        take_xT(lane, L1X)
                    for lane in LANES:
                        act.wait_ge(q_psum[lane], q_psum.upto(L1X, 1))
                        copy(small[lane][:, 0:S], bank[lane][3][:, 0:S], bias=part["L1x", "bq"]).then_inc(q_ready[lane], 1)
                    exponentials_of_banks(L1X, 5)
                    for lane in LANES:
                        act.wait_ge(mix_psum[lane], mix_psum.upto(L1X, 1))
                        copy(wide_b[lane][:, 0:S], bank[lane][0][:, 0:S]).then_inc(mixT_ready[lane], 1)
                    for lane in LANES:
                        act.wait_ge(kv_psum[lane], kv_psum.upto(L1X, 1))
                        copy(v[lane][0:K, 0:512], bank[lane][3][0:K, :]).then_inc(kv_ready[lane], 1)

                    for lane in LANES:
                        take_xT(lane, L1F)
                    for lane in LANES:
                        act.wait_ge(hidden_psum[lane], hidden_psum.upto(L1F, 1))
                        nc.scalar.activation(wide_b[lane][:, 0:512], bank[lane][1][:, :], ACT.Gelu)\
                            .then_inc(hidden_ready[lane], 1)
                    for lane in LANES:
                        act.wait_ge(kv_psum[lane], kv_psum.upto(L1F, 1))
                        copy(v[lane][0:K, 512:1024], bank[lane][0][0:K, :]).then_inc(kv_ready[lane], 1)

                    for lane in LANES:
                        act.wait_ge(kv_psum[lane], kv_psum.upto(L2X, 1))
                        copy(wide_a[lane][0:K, 1024:1280], bank[lane][1][0:K, 0:2 * D]).then_inc(kv_ready[lane], 1)
                    act.wait_ge(hiddenT_psum[1], hiddenT_psum.upto(L1F, 1))
                    for c in range(4):
                        last = copy(wide_a[1][:, 128 * c:128 * c + 128], bank[1][2][:, 128 * c:128 * c + 128],
                                    bias=part["L1f", "lnb"][:, c:c + 1], scale=part["L1f", "lnw"][:, c:c + 1])
                    last.then_inc(hiddenT_ready[1], 1)
                    for lane in LANES:
                        take_xT(lane, L2X)
                    for lane in LANES:
                        act.wait_ge(q_psum[lane], q_psum.upto(L2X, 1))
                        copy(small[lane][:, 256:256 + D], bank[lane][2][:, 0:D]).then_inc(q_ready[lane], 1)
                    for lane in LANES:
                        for half in range(2):
                            act.wait_ge(kv_psum[lane], kv_psum.upto(L2X, half + 2))
                            copy(wide_b[lane][:, 1024 + 4 * K * half:1024 + 4 * K * (half + 1)],
                                 bank[lane][half][:, 0:4 * K]).then_inc(kv_ready[lane], 1)
                    for lane in LANES:
                        act.wait_ge(qkT_psum[lane], qkT_psum.upto(L2X, 1))
                        copy(wide_a[lane][:, 0:S], bank[lane][3][:, 0:S], scale=part["L2x", "qn"])
                        copy(wide_a[lane][:, S:S + K], bank[lane][3][:, S:S + K], scale=part["L2x", "kn"])\
                            .then_inc(qkT_ready[lane], 1)
                    for lane in LANES:
                        exponentials(lane, L2X, range(H2X), lambda n, h: wide_b[n][:, K * h:K * h + K], K, 64 ** -0.5)
                    for lane in LANES:
                        act.wait_ge(pT_psum[lane], pT_psum.upto(L2X, 1))
                        copy(wide_a[lane][0:K, 256:512], bank[lane][2][0:K, 0:256]).then_inc(pT_ready[lane], 1)
                    for lane in LANES:
                        act.wait_ge(mix_psum[lane], mix_psum.upto(L2X, 1))
                        copy(wide_b[lane][:, 0:S], bank[lane][3][:, 0:S]).then_inc(mixT_ready[lane], 1)

                    for lane in LANES:
                        take_xT(lane, L2F)
                    for lane in LANES:
                        act.wait_ge(logits_taken[lane], logits_taken.upto(L2F, 1))
                        nc.scalar.activation(route[:, 1, E * lane:E * lane + E], route[:, 0, E * lane:E * lane + E], ACT.Exp,
                                             bias=per_group[:, 3, lane:lane + 1]).then_inc(gate_exp[lane], 1)
                    for lane in LANES:
                        for i in range(4):
                            act.wait_ge(hidden_biased[lane], hidden_biased.upto(L2F, i + 1))
                            h = wide_a[lane][:, 512 * i:512 * i + 512]
                            nc.scalar.activation(h, h, ACT.Gelu).then_inc(hidden_ready[lane], 1)
                    for lane in LANES:
                        act.wait_ge(gateT_psum[lane], gateT_psum.upto(L2F, 1))
                        copy(gateT[lane][0:E, :], bank[lane][0][0:E, 0:S]).then_inc(gateT_ready[lane], 1)

                    for lane in LANES:
                        take_xT(lane, L3X)
                    for half in range(2):
                        for lane in LANES:
                            act.wait_ge(q_psum[lane], q_psum.upto(L3X, half + 1))
                            copy(wide_a[lane][:, 512 * half:512 * half + 512], bank[lane][2 + half][:, :])\
                                .then_inc(q_ready[lane], 1)
                    exponentials_of_banks(L3X, 4)
                    for half in range(2):
                        for lane in LANES:
                            act.wait_ge(mix_psum[lane], mix_psum.upto(L3X, half + 1))
                            copy(wide_b[lane][:, 512 * half:512 * half + 512], bank[lane][half][:, :])\
                                .then_inc(mixT_ready[lane], 1)

                    for lane in LANES:
                        take_xT(lane, L3F)
                    for lane in LANES:
                        act.wait_ge(gate_psum[lane], gate_psum.upto(L3F, 1))
                        nc.scalar.activation(route[:, 1, E * lane:E * lane + E], bank[lane][1][:, 0:E], ACT.Exp,
                                             scale=-1.0).then_inc(logits_ready[lane], 1)
                    for lane in LANES:
                        act.wait_ge(hidden_psum[lane], hidden_psum.upto(L3F, 1))
                        copy(small[lane][0:64, 0:S], bank[lane][2][0:64, 0:S]).then_inc(hidden_ready[lane], 1)
                    for lane in LANES:
                        for n, b_from in enumerate((3, 1)):
                            cols = slice(512 * n, 512 * n + 512)
                            act.wait_ge(hidden_psum[lane], hidden_psum.upto(L3F, n + 2))
                            nc.scalar.activation(wide_b[lane][:, cols], bank[lane][b_from][:, :], ACT.Relu)\
                                .then_inc(hidden_ready[lane], 1)
                            act.wait_ge(hidden_ready[lane], hidden_ready.upto(L3F, n + 2))
                            nc.scalar.activation(wide_a[lane][:, cols], wide_b[lane][:, cols], ACT.Square)\
                                .then_inc(squared[lane], 1)
                    for lane in LANES:
                        act.wait_ge(expertT_psum[lane], expertT_psum.upto(L3F, 1))
                        copy(gateT[lane][0:64, :], bank[lane][1][0:64, 0:S]).then_inc(expertT_ready[lane], 1)

                @block.gpsimd
                def _(pool):
                    chain = [0]

                    def link(ins):
                        chain[0] += 1
                        ins.then_inc(pool_chain, 1)
                        pool.wait_ge(pool_chain, chain[0])

                    def inverse_root(lane, layer, n, cols, rows=128):
                        pool.wait_ge(var_ready[lane], var_ready.upto(layer, n))
                        nc.gpsimd.tensor_tensor(rstd[lane][0:rows, cols], var_eps[lane][0:rows, cols],
                                                part["const", "minus_half"][0:rows, 0:cols.stop - cols.start], ALU.pow)\
                            .then_inc(rstd_ready[lane], 1)

                    def normalise_probs(layer):
                        for i in range(4):
                            for lane in LANES:
                                pool.wait_ge(inv_ready[lane], inv_ready.upto(layer, i + 1))
                                p3 = wide_b[lane][:, 4 * K * i:4 * K * (i + 1)].rearrange("p (h k) -> p h k", k=K)
                                nc.gpsimd.tensor_tensor(
                                    p3, p3, row_inv[lane][:, 4 * i:4 * i + 4].unsqueeze(2).broadcast_to([128, 4, K]),
                                    ALU.mult).then_inc(probs_normed[lane], 1)

                    one = slice(0, 1)
                    pool.wait_ge(loaded["L0x"], 16)
                    pool.wait_ge(loaded["L1x"], 16)
                    for lane in LANES:
                        nc.gpsimd.tensor_tensor(x_bias[lane][:, :], x_all[:, bass.ds((b + lane) * D, D)], part["L0x", "bo"], ALU.add)\
                            .then_inc(x_bias_ready[lane], 1)
                    for lane in LANES:
                        inverse_root(lane, L0F, 1, one)
                    for lane in LANES:
                        pool.wait_ge(lens_ready[lane], 1)
                        link(nc.gpsimd.tensor_scalar(mask1[lane][:, :], part["const", "iota_k"], lens[lane][:, 1:2], MASKED,
                                                     ALU.is_ge, ALU.mult))
                        link(nc.gpsimd.tensor_tensor(mask1[lane][:, :], mask1[lane][:, :], part["const", "causal"], ALU.add))
                        link(nc.gpsimd.tensor_scalar(row_ok[lane][:, 0:1], lens[lane][:, 1:2], 1.0, None, ALU.is_ge))
                        link(nc.gpsimd.tensor_scalar(row_ok[lane][:, 1:2], part["const", "iota_q"], lens[lane][:, 0:1],
                                                     row_ok[lane][:, 0:1], ALU.is_lt, ALU.mult))
                        pool.wait_ge(masks_loaded, 3 * 16)
                        link(nc.gpsimd.tensor_copy(mask2[lane][:, :], pm[:, bass.ds((b + lane) * K, K)]))
                        link(nc.gpsimd.tensor_scalar(mask2[lane][:, :], mask2[lane][:, :], 0.5, None, ALU.is_lt))
                        nc.gpsimd.tensor_scalar(mask2[lane][:, :], mask2[lane][:, :], MASKED, None, ALU.mult)\
                            .then_inc(masks_ready[lane], 1)
                    for h in range(H0F):
                        for lane in LANES:
                            two = scaled[lane][:, 2 * (h % 2):2 * (h % 2) + 2, :]
                            pool.wait_ge(scaled_ready[lane], scaled_ready.upto(L0F, h + 1))
                            link(nc.gpsimd.tensor_tensor(two[:, 0, :], two[:, 0, :], two[:, 1, :], ALU.add))
                            pool.wait_ge(v_mixed[lane], v_mixed.upto(L0F, 2 * h + 2))
                            v_h = v[lane][:, 128 * h:128 * h + 128]
                            nc.gpsimd.tensor_tensor(v_h, v_h, two[:, 0, :], ALU.add).then_inc(v_summed[lane], 1)
                    for lane in LANES:
                        pool.wait_ge(mix_psum[lane], mix_psum.upto(L0F, 2))
                        nc.gpsimd.tensor_tensor(
                            wide_a[lane][:, 0:H1X * K].rearrange("p (h k) -> p h k", k=K),
                            small[lane][:, 128:128 + K].unsqueeze(1).broadcast_to([128, H1X, K]),
                            part["const", "head_rows"].unsqueeze(2).broadcast_to([128, H1X, K]), ALU.mult)\
                            .then_inc(k_blocks[lane], 1)
                    for lane in LANES:
                        for i in range(4):
                            last = nc.gpsimd.tensor_tensor(
                                v[lane][0:K, 128 * i:128 * i + 128].rearrange("p (h c) -> p h c", c=32),
                                small[lane][0:K, 384 + 32 * i:416 + 32 * i].unsqueeze(1).broadcast_to([K, 4, 32]),
                                part["const", "head_cols"][0:K, :].rearrange("p (h c) -> p h c", c=32), ALU.mult)
                        last.then_inc(v_blocks[lane], 1)
                    for h in range(H0F):
                        for lane in LANES:
                            two = scaled[lane][:, 2 * (h % 2):2 * (h % 2) + 2, :]
                            pool.wait_ge(scaled_ready[lane], scaled_ready.upto(L0F, H0F + h + 1))
                            if h == 0:
                                nc.gpsimd.tensor_tensor(pooled[lane][:, :], two[:, 0, :], two[:, 1, :], ALU.add)\
                                    .then_inc(out_summed[lane], 1)
                            else:
                                link(nc.gpsimd.tensor_tensor(two[:, 0, :], two[:, 0, :], two[:, 1, :], ALU.add))
                                nc.gpsimd.tensor_tensor(pooled[lane][:, :], pooled[lane][:, :], two[:, 0, :], ALU.add)\
                                    .then_inc(out_summed[lane], 1)
                                pool.wait_ge(out_summed[lane], out_summed.upto(L0F, h + 1))
                    for lane in LANES:
                        inverse_root(lane, L1X, 1, one)
                    for lane in LANES:
                        nc.gpsimd.tensor_tensor(x_bias[lane][:, :], x[lane][:, :], part["L1x", "bo"], ALU.add)\
                            .then_inc(x_bias_ready[lane], 1)
                    normalise_probs(L1X)
                    for lane in LANES:
                        inverse_root(lane, L1F, 1, one)
                    for lane in LANES:
                        inverse_root(lane, L1F, 2, one)
                    for lane in LANES:
                        inverse_root(lane, L2X, 1, one)
                    for lane in LANES:
                        inverse_root(lane, L2X, 2, slice(0, 2))
                        inverse_root(lane, L2X, 2, slice(2, 4), K)
                    for lane in LANES:
                        inverse_root(lane, L2F, 1, one)
                    for lane in LANES:
                        inverse_root(lane, L3X, 1, one)
                    normalise_probs(L3X)
                    for lane in LANES:
                        inverse_root(lane, L3F, 1, one)
                    pool.wait_ge(again_loaded, 2 * 16)
                    for lane in LANES:
                        nc.gpsimd.tensor_copy(ctxT[lane][:, :], ctx_all[:, bass.ds((b + len(LANES) + lane) * K, K)])
                    for lane in LANES:
                        inverse_root(lane, L3F, 2, one)

                @block.vector
                def _(dve):
                    chain = [0]

                    def link(ins):
                        chain[0] += 1
                        ins.then_inc(dve_chain, 1)
                        dve.wait_ge(dve_chain, chain[0])

                    def ts(o, i, s1, s2, op0, op1=None):
                        if op1 is None:
                            return nc.vector.tensor_scalar(o, i, s1, None, op0)
                        return nc.vector.tensor_scalar(o, i, s1, s2, op0, op1)

                    def tt(o, a, c, op):
                        return nc.vector.tensor_tensor(o, a, c, op)

                    def norm_stats(lane, rows):
                        link(nc.vector.bn_stats(stats[lane][:, 0, :], rows))
                        link(nc.vector.bn_aggr(mean_var[lane][:, 0, :], stats[lane][:, 0, :]))
                        ts(var_eps[lane][:, 0:1], mean_var[lane][:, 0, 1:2], 1e-5, None, ALU.add)\
                            .then_inc(var_ready[lane], 1)

                    def norm_apply(lane, layer):
                        dve.wait_ge(rstd_ready[lane], rstd_ready.upto(layer, 1))
                        ts(xn[lane][:, :], x[lane][:, :], mean_var[lane][:, 0, 0:1], rstd[lane][:, 0:1],
                           ALU.subtract, ALU.mult).then_inc(xn_ready[lane], 1)

                    def x_done(lane, layer, ins):
                        ins.then_inc(x_ready[lane], 1)
                        dve.wait_ge(x_ready[lane], x_ready.upto(layer, 1))
                        if layer < L3F:
                            norm_stats(lane, x[lane][:, :])

                    def add_output(lane, layer, psum):
                        dve.wait_ge(out_psum[lane], out_psum.upto(layer, 1))
                        x_done(lane, layer, tt(x[lane][:, :], psum, x[lane][:, :], ALU.add))

                    def top2(groups, values, at=0):
                        cols = slice(at, at + groups * E)

                        def g(i):
                            return route[:, i, cols].rearrange("p (g e) -> p g e", e=E)

                        def each(i):
                            return per_group[:, i, 0:groups].unsqueeze(2).broadcast_to([128, groups, E])
                        order = part["const", "first"].unsqueeze(1).broadcast_to([128, groups, E])
                        left = values
                        for nth in range(2):
                            link(nc.vector.tensor_reduce(per_group[:, 0, 0:groups], g(left), AX.X, ALU.max))
                            link(tt(g(3), g(left), each(0), ALU.is_equal))
                            link(tt(g(3), g(3), order, ALU.mult))
                            link(nc.vector.tensor_reduce(per_group[:, 1, 0:groups], g(3), AX.X, ALU.max))
                            link(tt(g(4 + nth), g(3), each(1), ALU.is_equal))
                            if nth == 0:
                                link(nc.vector.scalar_tensor_tensor(route[:, 2, cols], route[:, 4, cols], GONE,
                                                                    route[:, left, cols], ALU.mult, ALU.add))
                                left = 2
                        link(tt(g(5), g(4), g(5), ALU.add))

                    def sum_of(groups, i, at=0):
                        link(nc.vector.tensor_reduce(per_group[:, 1, 0:groups],
                                                     route[:, i, at:at + groups * E].rearrange("p (g e) -> p g e", e=E),
                                                     AX.X, ALU.add))

                    def times_inverse(groups, i, at=0):
                        return tt(gate[:, at:at + groups * E].rearrange("p (g e) -> p g e", e=E),
                                  route[:, i, at:at + groups * E].rearrange("p (g e) -> p g e", e=E),
                                  per_group[:, 2, 0:groups].unsqueeze(2).broadcast_to([128, groups, E]), ALU.mult)

                    def l0_choose(t):
                        at = 128 * t
                        cols = slice(at, at + 128)
                        link(ts(route[:, 1, cols], route[:, 1, cols], 1.0, None, ALU.add))
                        link(nc.vector.reciprocal(route[:, 6, cols], route[:, 1, cols]))
                        top2(16, 0, at)
                        link(tt(route[:, 6, cols], route[:, 6, cols], route[:, 5, cols], ALU.mult))

                    def l0_gates(t):
                        at = 128 * t
                        sum_of(16, 6, at)
                        link(ts(per_group[:, 1, 0:16], per_group[:, 1, 0:16], 1e-9, None, ALU.max))
                        link(nc.vector.reciprocal(per_group[:, 2, 0:16], per_group[:, 1, 0:16]))
                        link(ts(per_group[:, 2, 0:16], per_group[:, 2, 0:16], part["L0f", "route"], None, ALU.mult))
                        return times_inverse(16, 6, at)

                    def in_order(lane, before, ins):
                        chain[0] += 1
                        ins.then_inc(dve_chain, 1)
                        before[lane] = chain[0]

                    for lane in LANES:
                        dve.wait_ge(kv_psum[lane], kv_psum.upto(L0X, 2))
                        tt(v[lane][0:K, 0:D], bank[lane][2][0:K, 0:D], part["L0x", "bv"][0:K, :], ALU.add)\
                            .then_inc(v_ready[lane], 1)
                    dve.wait_ge(masks_loaded, 3 * 16)
                    for lane in LANES:
                        cols = bass.ds((b + lane) * K, K)
                        nc.vector.tensor_reduce(lens[lane][:, 0:1], qm[:, cols], AX.X, ALU.add)
                        nc.vector.tensor_reduce(lens[lane][:, 1:2], km[:, cols], AX.X, ALU.add).then_inc(lens_ready[lane], 1)
                    for lane in LANES:
                        dve.wait_ge(scores_psum[lane], scores_psum.upto(L0X, 1))
                        link(nc.vector.reduce_max(max_neg[lane][:, 0:1], bank[lane][0][:, 0:K], AX.X))
                        ts(max_neg[lane][:, 0:1], max_neg[lane][:, 0:1], -D ** -0.5, None, ALU.mult)\
                            .then_inc(max_ready[lane], 1)
                    for lane in LANES:
                        dve.wait_ge(probs_ready[lane], probs_ready.upto(L0X, 1))
                        link(nc.vector.reciprocal(row_inv[lane][:, 0:1], row_sum[lane][:, 0:1]))
                    for lane in LANES:
                        dve.wait_ge(x_bias_ready[lane], x_bias_ready.upto(L0X, 1))
                        dve.wait_ge(out_psum[lane], out_psum.upto(L0X, 1))
                        x_done(lane, L0X, nc.vector.scalar_tensor_tensor(
                            x[lane][:, :], bank[lane][3][:, 0:D], row_inv[lane][:, 0:1], x_bias[lane][:, :],
                            ALU.mult, ALU.add))

                    for lane in LANES:
                        dve.wait_ge(kv_psum[lane], kv_psum.upto(L0X, 3))
                        ts(small[lane][:, 128:128 + K], bank[lane][0][:, 0:K], part["L1x", "bk"], None, ALU.add)
                        tt(small[lane][0:K, 384:512], bank[lane][0][0:K, 128:256], part["L1x", "bv"][0:K, :], ALU.add)\
                            .then_inc(v_ready[lane], 1)

                    for lane in LANES:
                        norm_apply(lane, L0F)
                    for lane in LANES:
                        dve.wait_ge(logits_ready[lane], logits_ready.upto(L0F, 1))
                    l0_choose(0)
                    for lane in LANES:
                        for half in range(2):
                            dve.wait_ge(scores_psum[lane], scores_psum.upto(L0F, half + 1))
                            link(nc.vector.tensor_reduce(max_neg[lane][:, 4 * half:4 * half + 4],
                                                         bank[lane][2 + half][:, :].rearrange("p (h k) -> p h k", k=S),
                                                         AX.X, ALU.max))
                        ts(max_neg[lane][:, 0:H0F], max_neg[lane][:, 0:H0F], -D ** -0.5, None, ALU.mult)\
                            .then_inc(max_ready[lane], 1)
                    l0_gates(0).then_inc(gate_ready[0], 1)

                    def mix_experts(h, psum, done, column, to, fresh):
                        before = [chain[0], chain[0]]
                        for e in range(6):
                            half = e // 4
                            for lane in LANES:
                                if e % 4 == 0:
                                    dve.wait_ge(psum[lane], psum.upto(L0F, 2 * h + half + 1))
                                if e == 4:
                                    dve.wait_ge(scaled_ready[lane], scaled_ready.upto(L0F, (0 if fresh else H0F) + h + 1))
                                y = bank[lane][2 * (h % 2) + half][:, 128 * (e % 4):128 * (e % 4) + 128]
                                at = column + 64 * lane + E * h + e
                                g = gate[:, at:at + 1]
                                if e == 4:
                                    dve.wait_ge(done[lane], done.upto(L0F, 2 * h + 1))
                                elif e > 0:
                                    dve.wait_ge(dve_chain, before[lane])
                                elif not fresh and h > 0:
                                    dve.wait_ge(done[lane], done.upto(L0F, 2 * h))
                                if fresh and e == 0:
                                    ins = ts(to(lane), y, g, None, ALU.mult)
                                else:
                                    ins = nc.vector.scalar_tensor_tensor(to(lane), y, g, to(lane), ALU.mult, ALU.add)
                                if e in (3, 5):
                                    ins.then_inc(done[lane], 1)
                                else:
                                    in_order(lane, before, ins)

                    dve.wait_ge(gate_ready[0], gate_ready.upto(L0F, 1))
                    for h in range(H0F):
                        mix_experts(h, v_psum, v_mixed, 0, lambda lane: v[lane][:, 128 * h:128 * h + 128], True)
                    l0_choose(1)
                    link(l0_gates(1))
                    for lane in LANES:
                        dve.wait_ge(probs_ready[lane], probs_ready.upto(L0F, 1))
                        link(nc.vector.reciprocal(row_inv[lane][:, 0:H0F], row_sum[lane][:, 0:H0F]))
                        g_out = gate[:, 128 + 64 * lane:192 + 64 * lane].rearrange("p (h e) -> p h e", e=E)
                        last = tt(g_out, g_out, row_inv[lane][:, 0:H0F].unsqueeze(2).broadcast_to([128, H0F, E]), ALU.mult)
                        if lane == 0:
                            link(last)
                    last.then_inc(gate_ready[0], 1)
                    dve.wait_ge(gate_ready[0], gate_ready.upto(L0F, 2))
                    for h in range(H0F):
                        mix_experts(h, out_psum, out_mixed, 128, lambda lane: x[lane][:, :], False)
                    for lane in LANES:
                        dve.wait_ge(out_mixed[lane], out_mixed.upto(L0F, 2 * H0F))
                        dve.wait_ge(out_summed[lane], out_summed.upto(L0F, H0F))
                        x_done(lane, L0F, tt(x[lane][:, :], x[lane][:, :], pooled[lane][:, :], ALU.add))

                    for lane in LANES:
                        norm_apply(lane, L1X)
                    def take_scores(layer, scale, added):
                        def step(i, lane):
                            done = 4 if layer == L3X and i >= 2 else i + 1
                            dve.wait_ge(scores_psum[lane], scores_psum.upto(layer, done))
                            s3 = wide_b[lane][:, 4 * K * i:4 * K * (i + 1)].rearrange("p (h k) -> p h k", k=K)
                            link(nc.vector.scalar_tensor_tensor(
                                s3, bank[lane][i][:, 0:4 * K].rearrange("p (h k) -> p h k", k=K), scale,
                                added(lane).unsqueeze(1).broadcast_to([128, 4, K]), ALU.mult, ALU.add))
                            nc.vector.tensor_reduce(max_neg[lane][:, 4 * i:4 * i + 4], s3, AX.X, ALU.max, negate=True)\
                                .then_inc(max_ready[lane], 1)
                        return step

                    def take_transposed(layer, i, lane):
                        dve.wait_ge(pT_psum[lane], pT_psum.upto(layer, i + 1))
                        nc.vector.tensor_copy(wide_a[lane][0:K, 512 * i:512 * i + 512], bank[lane][i][0:K, :])\
                            .then_inc(pT_ready[lane], 1)

                    def invert_sums(layer, i, lane):
                        dve.wait_ge(probs_ready[lane], probs_ready.upto(layer, i + 1))
                        nc.vector.reciprocal(row_inv[lane][:, 4 * i:4 * i + 4], row_sum[lane][:, 4 * i:4 * i + 4])\
                            .then_inc(inv_ready[lane], 1)

                    def softmax_banks(layer, behind, scale, added):
                        scores_step = take_scores(layer, scale, added)
                        steps = [(i, lane) for i in range(4) for lane in LANES]
                        for n in range(len(steps) + behind):
                            if n < len(steps):
                                scores_step(*steps[n])
                            if 2 <= n < len(steps) + 2:
                                invert_sums(layer, *steps[n - 2])
                            if n >= behind and steps[n - behind][1] == 0:
                                take_transposed(layer, *steps[n - behind])

                    for lane in LANES:
                        dve.wait_ge(masks_ready[lane], 1)
                    softmax_banks(L1X, 5, 8 ** -0.5, lambda lane: mask1[lane][:, :])
                    for lane in LANES:
                        dve.wait_ge(x_bias_ready[lane], x_bias_ready.upto(L1X, 1))
                        dve.wait_ge(out_psum[lane], out_psum.upto(L1X, 1))
                        x_done(lane, L1X, nc.vector.scalar_tensor_tensor(
                            x[lane][:, :], bank[lane][2][:, 0:D], row_ok[lane][:, 1:2], x_bias[lane][:, :],
                            ALU.mult, ALU.add))

                    for lane in LANES:
                        norm_apply(lane, L1F)
                    for lane in LANES:
                        dve.wait_ge(hidden_ready[lane], hidden_ready.upto(L1F, 1))
                        link(nc.vector.bn_stats(stats[lane][:, 1, :], wide_b[lane][:, 0:512]))
                        link(nc.vector.bn_aggr(mean_var[lane][:, 1, :], stats[lane][:, 1, :]))
                        ts(var_eps[lane][:, 0:1], mean_var[lane][:, 1, 1:2], 1e-5, None, ALU.add)\
                            .then_inc(var_ready[lane], 1)
                    for lane in LANES:
                        dve.wait_ge(rstd_ready[lane], rstd_ready.upto(L1F, 2))
                        ts(wide_b[lane][:, 512:1024], wide_b[lane][:, 0:512], mean_var[lane][:, 1, 0:1],
                           rstd[lane][:, 0:1], ALU.subtract, ALU.mult).then_inc(hidden_normed[lane], 1)
                    dve.wait_ge(hiddenT_psum[0], hiddenT_psum.upto(L1F, 1))
                    for c in range(4):
                        last = ts(wide_a[0][:, 128 * c:128 * c + 128], bank[0][2][:, 128 * c:128 * c + 128],
                                  part["L1f", "lnw"][:, c:c + 1], part["L1f", "lnb"][:, c:c + 1], ALU.mult, ALU.add)
                    last.then_inc(hiddenT_ready[0], 1)
                    for lane in LANES:
                        add_output(lane, L1F, bank[lane][3][:, 0:D])

                    for lane in LANES:
                        norm_apply(lane, L2X)
                    for lane in LANES:
                        dve.wait_ge(kv_ready[lane], kv_ready.upto(L2X, 1))
                        dve.wait_ge(q_ready[lane], q_ready.upto(L2X, 1))
                        for h in range(H2X):
                            nc.vector.bn_stats(stats[lane][:, h, :], small[lane][:, 256 + 64 * h:256 + 64 * h + 64])
                            link(nc.vector.bn_stats(stats[lane][0:K, 2 + h, :], wide_a[lane][0:K, 1024 + 64 * h:1088 + 64 * h]))
                        for h in range(H2X):
                            nc.vector.bn_aggr(mean_var[lane][:, h, :], stats[lane][:, h, :])
                            link(nc.vector.bn_aggr(mean_var[lane][0:K, 2 + h, :], stats[lane][0:K, 2 + h, :]))
                        ts(var_eps[lane][:, 0:2], mean_var[lane][:, 0:2, 1], 1e-6, None, ALU.add)
                        ts(var_eps[lane][0:K, 2:4], mean_var[lane][0:K, 2:4, 1], 1e-6, None, ALU.add)\
                            .then_inc(var_ready[lane], 1)
                    for lane in LANES:
                        dve.wait_ge(rstd_ready[lane], rstd_ready.upto(L2X, 3))
                        for h in range(H2X):
                            ts(small[lane][:, 64 * h:64 * h + 64], small[lane][:, 256 + 64 * h:256 + 64 * h + 64],
                               mean_var[lane][:, h, 0:1], rstd[lane][:, h:h + 1], ALU.subtract, ALU.mult)
                            last = ts(small[lane][0:K, 128 + 64 * h:128 + 64 * h + 64], wide_a[lane][0:K, 1024 + 64 * h:1088 + 64 * h],
                                      mean_var[lane][0:K, 2 + h, 0:1], rstd[lane][0:K, 2 + h:3 + h],
                                      ALU.subtract, ALU.mult)
                        last.then_inc(qk_normed[lane], 1)
                    for lane in LANES:
                        dve.wait_ge(scores_psum[lane], scores_psum.upto(L2X, 1))
                        for h in range(H2X):
                            link(tt(wide_b[lane][:, K * h:K * h + K], bank[lane][h][:, 0:K], mask2[lane][:, :], ALU.add))
                        link(nc.vector.tensor_reduce(max_neg[lane][:, 0:2],
                                                     wide_b[lane][:, 0:2 * K].rearrange("p (h k) -> p h k", k=K),
                                                     AX.X, ALU.max))
                        link(ts(row_ok[lane][:, 2:4], max_neg[lane][:, 0:2], 0.1 * MASKED, None, ALU.is_gt))
                        ts(max_neg[lane][:, 0:2], max_neg[lane][:, 0:2], -64 ** -0.5, None, ALU.mult)\
                            .then_inc(max_ready[lane], 1)
                    for lane in LANES:
                        dve.wait_ge(probs_ready[lane], probs_ready.upto(L2X, 1))
                        link(tt(row_sum[lane][:, 0:2], row_sum[lane][:, 0:2], row_ok[lane][:, 2:4], ALU.mult))
                        link(nc.vector.reciprocal(row_inv[lane][:, 0:2], row_sum[lane][:, 0:2]))
                        for h in range(H2X):
                            p = wide_b[lane][:, K * h:K * h + K]
                            last = ts(p, p, row_ok[lane][:, 2 + h:3 + h], row_inv[lane][:, h:h + 1], ALU.mult, ALU.mult)
                        last.then_inc(probs_normed[lane], 1)
                    for lane in LANES:
                        add_output(lane, L2X, bank[lane][0][:, 0:D])

                    for lane in LANES:
                        norm_apply(lane, L2F)
                    for lane in LANES:
                        dve.wait_ge(gate_psum[lane], gate_psum.upto(L2F, 1))
                        link(nc.vector.tensor_copy(route[:, 0, E * lane:E * lane + E], bank[lane][1][:, 0:E]))
                    nc.vector.tensor_reduce(per_group[:, 3, 0:2], route[:, 0, 0:2 * E].rearrange("p (g e) -> p g e", e=E),
                                            AX.X, ALU.max, negate=True).then_inc(logits_taken[0], 1)
                    dve.wait_ge(logits_taken[0], logits_taken.upto(L2F, 1))

                    def add_hidden_bias(lane):
                        for i, b_from in enumerate((2, 3, 0, 1)):
                            dve.wait_ge(hidden_psum[lane], hidden_psum.upto(L2F, i + 1))
                            tt(wide_a[lane][:, 512 * i:512 * i + 512].rearrange("p (c s) -> p c s", c=4),
                               bank[lane][b_from][:, :].rearrange("p (c s) -> p c s", c=4),
                               part["L2f", "b1"][:, 4 * i:4 * i + 4].unsqueeze(2).broadcast_to([128, 4, S]), ALU.add)\
                                .then_inc(hidden_biased[lane], 1)
                    add_hidden_bias(0)
                    top2(2, 0)
                    for lane in LANES:
                        dve.wait_ge(gate_exp[lane], gate_exp.upto(L2F, 1))
                    link(tt(route[:, 6, 0:2 * E], route[:, 1, 0:2 * E], route[:, 5, 0:2 * E], ALU.mult))
                    sum_of(2, 6)
                    link(nc.vector.reciprocal(per_group[:, 2, 0:2], per_group[:, 1, 0:2]))
                    times_inverse(2, 6).then_inc(gate_ready[0], 1)
                    add_hidden_bias(1)
                    dve.wait_ge(gate_ready[0], gate_ready.upto(L2F, 1))
                    before = [chain[0], chain[0]]
                    for e in range(E):
                        for lane in LANES:
                            if e % 4 == 0:
                                dve.wait_ge(out_psum[lane], out_psum.upto(L2F, e // 4 + 1))
                            dve.wait_ge(dve_chain, before[lane])
                            in_order(lane, before, nc.vector.scalar_tensor_tensor(
                                x[lane][:, :], bank[lane][2 + e // 4][:, 128 * (e % 4):128 * (e % 4) + 128],
                                gate[:, E * lane + e:E * lane + e + 1], x[lane][:, :], ALU.mult, ALU.add))
                    dve.wait_ge(dve_chain, before[1])
                    for lane in LANES:
                        dve.wait_ge(out_psum[lane], out_psum.upto(L2F, 3))
                        x_done(lane, L2F, tt(x[lane][:, :], bank[lane][1][:, 0:D], x[lane][:, :], ALU.add))

                    for lane in LANES:
                        norm_apply(lane, L3X)
                    softmax_banks(L3X, 4, D ** -0.5, lambda lane: part["L3x", "bias"])
                    for lane in LANES:
                        add_output(lane, L3X, bank[lane][2][:, 0:D])

                    for lane in LANES:
                        norm_apply(lane, L3F)

                    def next_x(lane):
                        return x_all[:, bass.ds((b + len(LANES) + lane) * D, D)]
                    dve.wait_ge(again_loaded, 2 * 16)
                    for lane in LANES:
                        norm_stats(lane, next_x(lane))
                    for lane in LANES:
                        dve.wait_ge(logits_ready[lane], logits_ready.upto(L3F, 1))
                    both = 2 * E
                    r = [route[:, i, 0:both] for i in range(7)]
                    halves = [r[i].rearrange("p (g e) -> p g e", e=4) for i in range(7)]
                    worth = [per_group[:, i, 0:4] for i in range(4)]

                    def to_halves(t):
                        return t.unsqueeze(2).broadcast_to([128, 4, 4])

                    def of_lanes(t):
                        return t.unsqueeze(1).broadcast_to([128, 2, E])
                    as_lanes = [r[i].rearrange("p (n e) -> p n e", e=E) for i in range(7)]
                    link(ts(r[1], r[1], 1.0, None, ALU.add))
                    link(nc.vector.reciprocal(r[6], r[1]))
                    link(tt(as_lanes[0], as_lanes[6], of_lanes(part["L3f", "cb"]), ALU.add))
                    link(nc.vector.tensor_reduce(worth[0], halves[0], AX.X, ALU.max))
                    link(tt(halves[3], halves[0], to_halves(worth[0]), ALU.is_equal))
                    link(tt(as_lanes[3], as_lanes[3], of_lanes(part["const", "first"]), ALU.mult))
                    link(nc.vector.tensor_reduce(worth[1], halves[3], AX.X, ALU.max))
                    link(tt(halves[4], halves[3], to_halves(worth[1]), ALU.is_equal))
                    link(nc.vector.scalar_tensor_tensor(r[2], r[4], GONE, r[0], ALU.mult, ALU.add))
                    link(nc.vector.tensor_reduce(worth[1], halves[2], AX.X, ALU.max))
                    link(tt(worth[0], worth[0], worth[1], ALU.add))
                    first_group, second_group = slice(0, 4, 2), slice(1, 4, 2)
                    link(tt(worth[3][:, first_group], worth[0][:, first_group], worth[0][:, second_group], ALU.is_ge))
                    link(ts(worth[3][:, second_group], worth[3][:, first_group], -1.0, 1.0, ALU.mult, ALU.add))
                    link(tt(halves[0], halves[0], to_halves(worth[3]), ALU.mult))
                    top2(2, 0)
                    link(tt(r[6], r[6], r[5], ALU.mult))
                    sum_of(2, 6)
                    link(ts(per_group[:, 1, 0:2], per_group[:, 1, 0:2], 1e-20, None, ALU.add))
                    link(nc.vector.reciprocal(per_group[:, 2, 0:2], per_group[:, 1, 0:2]))
                    link(times_inverse(2, 6))
                    for lane in LANES:
                        dve.wait_ge(expert_psum[lane], expert_psum.upto(L3F, 1))
                        g_all = gate[:, E * lane:E * lane + E].rearrange("p (c o) -> p o c", o=2)
                        for odd in range(2):
                            last = tt(wide_b[lane][:, 1024 + 256 * odd:1280 + 256 * odd].rearrange("p (c u) -> p c u", u=64),
                                      bank[lane][2 * odd][:, 0:256].rearrange("p (c u) -> p c u", u=64),
                                      g_all[:, odd, :].unsqueeze(2).broadcast_to([128, 4, 64]), ALU.mult)
                        link(last)
                        nc.vector.tensor_reduce(comb[lane],
                                                wide_b[lane][:, 1024:1536].rearrange("p (e u) -> p u e", u=64),
                                                AX.X, ALU.add).then_inc(expert_mixed[lane], 1)
                    for lane in LANES:
                        dve.wait_ge(rstd_ready[lane], rstd_ready.upto(L3F, 2))
                        dve.wait_ge(xnT_psum[lane], xnT_psum.upto(L3F, 1))
                        ts(xn[lane][:, :], next_x(lane), mean_var[lane][:, 0, 0:1], rstd[lane][:, 0:1],
                           ALU.subtract, ALU.mult)
                    for lane in LANES:
                        dve.wait_ge(out_psum[lane], out_psum.upto(L3F, 1))
                        tt(x_all[:, bass.ds((b + lane) * D, D)], bank[lane][3][:, 0:D], x[lane][:, :], ALU.add)\
                            .then_inc(x_ready[lane], 1)

            nc.gpsimd.sem_clear(range(numbers[0], numbers[-1] + 1))
            nc.all_engine_barrier()
        nc.sync.wait_ge(out_stored, 16 * B)


def kernel(**inputs):
    import numpy as np
    import concourse.bacc as bacc
    from concourse.bass_utils import run_bass_kernel_spmd

    a = {name: np.asarray(value) for name, value in inputs.items()}

    def rows(vector, n=128):
        return np.broadcast_to(vector[None, :], (n, vector.shape[0]))

    def pad(t):
        return np.concatenate([t, np.zeros((128 - t.shape[0], t.shape[1]), t.dtype)])

    def inner(t):
        return t.reshape(-1, 128, t.shape[1]).transpose(1, 0, 2).reshape(128, -1)

    def stacked(t):
        return t.transpose(1, 0, 2).reshape(128, -1)

    q, k = np.arange(128)[:, None], np.arange(K)[None, :]
    f = np.float32
    parts = {
        "const": [np.eye(128, dtype=f), np.where(k > q, f(MASKED), f(0)), rows(np.arange(K, dtype=f)), q.astype(f),
                  rows(np.arange(E, 0, -1).astype(f)), (q // 8 == np.arange(H1X)[None, :]).astype(f),
                  np.ones((128, 128), f), np.full((128, 4), -0.5, f),
                  rows(np.kron(np.eye(4, dtype=f), np.ones((1, 8), f)).reshape(128))],
        "L0x": [a["L0_xattn_Wk"].T, a["L0_xattn_Wv"].T, a["L0_xattn_Wq"].T, a["L0_xattn_Wo"].T,
                a["L0_xattn_bq"][:, None], rows(a["L0_xattn_bv"]), rows(a["L0_xattn_bo"])],
        "L0f": [a["L0_ffn_sel_v_w"].T, a["L0_ffn_sel_o_w"].T,
                stacked(a["L0_ffn_q_w"].reshape(H0F, 128, D)), stacked(a["L0_ffn_k_w"].reshape(H0F, 128, D)),
                rows(a["L0_ffn_route_scale"])],
        "L0v": [stacked(a["L0_ffn_v_w"])],
        "L0o": [stacked(a["L0_ffn_o_w"])],
        "L1x": [a["L1_xattn_W_K"], a["L1_xattn_W_V"], a["L1_xattn_W_Q"], a["L1_xattn_W_O"],
                a["L1_xattn_b_Q"][:, None], a["L1_xattn_b_K"][:, None], rows(a["L1_xattn_b_V"]), rows(a["L1_xattn_b_O"])],
        "L1f": [a["L1_ffn_W_fc"].T, inner(a["L1_ffn_W_proj"].T), a["L1_ffn_ln_w"].reshape(4, 128).T,
                a["L1_ffn_ln_b"].reshape(4, 128).T],
        "L2x": [a["L2_xattn_Wkv"], a["L2_xattn_Wq"], a["L2_xattn_Wo"], a["L2_xattn_qn_w"].reshape(128, 1),
                a["L2_xattn_kn_w"].reshape(128, 1)],
        "L2f": [a["L2_ffn_Wg"], stacked(a["L2_ffn_W1"]), a["L2_ffn_b1"].reshape(16, 128).T,
                inner(a["L2_ffn_W2"].reshape(2048, 128)), pad(a["L2_ffn_b2"])],
        "L3x": [a["L3_xattn_Wk"].T, a["L3_xattn_Wv"].T, a["L3_xattn_Wq"].T, inner(a["L3_xattn_Wp"].T),
                a["fside_1x1xSxS2_0"].reshape(S, K)],
        "L3f": [a["L3_ffn_gate"].T, rows(a["L3_ffn_corr_bias"]), a["L3_ffn_fc1_w"].T,
                pad(a["L3_ffn_w1"].transpose(2, 0, 1).reshape(64, 512)),
                a["L3_ffn_w2"].reshape(4, 2, 64, 64).transpose(1, 3, 0, 2).reshape(128, 256),
                pad(a["L3_ffn_fc2_w"].T), a["L3_ffn_up_w"].T, inner(a["L3_ffn_down_w"].T)],
    }
    arrays = {f"in_{name}": np.ascontiguousarray(np.concatenate(ps, axis=1)) for name, ps in parts.items()}
    for name in parts:
        assert arrays[f"in_{name}"].shape == (128, width(name)), (name, arrays[f"in_{name}"].shape)
    arrays["in_x"] = np.ascontiguousarray(a["x"].transpose(1, 0, 2).reshape(S, B * D))
    arrays["in_ctx"] = np.ascontiguousarray(a["ctx_1024"].transpose(2, 0, 1).reshape(D, B * K))
    arrays["in_q_mask"] = np.ascontiguousarray(rows(a["mask_BxS2_if1"].reshape(B * K)))
    arrays["in_k_mask"] = np.ascontiguousarray(rows(a["mask_BxS2_ik0"].reshape(B * K)))
    arrays["in_pair_mask"] = np.ascontiguousarray(a["mask_BxSxS2_bk0"].transpose(1, 0, 2).reshape(S, B * K))

    nc = bacc.Bacc("TRN2", target_bir_lowering=False, num_devices=1)
    d = {name: nc.dram_tensor(name, t.shape, mybir.dt.from_np(t.dtype), kind="ExternalInput").ap()
         for name, t in arrays.items()}
    out = nc.dram_tensor("out_0", (S, B * D), F32, kind="ExternalOutput").ap()
    build(nc, d["in_x"], d["in_ctx"], d["in_q_mask"], d["in_k_mask"], d["in_pair_mask"],
          {name: d[f"in_{name}"] for name in parts}, out)
    r = run_bass_kernel_spmd(nc, [arrays], core_ids=[0])
    return r.results[0]["out_0"].reshape(S, B, D).transpose(1, 0, 2)
```
